# Optimizing a Trainium2 kernel written in Bass

```python
import numpy as np
import jax
import jax.numpy as jnp

def _softmax(x, axis=-1):
    return jax.nn.softmax(x, axis=axis)

def _gelu(x):
    return jax.nn.gelu(x, approximate=True)

def _silu(x):
    return jax.nn.silu(x)

def _sigmoid(x):
    return jax.nn.sigmoid(x)

def _layernorm(x, axis=-1, eps=1e-05):
    m = jnp.mean(x, axis=axis, keepdims=True)
    v = jnp.var(x, axis=axis, keepdims=True)
    return (x - m) / jnp.sqrt(v + eps)

def _scatter_add(tgt, idx, src, axis=0):
    return tgt.at[idx].add(src)

def _segment_sum(src, seg, n):
    return jax.ops.segment_sum(src, seg, n)
kernel_name = 'mk_gnn_ffn_d2_gnn_r8_ddf2d8'

def setup_inputs(seed: int=0):
    np.random.seed(seed)
    _w = jnp.asarray

    def _rec_inputs():
        import jax
        import jax.numpy as jnp
        _gk = jax.random.key(seed)
        x = -8.776e-05 + 1 * jax.random.normal(jax.random.fold_in(_gk, 1), (1250, 512), jnp.float32)
        _s = jax.random.randint(jax.random.fold_in(_gk, 2), (10000,), 0, 1250, jnp.int32)
        _d = jax.random.randint(jax.random.fold_in(_gk, 3), (10000,), 0, 1250, jnp.int32)
        _loop = jnp.arange(1250, dtype=jnp.int32)
        src = jnp.concatenate([_s, _d, _loop])
        dst = jnp.concatenate([_d, _s, _loop])
        _o = jnp.argsort(dst, stable=True)
        src = src[_o]
        dst = dst[_o]
        return (x, src, dst)
    x, src, dst = _rec_inputs()

    def _L0_gnn_setup():
        import jax, jax.numpy as jnp
        import numpy as np
        N_NODES = 1250

        def sage_conv(x, src, dst, Wl, bl, Wr):
            msg = x[src]
            summed = jax.ops.segment_sum(msg, dst, num_segments=N_NODES)
            cnt = jax.ops.segment_sum(jnp.ones((src.shape[0],), x.dtype), dst, num_segments=N_NODES)
            mean = summed / jnp.maximum(cnt, 1.0)[:, None]
            return mean @ Wl.T + bl + x @ Wr.T
        key = jax.random.key(seed)
        ks = jax.random.split(key, 7)
        d = 512
        E = 20000
        x = jax.random.normal(ks[0], (N_NODES, d), jnp.float32)
        edge_index = jax.random.randint(ks[1], (2, E), 0, N_NODES, jnp.int64)
        s = 1.0 / np.sqrt(d)
        Wl0 = jax.random.normal(ks[2], (d, d), jnp.float32) * s
        bl0 = jnp.zeros((d,), jnp.float32)
        Wr0 = jax.random.normal(ks[3], (d, d), jnp.float32) * s
        Wl1 = jax.random.normal(ks[4], (d, d), jnp.float32) * s
        bl1 = jnp.zeros((d,), jnp.float32)
        Wr1 = jax.random.normal(ks[5], (d, d), jnp.float32) * s
        return {'x': x, 'edge_index': edge_index, 'Wl0': Wl0, 'bl0': bl0, 'Wr0': Wr0, 'Wl1': Wl1, 'bl1': bl1, 'Wr1': Wr1}
    _L0_gnn_all = _L0_gnn_setup()
    _L0_gnn_in = {k: v for k, v in _L0_gnn_all.items() if k in ('Wl0', 'bl0', 'Wr0', 'Wl1', 'bl1', 'Wr1')}
    del _L0_gnn_all

    def _L0_ffn_setup():
        import jax, jax.numpy as jnp
        import numpy as np
        DIM = 512
        HEADS = 8
        DIM_KEY = 32
        NUM_EXPERTS = 8192
        NUM_KEYS = 256
        TOPK = 16
        BN_EPS = 1e-05

        def peer_forward(x, w_q, keys, weight_down_embed, weight_up_embed):
            b, n, _ = x.shape
            q = x @ w_q * (1.0 / np.sqrt(1.0 + BN_EPS))
            queries = q.reshape(b, n, 2, HEADS, DIM_KEY).transpose(2, 0, 1, 3, 4)
            sim = jnp.einsum('pbnhd,hkpd->pbnhk', queries, keys)
            v0, i0 = jax.lax.top_k(sim[0], TOPK)
            v1, i1 = jax.lax.top_k(sim[1], TOPK)
            all_scores = v0[..., :, None] + i0[..., None, :].astype(v0.dtype)
            all_scores = all_scores.reshape(*all_scores.shape[:-2], -1)
            scores, pk_indices = jax.lax.top_k(all_scores, TOPK)
            weights_down = jnp.take(weight_down_embed, pk_indices, axis=0)
            weights_up = jnp.take(weight_up_embed, pk_indices, axis=0)
            h = jnp.einsum('bnd,bnhkd->bnhk', q, weights_down)
            h = jax.nn.gelu(h)
            h = h * jax.nn.softmax(scores, axis=-1)
            out = jnp.einsum('bnhk,bnhkd->bnd', h, weights_up)
            return out
        key = jax.random.key(seed)
        k1, k2, k3, k4, k5 = jax.random.split(key, 5)
        b, n = (2, 512)
        x = jax.random.normal(k1, (b, n, DIM), dtype=jnp.float32)
        w_q = jax.random.normal(k2, (DIM, DIM_KEY * HEADS * 2), dtype=jnp.float32) / np.sqrt(DIM)
        keys = jax.random.normal(k3, (HEADS, NUM_KEYS, 2, DIM_KEY), dtype=jnp.float32) * 0.01
        weight_down_embed = jax.random.normal(k4, (NUM_EXPERTS, DIM), dtype=jnp.float32) * 0.01
        weight_up_embed = jax.random.normal(k5, (NUM_EXPERTS, DIM), dtype=jnp.float32) * 0.01
        return {'x': x, 'w_q': w_q, 'keys': keys, 'weight_down_embed': weight_down_embed, 'weight_up_embed': weight_up_embed}
    _L0_ffn_all = _L0_ffn_setup()
    _L0_ffn_in = {k: v for k, v in _L0_ffn_all.items() if k in ('w_q', 'keys', 'weight_down_embed', 'weight_up_embed')}
    del _L0_ffn_all

    def _L1_gnn_setup():
        import jax, jax.numpy as jnp
        import numpy as np
        N_NODES = 1250
        N_EDGES = 20000
        D = 512
        key = jax.random.key(seed)
        k_h, k_e, k_w1, k_w2 = jax.random.split(key, 4)
        h = jax.random.normal(k_h, (N_NODES, D), dtype=jnp.float32)
        edge_index = jax.random.randint(k_e, (2, N_EDGES), 0, N_NODES, dtype=jnp.int64)
        scale = 1.0 / np.sqrt(D)
        W1 = jax.random.normal(k_w1, (D, D), dtype=jnp.float32) * scale
        b1 = jnp.zeros((D,), dtype=jnp.float32)
        W2 = jax.random.normal(k_w2, (D, D), dtype=jnp.float32) * scale
        b2 = jnp.zeros((D,), dtype=jnp.float32)
        return {'h': h, 'edge_index': edge_index, 'W1': W1, 'b1': b1, 'W2': W2, 'b2': b2}
    _L1_gnn_all = _L1_gnn_setup()
    _L1_gnn_in = {k: v for k, v in _L1_gnn_all.items() if k in ('W1', 'b1', 'W2', 'b2')}
    del _L1_gnn_all

    def _L1_ffn_setup():
        import jax, jax.numpy as jnp
        import numpy as np
        D_MODEL = 512
        N_HEADS = 8
        KV_OPTS = (8, 4, 1)
        D_K = D_MODEL // N_HEADS

        def gqa(x, wq, wk, wv, wo, n_kv):
            B, S, _ = x.shape
            groups = N_HEADS // n_kv
            q = (x @ wq).reshape(B, S, N_HEADS, D_K).transpose(0, 2, 1, 3)
            k = (x @ wk).reshape(B, S, n_kv, D_K).transpose(0, 2, 1, 3)
            v = (x @ wv).reshape(B, S, n_kv, D_K).transpose(0, 2, 1, 3)
            k = jnp.repeat(k, groups, axis=1)
            v = jnp.repeat(v, groups, axis=1)
            scores = jnp.einsum('bhqd,bhkd->bhqk', q, k) / jnp.sqrt(jnp.float32(D_K))
            attn = jax.nn.softmax(scores, axis=-1)
            out = jnp.einsum('bhqk,bhkd->bhqd', attn, v)
            out = out.transpose(0, 2, 1, 3).reshape(B, S, D_MODEL)
            return out @ wo
        key = jax.random.key(seed)
        ks = jax.random.split(key, 32)
        it = iter(ks)
        s = 0.02
        inp = {'x': jax.random.normal(next(it), (64, 1024, D_MODEL), dtype=jnp.float32)}
        inp['r_w1'] = jax.random.normal(next(it), (D_MODEL, D_MODEL // 4), jnp.float32) * s
        inp['r_b1'] = jnp.zeros((D_MODEL // 4,), jnp.float32)
        inp['r_w2'] = jax.random.normal(next(it), (D_MODEL // 4, len(KV_OPTS)), jnp.float32) * s
        inp['r_b2'] = jnp.zeros((len(KV_OPTS),), jnp.float32)
        for i, nkv in enumerate(KV_OPTS):
            inp[f'wq{i}'] = jax.random.normal(next(it), (D_MODEL, D_MODEL), jnp.float32) * s
            inp[f'wk{i}'] = jax.random.normal(next(it), (D_MODEL, nkv * D_K), jnp.float32) * s
            inp[f'wv{i}'] = jax.random.normal(next(it), (D_MODEL, nkv * D_K), jnp.float32) * s
            inp[f'wo{i}'] = jax.random.normal(next(it), (D_MODEL, D_MODEL), jnp.float32) * s
        return inp
    _L1_ffn_all = _L1_ffn_setup()
    _L1_ffn_in = {k: v for k, v in _L1_ffn_all.items() if k in ('r_w1', 'r_b1', 'r_w2', 'r_b2', 'wq0', 'wk0', 'wv0', 'wo0', 'wq1', 'wk1', 'wv1', 'wo1', 'wq2', 'wk2', 'wv2', 'wo2')}
    del _L1_ffn_all
    return {'x': x, 'src': src, 'dst': dst, 'L0_gnn_Wl0': _L0_gnn_in['Wl0'], 'L0_gnn_bl0': _L0_gnn_in['bl0'], 'L0_gnn_Wr0': _L0_gnn_in['Wr0'], 'L0_gnn_Wl1': _L0_gnn_in['Wl1'], 'L0_gnn_bl1': _L0_gnn_in['bl1'], 'L0_gnn_Wr1': _L0_gnn_in['Wr1'], 'L0_ffn_w_q': _L0_ffn_in['w_q'], 'L0_ffn_keys': _L0_ffn_in['keys'], 'L0_ffn_weight_down_embed': _L0_ffn_in['weight_down_embed'], 'L0_ffn_weight_up_embed': _L0_ffn_in['weight_up_embed'], 'L1_gnn_W1': _L1_gnn_in['W1'], 'L1_gnn_b1': _L1_gnn_in['b1'], 'L1_gnn_W2': _L1_gnn_in['W2'], 'L1_gnn_b2': _L1_gnn_in['b2'], 'L1_ffn_r_w1': _L1_ffn_in['r_w1'], 'L1_ffn_r_b1': _L1_ffn_in['r_b1'], 'L1_ffn_r_w2': _L1_ffn_in['r_w2'], 'L1_ffn_r_b2': _L1_ffn_in['r_b2'], 'L1_ffn_wq0': _L1_ffn_in['wq0'], 'L1_ffn_wk0': _L1_ffn_in['wk0'], 'L1_ffn_wv0': _L1_ffn_in['wv0'], 'L1_ffn_wo0': _L1_ffn_in['wo0'], 'L1_ffn_wq1': _L1_ffn_in['wq1'], 'L1_ffn_wk1': _L1_ffn_in['wk1'], 'L1_ffn_wv1': _L1_ffn_in['wv1'], 'L1_ffn_wo1': _L1_ffn_in['wo1'], 'L1_ffn_wq2': _L1_ffn_in['wq2'], 'L1_ffn_wk2': _L1_ffn_in['wk2'], 'L1_ffn_wv2': _L1_ffn_in['wv2'], 'L1_ffn_wo2': _L1_ffn_in['wo2']}

def reference(x, src, dst, L0_gnn_Wl0, L0_gnn_bl0, L0_gnn_Wr0, L0_gnn_Wl1, L0_gnn_bl1, L0_gnn_Wr1, L0_ffn_w_q, L0_ffn_keys, L0_ffn_weight_down_embed, L0_ffn_weight_up_embed, L1_gnn_W1, L1_gnn_b1, L1_gnn_W2, L1_gnn_b2, L1_ffn_r_w1, L1_ffn_r_b1, L1_ffn_r_w2, L1_ffn_r_b2, L1_ffn_wq0, L1_ffn_wk0, L1_ffn_wv0, L1_ffn_wo0, L1_ffn_wq1, L1_ffn_wk1, L1_ffn_wv1, L1_ffn_wo1, L1_ffn_wq2, L1_ffn_wk2, L1_ffn_wv2, L1_ffn_wo2):
    import jax
    import jax.numpy as jnp

    def _L0_gnn_ref(x, edge_index, Wl0, bl0, Wr0, Wl1, bl1, Wr1):
        import jax, jax.numpy as jnp
        import numpy as np
        N_NODES = 1250

        def sage_conv(x, src, dst, Wl, bl, Wr):
            msg = x[src]
            summed = jax.ops.segment_sum(msg, dst, num_segments=N_NODES)
            cnt = jax.ops.segment_sum(jnp.ones((src.shape[0],), x.dtype), dst, num_segments=N_NODES)
            mean = summed / jnp.maximum(cnt, 1.0)[:, None]
            return mean @ Wl.T + bl + x @ Wr.T
        src, dst = (edge_index[0], edge_index[1])
        h = jax.nn.relu(sage_conv(x, src, dst, Wl0, bl0, Wr0))
        h = jax.nn.relu(sage_conv(h, src, dst, Wl1, bl1, Wr1))
        return h

    def _L0_ffn_ref(x, w_q, keys, weight_down_embed, weight_up_embed):
        import jax, jax.numpy as jnp
        import numpy as np
        DIM = 512
        HEADS = 8
        DIM_KEY = 32
        NUM_EXPERTS = 8192
        NUM_KEYS = 256
        TOPK = 16
        BN_EPS = 1e-05

        def peer_forward(x, w_q, keys, weight_down_embed, weight_up_embed):
            b, n, _ = x.shape
            q = x @ w_q * (1.0 / np.sqrt(1.0 + BN_EPS))
            queries = q.reshape(b, n, 2, HEADS, DIM_KEY).transpose(2, 0, 1, 3, 4)
            sim = jnp.einsum('pbnhd,hkpd->pbnhk', queries, keys)
            v0, i0 = jax.lax.top_k(sim[0], TOPK)
            v1, i1 = jax.lax.top_k(sim[1], TOPK)
            all_scores = v0[..., :, None] + i0[..., None, :].astype(v0.dtype)
            all_scores = all_scores.reshape(*all_scores.shape[:-2], -1)
            scores, pk_indices = jax.lax.top_k(all_scores, TOPK)
            weights_down = jnp.take(weight_down_embed, pk_indices, axis=0)
            weights_up = jnp.take(weight_up_embed, pk_indices, axis=0)
            h = jnp.einsum('bnd,bnhkd->bnhk', q, weights_down)
            h = jax.nn.gelu(h)
            h = h * jax.nn.softmax(scores, axis=-1)
            out = jnp.einsum('bnhk,bnhkd->bnd', h, weights_up)
            return out
        return peer_forward(x, w_q, keys, weight_down_embed, weight_up_embed)

    def _L1_gnn_ref(h, edge_index, W1, b1, W2, b2):
        import jax, jax.numpy as jnp
        import numpy as np
        N_NODES = 1250
        N_EDGES = 20000
        D = 512
        send, rec = (edge_index[0], edge_index[1])
        agg = jax.ops.segment_sum(h[send], rec, num_segments=h.shape[0])
        x = h + agg
        x = jax.nn.relu(x @ W1 + b1)
        x = x @ W2 + b2
        return x

    def _L1_ffn_ref(x, r_w1, r_b1, r_w2, r_b2, wq0, wk0, wv0, wo0, wq1, wk1, wv1, wo1, wq2, wk2, wv2, wo2):
        import jax, jax.numpy as jnp
        import numpy as np
        D_MODEL = 512
        N_HEADS = 8
        KV_OPTS = (8, 4, 1)
        D_K = D_MODEL // N_HEADS

        def gqa(x, wq, wk, wv, wo, n_kv):
            B, S, _ = x.shape
            groups = N_HEADS // n_kv
            q = (x @ wq).reshape(B, S, N_HEADS, D_K).transpose(0, 2, 1, 3)
            k = (x @ wk).reshape(B, S, n_kv, D_K).transpose(0, 2, 1, 3)
            v = (x @ wv).reshape(B, S, n_kv, D_K).transpose(0, 2, 1, 3)
            k = jnp.repeat(k, groups, axis=1)
            v = jnp.repeat(v, groups, axis=1)
            scores = jnp.einsum('bhqd,bhkd->bhqk', q, k) / jnp.sqrt(jnp.float32(D_K))
            attn = jax.nn.softmax(scores, axis=-1)
            out = jnp.einsum('bhqk,bhkd->bhqd', attn, v)
            out = out.transpose(0, 2, 1, 3).reshape(B, S, D_MODEL)
            return out @ wo
        routing_input = x.mean(axis=1)
        logits = jax.nn.relu(routing_input @ r_w1 + r_b1) @ r_w2 + r_b2
        sel = jnp.argmax(jax.nn.softmax(logits, axis=-1), axis=-1)
        params = [(wq0, wk0, wv0, wo0), (wq1, wk1, wv1, wo1), (wq2, wk2, wv2, wo2)]
        out = jnp.zeros_like(x)
        for i, nkv in enumerate(KV_OPTS):
            yi = gqa(x, *params[i], nkv)
            mask = (sel == i)[:, None, None]
            out = jnp.where(mask, yi, out)
        return out
    edge_index = jnp.stack([src, dst])
    x = x + _L0_gnn_ref(_layernorm(x, axis=-1), edge_index, L0_gnn_Wl0, L0_gnn_bl0, L0_gnn_Wr0, L0_gnn_Wl1, L0_gnn_bl1, L0_gnn_Wr1)
    x = x + _L0_ffn_ref(_layernorm(x, axis=-1)[None], L0_ffn_w_q, L0_ffn_keys, L0_ffn_weight_down_embed, L0_ffn_weight_up_embed)[0]
    x = x + _L1_gnn_ref(_layernorm(x, axis=-1), edge_index, L1_gnn_W1, L1_gnn_b1, L1_gnn_W2, L1_gnn_b2)
    x = x + _L1_ffn_ref(_layernorm(x, axis=-1)[None], L1_ffn_r_w1, L1_ffn_r_b1, L1_ffn_r_w2, L1_ffn_r_b2, L1_ffn_wq0, L1_ffn_wk0, L1_ffn_wv0, L1_ffn_wo0, L1_ffn_wq1, L1_ffn_wk1, L1_ffn_wv1, L1_ffn_wo1, L1_ffn_wq2, L1_ffn_wk2, L1_ffn_wv2, L1_ffn_wo2)[0]
    return x

_drawn_inputs = setup_inputs


def setup_inputs(seed=0):
    import zlib

    import numpy as np

    out = dict(_drawn_inputs(seed))
    spreads = {'L0_gnn_bl0': (0.0, 0.1),
     'L0_gnn_bl1': (0.0, 0.1),
     'L1_gnn_b1': (0.0, 0.564),
     'L1_gnn_b2': (0.0, 0.381),
     'L1_ffn_r_b1': (0.0, 0.1),
     'L1_ffn_r_b2': (0.0, 0.1)}
    factors = {'L0_ffn_w_q': 8.0,
     'L0_ffn_keys': 8.0,
     'L0_ffn_weight_down_embed': 8.0,
     'L0_ffn_weight_up_embed': 8.0,
     'L1_ffn_wq1': 22.408,
     'L1_ffn_wk1': 23.176}
    for name, (base, spread) in spreads.items():
        noise = np.random.default_rng([zlib.crc32(name.encode()), seed]).standard_normal(out[name].shape)
        drawn = base * np.exp(spread * noise) if base else spread * noise
        out[name] = jnp.asarray(drawn.astype(out[name].dtype))
    for name, factor in factors.items():
        out[name] = (out[name] * factor).astype(out[name].dtype)
    return out
```

```python
from contextlib import ExitStack

import concourse.bass as bass
from concourse import mybir

FP32 = mybir.dt.float32
BF16 = mybir.dt.bfloat16
FP16 = mybir.dt.float16
I32 = mybir.dt.int32
U32 = mybir.dt.uint32
ALU = mybir.AluOpType
ACT = mybir.ActivationFunctionType
X = mybir.AxisListType.X

NODES, D = 1250, 512
ROWS = 125
TILES = NODES // ROWS
FC = D // 128
EDGES = 21250
EROWS = 125
PER = 5
GROUPS = EDGES // (EROWS * PER)
WIN = 46
SLOTS = TILES + 1
WINDOWS = -(-NODES // WIN)
ADJ_W = NODES + WIN
OH_W = NODES + 3
HEADS, DKEY, KEYS, TOPK = 8, 32, 256, 16
GRID = TOPK * TOPK
DHEAD = 64
LN_EPS = 1e-5
BN_SCALE = float(1.0 / (1.0 + 1e-5) ** 0.5)
REPLACED = -3.0e38
TAKEN = -1.0e38
FREE = 1
GELU_A, GELU_C = 0.044715, 0.7978845608028654
KV_OPTS = (8, 4, 1)
SC = [(0, 512), (512, 1024), (1024, NODES)]
TB = [(0, 4), (4, 8), (8, TILES)]


def build(nc, a, out):
    ctx = ExitStack()
    with ctx:
        def sb(name, shape, dt=FP32):
            return ctx.enter_context(nc.sbuf_tensor(name, shape, dt))

        def sem(name):
            return ctx.enter_context(nc.semaphore(name))

        ds = bass.ds

        adj = sb("adj", [128, SLOTS, ADJ_W])
        regA = sb("regA", [128, TILES, D])
        regB = sb("regB", [128, TILES, D])
        xs = sb("xs", [128, TILES, D])
        wA = sb("wA", [128, FC, D])
        wB = sb("wB", [128, FC, D])
        wC = sb("wC", [128, FC, D])
        wD = sb("wD", [128, FC, D])
        wdT = sb("wdT", [128, FC, GRID])
        wu = sb("wu", [128, 2, D])
        sim = sb("sim", [128, HEADS, KEYS])
        grid = sb("grid", [128, HEADS, GRID])
        left = sb("left", [128, HEADS, GRID])
        row = sb("row", [128, D])
        colA = sb("colA", [128, FC, ROWS])
        colB = sb("colB", [128, FC, ROWS])
        xres = sb("xres", [128, D])
        ups = sb("ups", [128, D])
        hidT = sb("hidT", [128, 2 * ROWS])
        gt1 = sb("gt1", [128, 2 * ROWS])
        gelu = sb("gelu", [128, 2 * ROWS])
        coef = sb("coef", [128, 2 * ROWS])
        diag = sb("diag", [128, HEADS, ROWS])
        ident = sb("ident", [128, 128])
        ones_b = sb("ones_b", [128, 128], BF16)
        ones_r = sb("ones_r", [65, ROWS])
        biases = sb("biases", [65, D])
        st = sb("st", [128, 2, 6])
        mv = sb("mv", [128, 2, 2])
        rstd = sb("rstd", [128, 2])
        nhalf = sb("nhalf", [128, 2])
        v16 = sb("v16", [128, HEADS, TOPK])
        i16 = sb("i16", [128, HEADS, TOPK], U32)
        i16f = sb("i16f", [128, HEADS, TOPK])
        z16 = sb("z16", [128, HEADS, TOPK])
        e16 = sb("e16", [128, HEADS, TOPK])
        nz = sb("nz", [128, HEADS])
        zsum = sb("zsum", [128, HEADS])
        rz = sb("rz", [128, HEADS])
        b1c = sb("b1c", [128, FC])
        meanc = sb("meanc", [128, FC])
        rb1 = sb("rb1", [128, 1])
        rw2 = sb("rw2", [128, 3])
        hidr = sb("hidr", [128, 1])
        rt = sb("rt", [1, 32])
        rb2 = sb("rb2", [1, 3])
        seli = sb("seli", [1, 2], I32)
        basei = sb("basei", [1, GROUPS], I32)
        flagi = sb("flagi", [1, 2], I32)
        nmax = sb("nmax", [128, HEADS])
        psum_p = sb("psum_p", [128, HEADS])
        rinv = sb("rinv", [128, HEADS])
        ps = ctx.enter_context(nc.psum_tensor("ps", [128, 8, 512], FP32))

        xsf = xs[:, :, :].rearrange("p t n -> p (t n)")
        EG = EROWS * PER
        src_i = xsf[0:GROUPS, 0:EG].bitcast(I32)
        dst_i = xsf[0:GROUPS, 640:640 + EG].bitcast(I32)
        src_f = xsf[0:GROUPS, 1280:1280 + EG]
        rel_f = xsf[0:GROUPS, 1920:1920 + EG]
        bm = xsf[0:GROUPS, 2560:2562]
        src_c = xsf[0:EROWS, 2600:2600 + GROUPS * PER].rearrange("p (g j) -> p g j", j=PER)
        rel_c = xsf[0:EROWS, 2800:2800 + GROUPS * PER].rearrange("p (g j) -> p g j", j=PER)
        rem_c = xsf[0:EROWS, 3000:3000 + GROUPS * PER].rearrange("p (g j) -> p g j", j=PER)
        dst_f = xsf[0:GROUPS, 3200:3200 + EG]
        bmrow = xsf[0:1, 3900:3900 + 2 * GROUPS]
        cur = xsf[0:EROWS, 4000:4000 + PER]
        iota_w = xsf[0:EROWS, 4100:4100 + WIN]
        rem_t = xsf[0:EROWS, 4200:4200 + GROUPS * PER].rearrange("p (g j) -> p g j", j=PER)
        regBf = regB[:, :, :].rearrange("p t n -> p (t n)")
        half = 3136
        bf = regBf[0:EROWS, 0:half].bitcast(BF16)
        oh_src0 = bf[:, 0:PER * OH_W].rearrange("p (j n) -> p j n", j=PER)
        oh_dst = regBf[0:EROWS, half:half + 256].bitcast(BF16)[:, 0:2 * PER * WIN].rearrange(
            "p (b j w) -> p b j w", b=2, j=PER)
        iota_n = regBf[0:EROWS, 3500:3500 + 640].bitcast(FP16)[:, 0:OH_W]
        def words(t):
            return t[:, :, :].rearrange("p a b -> p (a b)")
        oh_src = [[oh_src0[:, j, :] for j in range(PER)],
                  [words((sim, sim, grid, grid, left)[j])[0:EROWS, 640 * (j % 2):640 * (j % 2) + 640].bitcast(BF16)[:, 0:OH_W]
                   for j in range(PER)]]
        rdeg = adj[:, TILES, 0:NODES]
        keyb = wB[:, :, :].rearrange("p a b -> p (a b)").rearrange("p (c n) -> p c n", c=2)
        adjf = adj[:, :, :].rearrange("p a b -> p (a b)")
        vals = adjf[:, 0:TILES * D].rearrange("p (t n) -> p t n", n=D)
        probs = [adjf[0:ROWS, 5120 + 1250 * i:6370 + 1250 * i] for i in range(2)]
        probT = [adjf[0:ROWS, 7620 + 1250 * i:8870 + 1250 * i].rearrange("p (t n) -> p t n", n=ROWS) for i in range(2)]
        attn = adjf[0:ROWS, 10120:10632]
        outs = adjf[0:ROWS, 10632:11144]
        regAf = regA[:, :, :].rearrange("p t n -> p (t n)")
        keyT = regAf[:, 0:FC * NODES].rearrange("p (c n) -> p c n", n=NODES)
        x4T = regBf[:, 0:FC * NODES].rearrange("p (c n) -> p c n", n=NODES)
        rw1 = wdT[:, :, 0:128]

        def cols(bank):
            return ps[:, bank, 0:FC * ROWS].rearrange("p (c n) -> p c n", n=ROWS)

        psAgg, psTr, psQ = cols(0), cols(1), cols(3)
        psOut = ps[0:ROWS, 2, :]
        psSim = ps[0:ROWS, 4:6, :]
        psHid = ps[:, 6, 0:2 * ROWS]
        psP = ps[:, 6, 256:256 + 2 * ROWS]
        psUp = ps[0:ROWS, 7, :]
        psAdj = [ps[:, i, 0:SLOTS * WIN].rearrange("p (s w) -> p s w", w=WIN) for i in range(2)]
        psE = ps[:, 2, :]
        def psS(i, c):
            return ps[0:ROWS, 3 * i + c, 0:SC[c][1] - SC[c][0]]
        def psSall(i):
            return ps[0:ROWS, 3 * i:3 * i + 3, :].rearrange("p a b -> p (a b)")[:, 0:NODES]
        psPT = ps[0:ROWS, 6, :]
        psPV = ps[0:ROWS, 7, :]

        x_in = sem("x_in")
        edges_in = sem("edges_in")
        sage0_in = sem("sage0_in")
        bias_in = sem("bias_in")
        sage1_in = sem("sage1_in")
        adj_zero = sem("adj_zero")
        consts_set = sem("consts_set")
        iotas_set = sem("iotas_set")
        edge_dve = sem("edge_dve")
        edge_cols = sem("edge_cols")
        adj_onehot = sem("adj_onehot")
        adj_counted = sem("adj_counted")
        adj_added = sem("adj_added")
        degrees_set = sem("degrees_set")
        base_read = sem("base_read")
        rem_dve = sem("rem_dve")
        rem_counted = sem("rem_counted")
        ln1_dve = sem("ln1_dve")
        ln1_rstd = sem("ln1_rstd")
        ln1_done = sem("ln1_done")
        s0_rows = sem("s0_rows")
        s0_agg = sem("s0_agg")
        s0_aggT = sem("s0_aggT")
        s0_tr = sem("s0_tr")
        s0_trT = sem("s0_trT")
        s0_dense = sem("s0_dense")
        s0_out = sem("s0_out")
        peer_in = sem("peer_in")
        expert_in = sem("expert_in")
        keys_zero = sem("keys_zero")
        x_again = sem("x_again")
        s1_rows = sem("s1_rows")
        s1_agg = sem("s1_agg")
        s1_aggT = sem("s1_aggT")
        s1_tr = sem("s1_tr")
        s1_trT = sem("s1_trT")
        s1_dense = sem("s1_dense")
        x1_dve = sem("x1_dve")
        x1_rstd = sem("x1_rstd")
        x1_norm = sem("x1_norm")
        f_tr = sem("f_tr")
        f_trT = sem("f_trT")
        f_q = sem("f_q")
        f_qT = sem("f_qT")
        f_sim = sem("f_sim")
        f_simS = sem("f_simS")
        f_hid = sem("f_hid")
        f_hidT = sem("f_hidT")
        p_top = sem("p_top")
        p_grid = sem("p_grid")
        p_pick = sem("p_pick")
        p_nz = sem("p_nz")
        p_exp = sem("p_exp")
        p_rz = sem("p_rz")
        p_weight = sem("p_weight")
        p_diag = sem("p_diag")
        b_p = sem("b_p")
        b_pS = sem("b_pS")
        b_up = sem("b_up")
        b_upS = sem("b_upS")
        g_pool = sem("g_pool")
        g_tanh = sem("g_tanh")
        g_done = sem("g_done")
        b_coef = sem("b_coef")
        x2_done = sem("x2_done")
        gin_in = sem("gin_in")
        b1_in = sem("b1_in")
        ln3_dve = sem("ln3_dve")
        ln3_rstd = sem("ln3_rstd")
        ln3_done = sem("ln3_done")
        self_added = sem("self_added")
        n_agg = sem("n_agg")
        n_aggT = sem("n_aggT")
        n_u = sem("n_u")
        n_uT = sem("n_uT")
        n_dense = sem("n_dense")
        x3_done = sem("x3_done")
        x4_dve = sem("x4_dve")
        x4_rstd = sem("x4_rstd")
        x4_norm = sem("x4_norm")
        x4_tr = sem("x4_tr")
        x4_trT = sem("x4_trT")
        router_in = sem("router_in")
        r_mean = sem("r_mean")
        r_hid = sem("r_hid")
        r_hidS = sem("r_hidS")
        r_logit = sem("r_logit")
        r_dve = sem("r_dve")
        r_exp = sem("r_exp")
        r_sel = sem("r_sel")
        kv_arrived = sem("kv_arrived")
        kv_ready = sem("kv_ready")
        qo_arrived = sem("qo_arrived")
        qo_ready = sem("qo_ready")
        k_cols = sem("k_cols")
        k_k = sem("k_k")
        k_kS = sem("k_kS")
        k_v = sem("k_v")
        k_vS = sem("k_vS")
        a_cols = sem("a_cols")
        a_q = sem("a_q")
        a_qT = sem("a_qT")
        a_s = sem("a_s")
        a_max = sem("a_max")
        a_exp = sem("a_exp")
        a_pt = sem("a_pt")
        a_ptS = sem("a_ptS")
        a_ptS2 = sem("a_ptS2")
        a_pv = sem("a_pv")
        a_dve = sem("a_dve")
        a_norm = sem("a_norm")
        a_otr = sem("a_otr")
        a_oT = sem("a_oT")
        a_o = sem("a_o")
        a_out = sem("a_out")
        stored = sem("stored")
        out_free = sem("out_free")
        FREED = (
            adj_added, s0_aggT, s0_tr, s0_trT, s0_dense, s0_out, s1_aggT, s1_dense,
            x1_norm, f_tr, f_trT, f_q, f_qT, f_simS, f_hid, f_hidT, p_top, p_grid,
            p_exp, p_weight, p_diag, b_p, b_pS, b_up, b_upS, g_done, x2_done,
            n_aggT, x3_done, x4_tr, x4_trT, k_kS, k_v, k_vS, a_pt, a_ptS, a_ptS2,
            a_exp, a_o, a_out, out_free)
        block = ctx.enter_context(nc.Block())

        def w_view(ap):
            return ap.rearrange("(f p) n -> p f n", p=128)

        @block.sync
        def _(sp):
            sp.dma_start(src_i, a["src"].rearrange("(g e) -> g e", e=EG)).then_inc(edges_in, 16)
            sp.dma_start(dst_i, a["dst"].rearrange("(g e) -> g e", e=EG)).then_inc(edges_in, 16)
            sp.dma_start(regA[0:ROWS, :, :], a["x"].rearrange("(t p) n -> p t n", p=ROWS)).then_inc(x_in, 16)
            for freed in FREED:
                sp.sem_inc(freed, FREE)
            sp.dma_start(wA[:, :, :], w_view(a["Wl0T"])).then_inc(sage0_in, 16)
            sp.dma_start(wB[:, :, :], w_view(a["Wr0T"])).then_inc(sage0_in, 16)
            for i, n in enumerate(("bl0", "bl1", "b2")):
                sp.dma_start(biases[32 * i:32 * i + 1, :], a[n].rearrange("(o n) -> o n", o=1)).then_inc(bias_in, 16)
            sp.dma_start(wC[:, :, :], w_view(a["Wl1T"])).then_inc(sage1_in, 16)
            sp.dma_start(wD[:, :, :], w_view(a["Wr1T"])).then_inc(sage1_in, 16)
            sp.dma_start(wdT[:, :, :], w_view(a["wdT"][:, 0:GRID])).then_inc(expert_in, 16)
            sp.dma_start(wu[:, :, :], a["wu"][0:GRID, :].rearrange("(e p) n -> p e n", p=128)).then_inc(expert_in, 16)
            sp.dma_start(b1c[:, :], a["b1c"]).then_inc(b1_in, 16)
            sp.dma_start(rb1[:, :], a["rb1"].rearrange("(p o) -> p o", o=1)).then_inc(b1_in, 16)
            sp.dma_start(rw2[:, :], a["rw2"]).then_inc(b1_in, 16)
            sp.dma_start(rb2[:, :], a["rb2"].rearrange("(o n) -> o n", o=1)).then_inc(b1_in, 16)
            sp.wait_ge(s0_dense, TILES + FREE)
            sp.dma_start(wA[:, :, :], w_view(a["wq"])).then_inc(peer_in, 16)
            sp.wait_ge(keys_zero, 1)
            for h in range(HEADS):
                b = h % 4
                sp.dma_start(keyb[32 * b:32 * b + 32, h // 4, KEYS * b:KEYS * b + KEYS],
                             a["keysT"][0, h]).then_inc(peer_in, 16)
            with sp.Fori(0, TILES) as t:
                sp.wait_ge(x1_norm, t + FREE)
                sp.dma_start(xres[0:ROWS, :], a["x"].rearrange("(t p) n -> p t n", p=ROWS)[:, ds(t, 1), :]
                             ).then_inc(x_again, 16)
            sp.wait_ge(s1_dense, TILES + FREE)
            sp.dma_start(wC[:, :, :], w_view(a["W1"])).then_inc(gin_in, 16)
            sp.dma_start(wD[:, :, :], w_view(a["W2"])).then_inc(gin_in, 16)
            sp.wait_ge(f_hid, TILES + FREE)
            sp.dma_start(rw1, w_view(a["rw1"])).then_inc(router_in, 16)
            sp.wait_ge(r_sel, 1)
            sel = sp.value_load(seli[0:1, 0:1], min_val=0, max_val=2)
            for i, n_kv in enumerate(KV_OPTS):
                reps = HEADS // n_kv
                with sp.If(sel == i):
                    for w, n in ((wA, "wk"), (wB, "wv")):
                        for f in range(FC):
                            for r in range(reps):
                                dst = w[:, f, :].rearrange("p (k r d) -> p k r d", r=reps, d=DHEAD)[:, :, r, :]
                                sp.dma_start(dst, w_view(a[f"{n}{i}"])[:, f, :].rearrange("p (k d) -> p k d", d=DHEAD)
                                             ).then_inc(kv_arrived, 16)
                    sp.wait_ge(n_dense, TILES)
                    sp.dma_start(wC[:, :, :], w_view(a[f"wq{i}"])).then_inc(qo_arrived, 16)
                    sp.dma_start(wD[:, :, :], w_view(a[f"wo{i}"])).then_inc(qo_arrived, 16)
                    sp.wait_ge(kv_arrived, 16 * 2 * reps * FC)
            sp.sem_inc(kv_ready, 1)
            sp.wait_ge(qo_arrived, 32)
            sp.sem_inc(qo_ready, 1)
            with sp.Fori(0, TILES) as t:
                sp.wait_ge(a_out, t + 1 + FREE)
                sp.dma_start(out.rearrange("(t p) n -> p t n", p=ROWS)[:, ds(t, 1), :], outs).then_inc(stored, 16)
                sp.wait_ge(stored, 16 * t + 16)
                sp.sem_inc(out_free, 1)
            sp.wait_ge(stored, 16 * TILES)

        @block.gpsimd
        def _(g):
            nc.gpsimd.memset(ident[:, :], 0.0).then_inc(consts_set, 1)
            nc.gpsimd.memset(nhalf[:, :], -0.5).then_inc(consts_set, 1)
            nc.gpsimd.memset(ones_b[:, :], 1.0).then_inc(consts_set, 1)
            nc.gpsimd.memset(ones_r[:, :], 1.0).then_inc(consts_set, 1)
            g.wait_ge(consts_set, 4)
            nc.gpsimd.affine_select(out=ident[:, :], in_=ident[:, :], compare_op=ALU.not_equal, fill=1.0, base=0,
                                    pattern=[[-1, 128]], channel_multiplier=1).then_inc(consts_set, 1)
            nc.gpsimd.iota(iota_n, pattern=[[1, OH_W]], base=0, channel_multiplier=0,
                           allow_small_or_imprecise_dtypes=True).then_inc(iotas_set, 1)
            nc.gpsimd.iota(iota_w, pattern=[[1, WIN]], base=0, channel_multiplier=0,
                           allow_small_or_imprecise_dtypes=True).then_inc(iotas_set, 1)
            nc.gpsimd.memset(adjf, 0.0).then_inc(adj_zero, 1)

            def inv_std(n, dve_sem, dve_at, sem_out, b):
                g.wait_ge(dve_sem, dve_at)
                g.nop(nofuse=True)
                nc.gpsimd.tensor_scalar(rstd[0:ROWS, b:b + 1], mv[0:ROWS, b, 1:2], LN_EPS, None, ALU.add
                                        ).then_inc(sem_out, 1)
                g.wait_ge(sem_out, n + 1)
                nc.gpsimd.tensor_tensor(rstd[0:ROWS, b:b + 1], rstd[0:ROWS, b:b + 1], nhalf[0:ROWS, 0:1], ALU.pow
                                        ).then_inc(sem_out, 1)

            with g.Fori(0, TILES // 2) as u:
                for b in range(2):
                    inv_std(4 * u + 2 * b, ln1_dve, 4 * u + 2 * (b + 1), ln1_rstd, b)

            g.wait_ge(ln1_done, TILES)
            with g.Fori(0, TILES) as t:
                g.wait_ge(s0_tr, t + FREE)
                g.nop(nofuse=True)
                nc.gpsimd.tensor_copy(row[0:ROWS, :], regA[0:ROWS, ds(t, 1), :]).then_inc(s0_rows, 1)
            g.wait_ge(s0_dense, TILES + FREE)
            nc.gpsimd.memset(wB[:, :, :], 0.0).then_inc(keys_zero, 1)

            def rows(t):
                g.wait_ge(s0_out, TILES + FREE)
                g.wait_ge(s0_tr, TILES + FREE)
                g.wait_ge(f_tr, t + FREE)
                g.nop(nofuse=True)
                nc.gpsimd.tensor_copy(row[0:ROWS, :], regB[0:ROWS, ds(t, 1), :]).then_inc(s1_rows, 1)

            def pair_scores(t, k):
                hs = slice(4 * k, 4 * k + 4)
                g.wait_ge(p_top, 10 * t + 5 * (k + 1) + FREE)
                if k == 0:
                    g.wait_ge(p_weight, 2 * t + FREE)
                g.nop(nofuse=True)
                nc.gpsimd.tensor_copy(i16f[0:ROWS, hs, :], i16[0:ROWS, hs, :]).then_inc(p_grid, 1)
                g.wait_ge(p_grid, 4 * t + 2 * k + 1 + FREE)
                o = grid[0:ROWS, hs, :].rearrange("p h (a b) -> p h a b", b=TOPK)
                nc.gpsimd.tensor_tensor(o, v16[0:ROWS, hs, :].unsqueeze(3).broadcast_to([ROWS, 4, TOPK, TOPK]),
                                        i16f[0:ROWS, hs, :].unsqueeze(2).broadcast_to([ROWS, 4, TOPK, TOPK]),
                                        ALU.add).then_inc(p_grid, 1)

            def neg_max(t, k):
                hs = slice(4 * k, 4 * k + 4)
                g.wait_ge(p_pick, 8 * t + 4 * k + 1)
                g.nop(nofuse=True)
                nc.gpsimd.tensor_scalar(nz[0:ROWS, hs], z16[0:ROWS, hs, 0], -1.0, None, ALU.mult).then_inc(p_nz, 1)

            def diagonals(t):
                g.wait_ge(p_rz, t + 1)
                g.wait_ge(b_p, t + FREE)
                g.nop(nofuse=True)
                for h in range(HEADS):
                    last = nc.gpsimd.tensor_scalar(diag[0:ROWS, h, :], ident[0:ROWS, 0:ROWS], rz[0:ROWS, h:h + 1],
                                                   None, ALU.mult)
                last.then_inc(p_diag, 1)

            def gelu_tile(t):
                g.wait_ge(f_hidT, t + 1 + FREE)
                nc.gpsimd.tensor_tensor(gt1[:, :], hidT[:, :], hidT[:, :], ALU.mult).then_inc(g_pool, 1)
                g.wait_ge(g_pool, 4 * t + 1)
                g.nop(nofuse=True)
                nc.gpsimd.tensor_scalar(gt1[:, :], gt1[:, :], GELU_A, 1.0, ALU.mult, ALU.add).then_inc(g_pool, 1)
                g.wait_ge(g_pool, 4 * t + 2)
                nc.gpsimd.tensor_tensor(gt1[:, :], gt1[:, :], hidT[:, :], ALU.mult).then_inc(g_pool, 1)
                g.wait_ge(g_tanh, t + 1)
                g.nop(nofuse=True)
                nc.gpsimd.tensor_scalar(gt1[:, :], gt1[:, :], 1.0, 0.5, ALU.add, ALU.mult).then_inc(g_pool, 1)
                g.wait_ge(g_pool, 4 * t + 4)
                nc.gpsimd.tensor_tensor(gelu[:, :], gt1[:, :], hidT[:, :], ALU.mult).then_inc(g_done, 1)

            def coefficients(t):
                g.wait_ge(b_pS, t + 1 + FREE)
                g.wait_ge(g_done, t + 1 + FREE)
                nc.gpsimd.tensor_tensor(coef[:, :], coef[:, :], gelu[:, :], ALU.mult).then_inc(b_coef, 1)

            def residual2(t):
                g.wait_ge(b_upS, t + 1 + FREE)
                nc.gpsimd.tensor_tensor(xs[0:ROWS, ds(t, 1), :], xs[0:ROWS, ds(t, 1), :], ups[0:ROWS, :].unsqueeze(1),
                                        ALU.add).then_inc(x2_done, 1)

            rows(0)
            inv_std(0, x1_dve, 3, x1_rstd, 0)
            gelu_tile(0)
            with g.Fori(1, TILES) as t:
                pair_scores(t - 1, 0)
                pair_scores(t - 1, 1)
                rows(t)
                neg_max(t - 1, 0)
                inv_std(2 * t, x1_dve, 3 * t + 3, x1_rstd, 0)
                neg_max(t - 1, 1)
                diagonals(t - 1)
                coefficients(t - 1)
                gelu_tile(t)
                residual2(t - 1)
            pair_scores(TILES - 1, 0)
            pair_scores(TILES - 1, 1)
            neg_max(TILES - 1, 0)
            neg_max(TILES - 1, 1)
            diagonals(TILES - 1)
            coefficients(TILES - 1)
            residual2(TILES - 1)

            g.wait_ge(s1_agg, TILES)
            for t in range(TILES):
                v = adj[0:ROWS, t, ROWS * t:ROWS * t + ROWS]
                last = nc.gpsimd.tensor_tensor(v, v, ident[0:ROWS, 0:ROWS], ALU.add)
            last.then_inc(self_added, 1)
            with g.Fori(0, TILES // 2) as u:
                for b in range(2):
                    inv_std(4 * u + 2 * b, ln3_dve, 4 * u + 2 * (b + 1), ln3_rstd, b)

            with g.Fori(0, TILES) as t:
                inv_std(2 * t, x4_dve, 2 * t + 2, x4_rstd, 0)

            with g.Fori(0, TILES) as t:
                g.wait_ge(x4_trT, TILES + FREE)
                g.wait_ge(k_v, t + FREE)
                g.nop(nofuse=True)
                nc.gpsimd.tensor_copy(colB[:, :, :], x4T[:, :, ds(t * ROWS, ROWS)]).then_inc(k_cols, 1)
            g.wait_ge(k_v, TILES + FREE)
            with g.Fori(0, TILES) as t:
                g.wait_ge(a_o, t + FREE)
                g.nop(nofuse=True)
                nc.gpsimd.tensor_copy(colB[:, :, :], x4T[:, :, ds(t * ROWS, ROWS)]).then_inc(a_cols, 1)

        @block.scalar
        def _(act):
            with act.Fori(0, TILES) as t:
                act.wait_ge(s0_tr, t + 1 + FREE)
                act.wait_ge(s0_dense, t + FREE)
                nc.scalar.copy(colB[:, :, :], psTr).then_inc(s0_trT, 1)
                act.wait_ge(s0_dense, t + 1 + FREE)
                nc.scalar.activation(regB[0:ROWS, ds(t, 1), :], psOut.unsqueeze(1), ACT.Relu).then_inc(s0_out, 1)

            def rows_T(t):
                act.wait_ge(s1_tr, t + 1)
                act.wait_ge(f_q, t + FREE)
                nc.scalar.copy(colB[:, :, :], psTr).then_inc(s1_trT, 1)

            def front(t):
                act.wait_ge(f_tr, t + 1 + FREE)
                nc.scalar.copy(colB[:, :, :], psTr).then_inc(f_trT, 1)
                act.wait_ge(f_q, t + 1 + FREE)
                nc.scalar.mul(colA[:, :, :], psQ, BN_SCALE).then_inc(f_qT, 1)

            def sims(t):
                for c in range(2):
                    act.wait_ge(f_sim, 2 * t + c + 1)
                    if c == 0:
                        act.wait_ge(p_top, 10 * t + FREE)
                    nc.scalar.copy(sim[0:ROWS, 4 * c:4 * c + 4, :].rearrange("p h k -> p (h k)"),
                                   psSim.rearrange("p a b -> p (a b)")).then_inc(f_simS, 1)

            def hidden(t):
                act.wait_ge(f_hid, t + 1 + FREE)
                act.wait_ge(g_done, t + FREE)
                nc.scalar.copy(hidT[:, :], psHid).then_inc(f_hidT, 1)
                act.wait_ge(g_pool, 4 * t + 3)
                nc.scalar.activation(gt1[:, :], gt1[:, :], ACT.Tanh, scale=GELU_C).then_inc(g_tanh, 1)

            def exps(t, k):
                act.wait_ge(p_nz, 2 * t + k + 1)
                act.wait_ge(p_pick, 8 * t + 4 * k + 2)
                for h in range(4 * k, 4 * k + 4):
                    last = nc.scalar.activation(grid[0:ROWS, h, :], grid[0:ROWS, h, :], ACT.Exp,
                                                bias=nz[0:ROWS, h:h + 1])
                act.wait_ge(p_pick, 8 * t + 4 * k + 3)
                for h in range(4 * k, 4 * k + 4):
                    last = nc.scalar.activation(e16[0:ROWS, h, :], z16[0:ROWS, h, :], ACT.Exp,
                                                bias=nz[0:ROWS, h:h + 1], accum_out=zsum[0:ROWS, h:h + 1])
                last.then_inc(p_exp, 1)

            def weights_S(t):
                act.wait_ge(b_p, t + 1 + FREE)
                act.wait_ge(b_up, t + FREE)
                nc.scalar.copy(coef[:, :], psP).then_inc(b_pS, 1)

            def up_S(t):
                act.wait_ge(b_up, t + 1 + FREE)
                act.wait_ge(x2_done, t + FREE)
                nc.scalar.copy(ups[0:ROWS, :], psUp).then_inc(b_upS, 1)

            rows_T(0)
            front(0)
            sims(0)
            hidden(0)
            with act.Fori(1, TILES) as t:
                rows_T(t)
                exps(t - 1, 0)
                front(t)
                exps(t - 1, 1)
                sims(t)
                weights_S(t - 1)
                hidden(t)
                up_S(t - 1)
            exps(TILES - 1, 0)
            exps(TILES - 1, 1)
            weights_S(TILES - 1)
            up_S(TILES - 1)

            def x4_T(t):
                act.wait_ge(x4_tr, t + 1 + FREE)
                nc.scalar.copy(x4T[:, :, ds(t * ROWS, ROWS)], psTr).then_inc(x4_trT, 1)

            def gin(t):
                act.wait_ge(n_agg, t + 1)
                nc.scalar.copy(colA[:, :, :], psAgg).then_inc(n_aggT, 1)
                act.wait_ge(n_u, t + 1)
                for c in range(FC):
                    last = nc.scalar.activation(colB[:, c, :], psQ[:, c, :], ACT.Relu, bias=b1c[:, c:c + 1])
                last.then_inc(n_uT, 1)

            act.wait_ge(b1_in, 64)
            gin(0)
            with act.Fori(1, TILES) as t:
                gin(t)
                x4_T(t - 1)
            x4_T(TILES - 1)

            act.wait_ge(r_hid, 1)
            nc.scalar.activation(hidr[:, :], psE[:, 0:1], ACT.Relu, bias=rb1[:, 0:1]).then_inc(r_hidS, 1)
            act.wait_ge(r_dve, 2)
            nc.scalar.activation(rt[0:1, 8:11], rt[0:1, 0:3], ACT.Exp, bias=rt[0:1, 4:5],
                                 accum_out=rt[0:1, 12:13]).then_inc(r_exp, 1)

            with act.Fori(0, TILES) as t:
                act.wait_ge(k_k, t + 1)
                nc.scalar.copy(keyT[:, :, ds(t * ROWS, ROWS)], psQ).then_inc(k_kS, 1)

            with act.Fori(0, TILES) as t:
                act.wait_ge(a_q, t + 1)
                nc.scalar.mul(colA[:, :, :], cols(6), DHEAD ** -0.5).then_inc(a_qT, 1)
                for h in range(HEADS):
                    if h >= 1:
                        act.wait_ge(a_pt, 3 * HEADS * t + 3 * h + FREE)
                        nc.scalar.copy(probT[(h - 1) % 2][:, 8:10, :],
                                       psPT[:, 0:2 * ROWS].rearrange("p (t n) -> p t n", n=ROWS)).then_inc(a_ptS2, 1)
                    act.wait_ge(a_max, HEADS * t + h + 1)
                    nc.scalar.activation(probs[h % 2], psSall(h % 2), ACT.Exp, bias=nmax[0:ROWS, h:h + 1],
                                         accum_out=psum_p[0:ROWS, h:h + 1]).then_inc(a_exp, 1)
                act.wait_ge(a_pt, 3 * HEADS * (t + 1) + FREE)
                nc.scalar.copy(probT[(HEADS - 1) % 2][:, 8:10, :],
                               psPT[:, 0:2 * ROWS].rearrange("p (t n) -> p t n", n=ROWS)).then_inc(a_ptS2, 1)
                act.wait_ge(a_otr, t + 1)
                nc.scalar.copy(colB[:, :, :], cols(6)).then_inc(a_oT, 1)

        @block.vector
        def _(v):
            v.wait_ge(edges_in, 32)
            nc.vector.tensor_copy(src_f, src_i).then_inc(edge_dve, 1)
            nc.vector.tensor_copy(dst_f, dst_i).then_inc(edge_dve, 1)
            v.wait_ge(edge_dve, 2)
            nc.vector.tensor_reduce(bm[:, 0:1], dst_f, X, ALU.min).then_inc(edge_dve, 1)
            v.wait_ge(edge_dve, 3)
            nc.vector.tensor_scalar(rel_f, dst_f, bm[:, 0:1], None, ALU.subtract).then_inc(edge_dve, 1)
            v.wait_ge(edge_dve, 4)
            nc.vector.tensor_reduce(bm[:, 1:2], rel_f, X, ALU.max).then_inc(edge_dve, 1)
            v.wait_ge(edge_cols, 1)
            nc.vector.tensor_copy(src_c.rearrange("p g j -> p j g"),
                                  psE[0:EROWS, 0:PER * GROUPS].rearrange("p (j g) -> p j g", j=PER)).then_inc(edge_dve, 1)
            nc.vector.tensor_copy(rel_c.rearrange("p g j -> p j g"),
                                  psE[0:EROWS, PER * GROUPS:2 * PER * GROUPS].rearrange("p (j g) -> p j g", j=PER)
                                  ).then_inc(edge_dve, 1)
            nc.vector.tensor_copy(bmrow, psE[0:1, 2 * PER * GROUPS:2 * (PER + 1) * GROUPS]).then_inc(edge_dve, 1)
            v.wait_ge(edge_dve, 8)
            nc.vector.tensor_copy(basei[:, :], bmrow[:, 0:GROUPS]).then_inc(edge_dve, 1)
            nc.vector.tensor_scalar(bmrow[:, GROUPS:2 * GROUPS], bmrow[:, GROUPS:2 * GROUPS], float(WIN), None,
                                    ALU.is_ge).then_inc(edge_dve, 1)
            v.wait_ge(edge_dve, 10)
            nc.vector.tensor_reduce(flagi[:, 0:1], bmrow[:, GROUPS:2 * GROUPS], X, ALU.max).then_inc(edge_dve, 1)

            v.wait_ge(iotas_set, 2)
            v.wait_ge(adj_zero, 1)
            v.wait_ge(edge_dve, 11)

            def onehots(g_, b):
                for j in range(PER):
                    nc.vector.tensor_scalar(oh_src[b][j].unsqueeze(1), iota_n.unsqueeze(1), src_c[:, ds(g_, 1), j], None,
                                            ALU.is_equal)
                nc.vector.tensor_tensor(oh_dst[:, b, :, :], iota_w.unsqueeze(1).broadcast_to([EROWS, PER, WIN]),
                                        rel_c[:, ds(g_, 1), :].rearrange("p g j -> p (g j)").unsqueeze(2).broadcast_to([EROWS, PER, WIN]),
                                        ALU.is_equal).then_inc(adj_onehot, 1)

            def add_window(n, g_, b):
                v.wait_ge(adj_counted, n + 1)
                v.wait_ge(adj_added, n + FREE)
                first = v.value_load(basei[0:1, ds(g_, 1)], min_val=0, max_val=NODES - 1)
                w = adj[:, :, ds(first, WIN)]
                nc.vector.tensor_tensor(w, w, psAdj[b], ALU.add).then_inc(adj_added, 1)

            onehots(0, 0)
            onehots(1, 1)
            with v.Fori(0, GROUPS // 2 - 1) as u:
                for b in range(2):
                    add_window(2 * u + b, 2 * u + b, b)
                    onehots(2 * u + b + 2, b)
            add_window(GROUPS - 2, GROUPS - 2, 0)
            add_window(GROUPS - 1, GROUPS - 1, 1)

            v.wait_ge(adj_added, GROUPS + FREE)
            spread = v.value_load(flagi[0:1, 0:1], min_val=0, max_val=1)
            with v.If(spread == 1):
                v.wait_ge(rem_counted, 1)
                nc.vector.tensor_tensor(rem_c.rearrange("p g j -> p j g"), rel_c.rearrange("p g j -> p j g"),
                                        psE[0:EROWS, 0:GROUPS].unsqueeze(1).broadcast_to([EROWS, PER, GROUPS]),
                                        ALU.add).then_inc(rem_dve, 1)
                nc.vector.tensor_scalar(rem_t, rel_c, float(WIN), -float(4 * NODES), ALU.is_lt, ALU.mult
                                        ).then_inc(rem_dve, 1)
                v.wait_ge(rem_dve, 2)
                nc.vector.tensor_tensor(rem_c, rem_c, rem_t, ALU.add).then_inc(rem_dve, 1)
                v.wait_ge(rem_dve, 3)
                with v.Fori(0, GROUPS) as gi:
                    v.wait_ge(rem_dve, 3 + gi * (3 * WINDOWS + 1))
                    for j in range(PER):
                        nc.vector.tensor_scalar(oh_src[0][j].unsqueeze(1), iota_n.unsqueeze(1), src_c[:, ds(gi, 1), j],
                                                None, ALU.is_equal)
                    nc.vector.tensor_copy(cur, rem_c[:, ds(gi, 1), :].rearrange("p g j -> p (g j)")
                                          ).then_inc(rem_dve, 1)
                    with v.Fori(0, WINDOWS) as wi:
                        n = 3 + gi * (3 * WINDOWS + 1) + 1 + 3 * wi
                        v.wait_ge(rem_dve, n)
                        nc.vector.tensor_tensor(oh_dst[:, 0, :, :], iota_w.unsqueeze(1).broadcast_to([EROWS, PER, WIN]),
                                                cur.unsqueeze(2).broadcast_to([EROWS, PER, WIN]),
                                                ALU.is_equal).then_inc(rem_dve, 1)
                        v.wait_ge(rem_dve, n + 1)
                        nc.vector.tensor_scalar(cur, cur, float(WIN), None, ALU.subtract).then_inc(rem_dve, 1)
                        v.wait_ge(rem_counted, gi * WINDOWS + wi + 2)
                        w = adj[:, :, ds(wi * WIN, WIN)]
                        nc.vector.tensor_tensor(w, w, psAdj[0], ALU.add).then_inc(rem_dve, 1)
                v.wait_ge(rem_dve, 3 + GROUPS * (3 * WINDOWS + 1))
            nc.vector.tensor_scalar(rdeg, rdeg, 1.0, None, ALU.max).then_inc(degrees_set, 1)
            v.wait_ge(degrees_set, 1)
            nc.vector.reciprocal(rdeg, rdeg).then_inc(degrees_set, 1)

            def norm_two(u, buf_in, buf_out, dve, rs, done):
                for b in range(2):
                    nc.vector.bn_stats(st[0:ROWS, b, :], buf_in[0:ROWS, ds(2 * u + b, 1), :]).then_inc(dve, 1)
                    v.wait_ge(dve, 4 * u + 2 * b + 1)
                    v.nop(nofuse=True)
                    nc.vector.bn_aggr(mv[0:ROWS, b, :], st[0:ROWS, b, :]).then_inc(dve, 1)
                for b in range(2):
                    v.wait_ge(rs, 4 * u + 2 * b + 2)
                    nc.vector.tensor_scalar(buf_out[0:ROWS, ds(2 * u + b, 1), :], buf_in[0:ROWS, ds(2 * u + b, 1), :],
                                            mv[0:ROWS, b, 0:1], rstd[0:ROWS, b:b + 1], ALU.subtract, ALU.mult
                                            ).then_inc(done, 1)

            v.wait_ge(x_in, 16)
            v.wait_ge(consts_set, 5)
            with v.Fori(0, TILES // 2) as u:
                norm_two(u, regA, regA, ln1_dve, ln1_rstd, ln1_done)

            v.wait_ge(degrees_set, 2)

            def mean_T(t, agg, dense, outsem):
                v.wait_ge(agg, t + 1)
                v.wait_ge(dense, t + FREE)
                nc.vector.tensor_tensor(colA[:, :, :], psAgg,
                                        adj[:, TILES:TILES + 1, ds(t * ROWS, ROWS)].broadcast_to([128, FC, ROWS]),
                                        ALU.mult).then_inc(outsem, 1)

            with v.Fori(0, TILES) as t:
                mean_T(t, s0_agg, s0_dense, s0_aggT)

            def mean_T2(t):
                v.wait_ge(f_hid, t + FREE)
                mean_T(t, s1_agg, s1_dense, s1_aggT)

            def x1_tile(t):
                v.wait_ge(s1_dense, t + 1 + FREE)
                v.wait_ge(x_again, 16 * t + 16)
                nc.vector.scalar_tensor_tensor(xs[0:ROWS, ds(t, 1), :], psOut.unsqueeze(1), 0.0, xres[0:ROWS, :].unsqueeze(1),
                                               ALU.max, ALU.add).then_inc(x1_dve, 1)
                v.wait_ge(x1_dve, 3 * t + 1)
                v.nop(nofuse=True)
                nc.vector.bn_stats(st[0:ROWS, 0, :], xs[0:ROWS, ds(t, 1), :]).then_inc(x1_dve, 1)
                v.wait_ge(x1_dve, 3 * t + 2)
                v.nop(nofuse=True)
                nc.vector.bn_aggr(mv[0:ROWS, 0, :], st[0:ROWS, 0, :]).then_inc(x1_dve, 1)
                v.wait_ge(x1_rstd, 2 * t + 2)
                v.wait_ge(s1_tr, t + 1)
                nc.vector.tensor_scalar(row[0:ROWS, :].unsqueeze(1), xs[0:ROWS, ds(t, 1), :], mv[0:ROWS, 0, 0:1], rstd[0:ROWS, 0:1],
                                        ALU.subtract, ALU.mult).then_inc(x1_norm, 1)

            def top16(t, k):
                hs = range(4 * k, 4 * k + 4)
                v.wait_ge(f_simS, 2 * t + k + 1 + FREE)
                v.wait_ge(p_grid, 4 * t + FREE)
                n = 10 * t + 5 * k
                v.nop(nofuse=True)
                for h in hs:
                    last = nc.vector.max(v16[0:ROWS, h, 0:8], sim[0:ROWS, h, :])
                last.then_inc(p_top, 1)
                v.wait_ge(p_top, n + 1 + FREE)
                v.nop(nofuse=True)
                for h in hs:
                    last = nc.vector.max_index(i16[0:ROWS, h, 0:8], v16[0:ROWS, h, 0:8], sim[0:ROWS, h, :])
                last.then_inc(p_top, 1)
                v.wait_ge(p_top, n + 2 + FREE)
                v.nop(nofuse=True)
                for h in hs:
                    last = nc.vector.match_replace(sim[0:ROWS, h, :], v16[0:ROWS, h, 0:8], sim[0:ROWS, h, :], REPLACED)
                last.then_inc(p_top, 1)
                v.wait_ge(p_top, n + 3 + FREE)
                v.nop(nofuse=True)
                for h in hs:
                    last = nc.vector.max(v16[0:ROWS, h, 8:16], sim[0:ROWS, h, :])
                last.then_inc(p_top, 1)
                v.wait_ge(p_top, n + 4 + FREE)
                v.nop(nofuse=True)
                for h in hs:
                    last = nc.vector.max_index(i16[0:ROWS, h, 8:16], v16[0:ROWS, h, 8:16], sim[0:ROWS, h, :])
                last.then_inc(p_top, 1)

            def pick16(t, k):
                hs = range(4 * k, 4 * k + 4)
                n = 8 * t + 4 * k
                v.wait_ge(p_grid, 4 * t + 2 * k + 2 + FREE)
                v.wait_ge(p_exp, 2 * t + FREE)
                v.nop(nofuse=True)
                for h in hs:
                    last = nc.vector.max(z16[0:ROWS, h, 0:8], grid[0:ROWS, h, :])
                last.then_inc(p_pick, 1)
                v.wait_ge(p_pick, n + 1)
                v.wait_ge(b_p, t + FREE)
                v.nop(nofuse=True)
                for h in hs:
                    last = nc.vector.match_replace(left[0:ROWS, h, :], z16[0:ROWS, h, 0:8], grid[0:ROWS, h, :], REPLACED)
                last.then_inc(p_pick, 1)
                v.wait_ge(p_pick, n + 2)
                v.nop(nofuse=True)
                for h in hs:
                    last = nc.vector.max(z16[0:ROWS, h, 8:16], left[0:ROWS, h, :])
                last.then_inc(p_pick, 1)
                v.wait_ge(p_pick, n + 3)
                v.nop(nofuse=True)
                for h in hs:
                    last = nc.vector.match_replace(left[0:ROWS, h, :], z16[0:ROWS, h, 8:16], left[0:ROWS, h, :], REPLACED)
                last.then_inc(p_pick, 1)

            def chosen(t, k):
                hs = slice(4 * k, 4 * k + 4)
                v.wait_ge(p_pick, 8 * t + 4 * k + 4)
                v.wait_ge(p_exp, 2 * t + k + 1 + FREE)
                nc.vector.scalar_tensor_tensor(left[0:ROWS, hs, :], left[0:ROWS, hs, :], TAKEN, grid[0:ROWS, hs, :],
                                               ALU.is_le, ALU.mult).then_inc(p_weight, 1)

            def inv_sums(t):
                v.wait_ge(p_exp, 2 * t + 2 + FREE)
                v.wait_ge(p_diag, t + FREE)
                nc.vector.reciprocal(rz[0:ROWS, :], zsum[0:ROWS, :]).then_inc(p_rz, 1)

            mean_T2(0)
            x1_tile(0)
            top16(0, 0)
            top16(0, 1)
            with v.Fori(1, TILES) as t:
                mean_T2(t)
                pick16(t - 1, 0)
                x1_tile(t)
                pick16(t - 1, 1)
                chosen(t - 1, 0)
                inv_sums(t - 1)
                chosen(t - 1, 1)
                top16(t, 0)
                top16(t, 1)
            pick16(TILES - 1, 0)
            pick16(TILES - 1, 1)
            chosen(TILES - 1, 0)
            inv_sums(TILES - 1)
            chosen(TILES - 1, 1)

            v.wait_ge(x2_done, TILES + FREE)
            with v.Fori(0, TILES // 2) as u:
                norm_two(u, xs, regA, ln3_dve, ln3_rstd, ln3_done)

            with v.Fori(0, TILES) as t:
                v.wait_ge(n_dense, t + 1)
                nc.vector.tensor_tensor(xs[0:ROWS, ds(t, 1), :], xs[0:ROWS, ds(t, 1), :], psOut.unsqueeze(1), ALU.add
                                        ).then_inc(x3_done, 1)
                v.wait_ge(x3_done, t + 1 + FREE)
                v.nop(nofuse=True)
                nc.vector.bn_stats(st[0:ROWS, 0, :], xs[0:ROWS, ds(t, 1), :]).then_inc(x4_dve, 1)
                v.wait_ge(x4_dve, 2 * t + 1)
                v.nop(nofuse=True)
                nc.vector.bn_aggr(mv[0:ROWS, 0, :], st[0:ROWS, 0, :]).then_inc(x4_dve, 1)
                v.wait_ge(x4_rstd, 2 * t + 2)
                v.wait_ge(x4_tr, t + FREE)
                nc.vector.tensor_scalar(row[0:ROWS, :].unsqueeze(1), xs[0:ROWS, ds(t, 1), :], mv[0:ROWS, 0, 0:1], rstd[0:ROWS, 0:1],
                                        ALU.subtract, ALU.mult).then_inc(x4_norm, 1)

            v.wait_ge(x4_trT, TILES + FREE)
            nc.vector.tensor_reduce(meanc[:, :], x4T, X, ALU.add).then_inc(r_mean, 1)
            v.wait_ge(r_mean, 1)
            nc.vector.tensor_scalar(meanc[:, :], meanc[:, :], 1.0 / NODES, None, ALU.mult).then_inc(r_mean, 1)
            v.wait_ge(r_logit, 1)
            v.wait_ge(b1_in, 64)
            nc.vector.tensor_tensor(rt[0:1, 0:3], psE[0:1, 4:7], rb2[0:1, :], ALU.add).then_inc(r_dve, 1)
            v.wait_ge(r_dve, 1)
            nc.vector.tensor_reduce(rt[0:1, 4:5], rt[0:1, 0:3], X, ALU.max, negate=True).then_inc(r_dve, 1)
            v.wait_ge(r_exp, 1)
            nc.vector.reciprocal(rt[0:1, 13:14], rt[0:1, 12:13]).then_inc(r_dve, 1)
            v.wait_ge(r_dve, 3)
            nc.vector.tensor_scalar(rt[0:1, 16:19], rt[0:1, 8:11], rt[0:1, 13:14], None, ALU.mult).then_inc(r_dve, 1)
            v.wait_ge(r_dve, 4)
            nc.vector.tensor_reduce(rt[0:1, 20:21], rt[0:1, 16:19], X, ALU.max).then_inc(r_dve, 1)
            v.wait_ge(r_dve, 5)
            nc.vector.tensor_scalar(rt[0:1, 24:27], rt[0:1, 16:19], rt[0:1, 20:21], None, ALU.is_lt).then_inc(r_dve, 1)
            v.wait_ge(r_dve, 6)
            nc.vector.tensor_scalar(rt[0:1, 28:29], rt[0:1, 25:26], 1.0, None, ALU.add).then_inc(r_dve, 1)
            v.wait_ge(r_dve, 7)
            nc.vector.tensor_tensor(seli[0:1, 0:1], rt[0:1, 28:29], rt[0:1, 24:25], ALU.mult).then_inc(r_sel, 1)

            with v.Fori(0, TILES) as t:
                v.wait_ge(k_v, t + 1 + FREE)
                nc.vector.tensor_copy(vals[0:ROWS, ds(t, 1), :], psOut.unsqueeze(1)).then_inc(k_vS, 1)

            def probs_T(t, h, c):
                lo, hi = TB[c]
                v.wait_ge(a_pt, 3 * HEADS * t + 3 * h + c + 1 + FREE)
                nc.vector.tensor_copy(probT[h % 2][:, lo:hi, :],
                                      psPT[:, 0:(hi - lo) * ROWS].rearrange("p (t n) -> p t n", n=ROWS)
                                      ).then_inc(a_ptS, 1)

            with v.Fori(0, TILES) as t:
                for h in range(HEADS):
                    if h >= 1:
                        probs_T(t, h - 1, 0)
                        probs_T(t, h - 1, 1)
                    v.wait_ge(a_s, HEADS * t + h + 1)
                    v.wait_ge(a_exp, HEADS * t + FREE)
                    nc.vector.tensor_reduce(nmax[0:ROWS, h:h + 1], psSall(h % 2), X, ALU.max, negate=True
                                            ).then_inc(a_max, 1)
                probs_T(t, HEADS - 1, 0)
                probs_T(t, HEADS - 1, 1)
                v.wait_ge(a_exp, HEADS * t + HEADS + FREE)
                nc.vector.reciprocal(rinv[0:ROWS, :], psum_p[0:ROWS, :]).then_inc(a_dve, 1)
                v.wait_ge(a_dve, t + 1)
                v.wait_ge(a_pv, HEADS * (t + 1))
                nc.vector.tensor_tensor(attn.rearrange("p (h d) -> p h d", d=DHEAD), psPV.rearrange("p (h d) -> p h d", d=DHEAD),
                                        rinv[0:ROWS, :].unsqueeze(2).broadcast_to([ROWS, HEADS, DHEAD]),
                                        ALU.mult).then_inc(a_norm, 1)
                v.wait_ge(a_o, t + 1 + FREE)
                v.wait_ge(out_free, t + FREE)
                nc.vector.tensor_tensor(outs.unsqueeze(1), ps[0:ROWS, 7, :].unsqueeze(1), xs[0:ROWS, ds(t, 1), :], ALU.add
                                        ).then_inc(a_out, 1)

        @block.tensor
        def _(pe):
            mm, tr = nc.tensor.matmul, nc.tensor.transpose
            idr = ident[0:ROWS, 0:ROWS]
            pe.wait_ge(consts_set, 5)
            pe.wait_ge(edge_dve, 5)
            idg = ident[0:GROUPS, 0:GROUPS]
            for j in range(PER):
                tr(psE[0:EROWS, GROUPS * j:GROUPS * (j + 1)], src_f[:, EROWS * j:EROWS * (j + 1)], idg)
            for j in range(PER):
                tr(psE[0:EROWS, GROUPS * (PER + j):GROUPS * (PER + j + 1)], rel_f[:, EROWS * j:EROWS * (j + 1)], idg)
            tr(psE[0:1, 2 * PER * GROUPS:(2 * PER + 1) * GROUPS], bm[:, 0:1], idg)
            tr(psE[0:1, (2 * PER + 1) * GROUPS:(2 * PER + 2) * GROUPS], bm[:, 1:2], idg).then_inc(edge_cols, 1)

            def count(b, ohs):
                for t in range(TILES):
                    for j in range(PER):
                        mm(psAdj[b][:, t, :], ohs[j][:, ROWS * t:ROWS * t + 128], oh_dst[:, b, j, :],
                           start=j == 0, stop=j == PER - 1)
                for j in range(PER):
                    last = mm(psAdj[b][:, TILES, :], ones_b[0:EROWS, :], oh_dst[:, b, j, :],
                              start=j == 0, stop=j == PER - 1)
                return last

            with pe.Fori(0, GROUPS // 2) as u:
                for b in range(2):
                    pe.wait_ge(adj_onehot, 2 * u + b + 1)
                    count(b, oh_src[b]).then_inc(adj_counted, 1)
            pe.wait_ge(adj_added, GROUPS + FREE)
            spread = pe.value_load(flagi[0:1, 0:1], min_val=0, max_val=1)
            with pe.If(spread == 1):
                mm(psE[0:EROWS, 0:GROUPS], ones_r[0:1, 0:EROWS], bmrow[:, 0:GROUPS], start=True, stop=True
                   ).then_inc(rem_counted, 1)
                with pe.Fori(0, GROUPS) as gi:
                    with pe.Fori(0, WINDOWS) as wi:
                        pe.wait_ge(rem_dve, 3 + gi * (3 * WINDOWS + 1) + 1 + 3 * wi + 1)
                        count(0, oh_src[0]).then_inc(rem_counted, 1)

            def aggregate(t, x):
                for f in range(FC):
                    for k in range(TILES):
                        last = mm(psAgg[:, f, :], x[0:ROWS, k, 128 * f:128 * f + 128],
                                  adj[0:ROWS, k, ds(t * ROWS, ROWS)], start=k == 0, stop=k == TILES - 1)
                return last

            def transpose4(o, x):
                for f in range(FC):
                    last = tr(o[:, f, :], x[:, 128 * f:128 * f + 128], idr)
                return last

            def to_rows(o, lhs, w, start=True, stop=True):
                for f in range(FC):
                    last = mm(o, lhs[:, f, :], w[:, f, :], start=start and f == 0, stop=stop and f == FC - 1)
                return last

            def to_cols(o, w, rhs):
                for c in range(o.shape[1]):
                    for f in range(FC):
                        last = mm(o[:, c, :], w[:, f, 128 * c:128 * c + 128], rhs[:, f, :],
                                  start=f == 0, stop=f == FC - 1)
                return last

            def bias(o, i, stop):
                return mm(o, ones_r[32 * i:32 * i + 1, :], biases[32 * i:32 * i + 1, :], start=False, stop=stop)

            pe.wait_ge(degrees_set, 2)
            pe.wait_ge(ln1_done, TILES)
            pe.wait_ge(sage0_in, 32)
            pe.wait_ge(bias_in, 48)
            with pe.Fori(0, TILES) as t:
                pe.wait_ge(s0_aggT, t + FREE)
                aggregate(t, regA).then_inc(s0_agg, 1)
                pe.wait_ge(s0_rows, t + 1)
                pe.wait_ge(s0_trT, t + FREE)
                transpose4(psTr, row[0:ROWS, :]).then_inc(s0_tr, 1)
                pe.wait_ge(s0_out, t + FREE)
                pe.wait_ge(s0_aggT, t + 1 + FREE)
                to_rows(psOut, colA, wA, stop=False)
                pe.wait_ge(s0_trT, t + 1 + FREE)
                to_rows(psOut, colB, wB, start=False, stop=False)
                bias(psOut, 0, True).then_inc(s0_dense, 1)

            pe.wait_ge(s0_out, TILES + FREE)
            pe.wait_ge(sage1_in, 32)

            def sage(t):
                pe.wait_ge(s1_aggT, t + FREE)
                aggregate(t, regB).then_inc(s1_agg, 1)
                pe.wait_ge(s1_rows, t + 1)
                pe.wait_ge(f_trT, t + FREE)
                transpose4(psTr, row[0:ROWS, :]).then_inc(s1_tr, 1)
                pe.wait_ge(x1_norm, t + FREE)
                pe.wait_ge(s1_aggT, t + 1 + FREE)
                to_rows(psOut, colA, wC, stop=False)
                pe.wait_ge(s1_trT, t + 1)
                to_rows(psOut, colB, wD, start=False, stop=False)
                bias(psOut, 1, True).then_inc(s1_dense, 1)

            def front(t):
                pe.wait_ge(x1_norm, t + 1 + FREE)
                transpose4(psTr, row[0:ROWS, :]).then_inc(f_tr, 1)
                pe.wait_ge(f_trT, t + 1 + FREE)
                pe.wait_ge(f_qT, t + FREE)
                to_cols(psQ, wA, colB).then_inc(f_q, 1)
                pe.wait_ge(f_qT, t + 1 + FREE)
                for c in range(2):
                    pe.wait_ge(f_simS, 2 * t + c + FREE)
                    for n in range(2):
                        last = mm(psSim[:, n, :], colA[:, c, :], keyb[:, c, 512 * n:512 * n + 512],
                                  start=True, stop=True)
                    last.then_inc(f_sim, 1)
                pe.wait_ge(f_hidT, t + FREE)
                to_cols(psHid.rearrange("p (c n) -> p c n", n=ROWS), wdT, colA).then_inc(f_hid, 1)

            def back(t):
                pe.wait_ge(p_weight, 2 * t + 2 + FREE)
                pe.wait_ge(p_diag, t + 1 + FREE)
                pe.wait_ge(b_pS, t + FREE)
                pe.wait_ge(f_hidT, t + 1 + FREE)
                for e in range(2):
                    for h in range(HEADS):
                        last = mm(psP[:, ROWS * e:ROWS * (e + 1)], left[0:ROWS, h, 128 * e:128 * e + 128],
                                  diag[0:ROWS, h, :], start=h == 0, stop=h == HEADS - 1)
                last.then_inc(b_p, 1)
                pe.wait_ge(b_coef, t + 1)
                pe.wait_ge(b_upS, t + FREE)
                for e in range(2):
                    last = mm(psUp, coef[:, ROWS * e:ROWS * (e + 1)], wu[:, e, :], start=e == 0, stop=e == 1)
                last.then_inc(b_up, 1)

            sage(0)
            pe.wait_ge(peer_in, 16 * (1 + HEADS))
            pe.wait_ge(expert_in, 32)
            front(0)
            with pe.Fori(1, TILES) as t:
                sage(t)
                front(t)
                back(t - 1)
            back(TILES - 1)

            def gin(t):
                pe.wait_ge(n_aggT, t + FREE)
                aggregate(t, regA).then_inc(n_agg, 1)

            def gin_mlp(t):
                pe.wait_ge(n_aggT, t + 1 + FREE)
                to_cols(psQ, wC, colA).then_inc(n_u, 1)
                pe.wait_ge(n_uT, t + 1)
                pe.wait_ge(x3_done, t + FREE)
                to_rows(psOut, colB, wD, stop=False)
                bias(psOut, 2, True).then_inc(n_dense, 1)

            def x4_transposed(t):
                pe.wait_ge(x4_norm, t + 1)
                pe.wait_ge(x4_trT, t + FREE)
                transpose4(psTr, row[0:ROWS, :]).then_inc(x4_tr, 1)

            pe.wait_ge(ln3_done, TILES)
            pe.wait_ge(self_added, 1)
            pe.wait_ge(gin_in, 32)
            gin(0)
            gin_mlp(0)
            with pe.Fori(1, TILES) as t:
                gin(t)
                x4_transposed(t - 1)
                gin_mlp(t)
            x4_transposed(TILES - 1)

            pe.wait_ge(router_in, 16)
            pe.wait_ge(r_mean, 2)
            pe.wait_ge(b1_in, 64)
            for f in range(FC):
                last = mm(psE[:, 0:1], rw1[:, f, :], meanc[:, f:f + 1], start=f == 0, stop=f == FC - 1)
            last.then_inc(r_hid, 1)
            pe.wait_ge(r_hidS, 1)
            mm(psE[0:1, 4:7], hidr[:, :], rw2[:, :], start=True, stop=True).then_inc(r_logit, 1)

            pe.wait_ge(kv_ready, 1)
            with pe.Fori(0, TILES) as t:
                pe.wait_ge(k_cols, t + 1)
                pe.wait_ge(k_kS, t + FREE)
                to_cols(psQ, wA, colB).then_inc(k_k, 1)
                pe.wait_ge(k_vS, t + FREE)
                to_rows(psOut, colB, wB).then_inc(k_v, 1)

            pe.wait_ge(qo_ready, 1)
            pe.wait_ge(k_kS, TILES + FREE)
            pe.wait_ge(k_vS, TILES + FREE)

            def score(t, h, c):
                r = slice(64 * (h % 2), 64 * (h % 2) + 64)
                if c == 0 and h >= 2:
                    pe.wait_ge(a_exp, HEADS * t + h - 1 + FREE)
                last = mm(psS(h % 2, c), colA[r, h // 2, :], keyT[r, h // 2, SC[c][0]:SC[c][1]], start=True, stop=True)
                if c == 2:
                    last.then_inc(a_s, 1)

            def prob_tr(t, h, c):
                lo, hi = TB[c]
                pe.wait_ge(a_exp, HEADS * t + h + 1 + FREE)
                if c == 0:
                    pe.wait_ge(a_ptS2, HEADS * t + h + FREE)
                else:
                    pe.wait_ge(a_ptS, 2 * HEADS * t + 2 * h + c + FREE)
                for k in range(lo, hi):
                    last = tr(psPT[:, ROWS * (k - lo):ROWS * (k - lo + 1)], probs[h % 2][:, ROWS * k:ROWS * (k + 1)], idr)
                last.then_inc(a_pt, 1)

            def prob_v(t, h):
                pe.wait_ge(a_ptS, 2 * HEADS * t + 2 * h + 2 + FREE)
                pe.wait_ge(a_ptS2, HEADS * t + h + 1 + FREE)
                for k in range(TILES):
                    last = mm(psPV[:, DHEAD * h:DHEAD * (h + 1)], probT[h % 2][:, k, :],
                              vals[0:ROWS, k, DHEAD * h:DHEAD * (h + 1)], start=k == 0, stop=k == TILES - 1)
                last.then_inc(a_pv, 1)

            with pe.Fori(0, TILES) as t:
                pe.wait_ge(a_cols, t + 1)
                pe.wait_ge(a_out, t + FREE)
                to_cols(cols(6), wC, colB).then_inc(a_q, 1)
                pe.wait_ge(a_qT, t + 1)
                for c in range(3):
                    score(t, 0, c)
                for h in range(HEADS):
                    for c in range(3):
                        if h + 1 < HEADS:
                            score(t, h + 1, c)
                        prob_tr(t, h, c)
                    if h >= 1:
                        prob_v(t, h - 1)
                prob_v(t, HEADS - 1)
                pe.wait_ge(a_norm, t + 1)
                transpose4(cols(6), attn).then_inc(a_otr, 1)
                pe.wait_ge(a_oT, t + 1)
                to_rows(ps[0:ROWS, 7, :], colB, wD).then_inc(a_o, 1)


def kernel(x, src, dst, L0_gnn_Wl0, L0_gnn_bl0, L0_gnn_Wr0, L0_gnn_Wl1, L0_gnn_bl1, L0_gnn_Wr1, L0_ffn_w_q,
           L0_ffn_keys, L0_ffn_weight_down_embed, L0_ffn_weight_up_embed, L1_gnn_W1, L1_gnn_b1, L1_gnn_W2,
           L1_gnn_b2, L1_ffn_r_w1, L1_ffn_r_b1, L1_ffn_r_w2, L1_ffn_r_b2, L1_ffn_wq0, L1_ffn_wk0, L1_ffn_wv0,
           L1_ffn_wo0, L1_ffn_wq1, L1_ffn_wk1, L1_ffn_wv1, L1_ffn_wo1, L1_ffn_wq2, L1_ffn_wk2, L1_ffn_wv2,
           L1_ffn_wo2):
    import numpy as np
    import concourse.bacc as bacc
    from concourse.bass_utils import run_bass_kernel_spmd

    given = dict(x=x, src=src, dst=dst, Wl0T=np.asarray(L0_gnn_Wl0).T, bl0=L0_gnn_bl0, Wr0T=np.asarray(L0_gnn_Wr0).T,
                 Wl1T=np.asarray(L0_gnn_Wl1).T, bl1=L0_gnn_bl1, Wr1T=np.asarray(L0_gnn_Wr1).T, wq=L0_ffn_w_q,
                 keysT=np.asarray(L0_ffn_keys).transpose(2, 0, 3, 1), wdT=np.asarray(L0_ffn_weight_down_embed).T,
                 wu=L0_ffn_weight_up_embed, W1=L1_gnn_W1, b1c=np.asarray(L1_gnn_b1).reshape(FC, 128).T, W2=L1_gnn_W2, b2=L1_gnn_b2,
                 rw1=L1_ffn_r_w1, rb1=L1_ffn_r_b1, rw2=L1_ffn_r_w2, rb2=L1_ffn_r_b2,
                 wq0=L1_ffn_wq0, wk0=L1_ffn_wk0, wv0=L1_ffn_wv0, wo0=L1_ffn_wo0,
                 wq1=L1_ffn_wq1, wk1=L1_ffn_wk1, wv1=L1_ffn_wv1, wo1=L1_ffn_wo1,
                 wq2=L1_ffn_wq2, wk2=L1_ffn_wk2, wv2=L1_ffn_wv2, wo2=L1_ffn_wo2)
    nc = bacc.Bacc("TRN2", target_bir_lowering=False, num_devices=1)
    arrays, aps = {}, {}
    for name, value in given.items():
        v = np.ascontiguousarray(value)
        arrays[f"in_{name}"] = v
        aps[name] = nc.dram_tensor(f"in_{name}", v.shape, mybir.dt.from_np(v.dtype), kind="ExternalInput").ap()
    out = nc.dram_tensor("out_x", (NODES, D), FP32, kind="ExternalOutput").ap()
    build(nc, aps, out)
    r = run_bass_kernel_spmd(nc, [arrays], core_ids=[0])
    return r.results[0]["out_x"]
```

```python
from contextlib import ExitStack

import concourse.bass as bass
from concourse import mybir

FP32 = mybir.dt.float32
BF16 = mybir.dt.bfloat16
FP16 = mybir.dt.float16
I32 = mybir.dt.int32
U32 = mybir.dt.uint32
ALU = mybir.AluOpType
ACT = mybir.ActivationFunctionType
X = mybir.AxisListType.X

NODES, D = 1250, 512
ROWS = 125
TILES = NODES // ROWS
FC = D // 128
EDGES = 21250
EROWS = 125
PER = 5
GROUPS = EDGES // (EROWS * PER)
WIN = 46
SLOTS = TILES + 1
WINDOWS = -(-NODES // WIN)
ADJ_W = NODES + WIN
OH_W = NODES + 3
HEADS, DKEY, KEYS, TOPK = 8, 32, 256, 16
GRID = TOPK * TOPK
DHEAD = 64
LN_EPS = 1e-5
BN_SCALE = float(1.0 / (1.0 + 1e-5) ** 0.5)
REPLACED = -3.0e38
TAKEN = -1.0e38
FREE = 1
GELU_A, GELU_C = 0.044715, 0.7978845608028654
KV_OPTS = (8, 4, 1)
SC = [[(0, 512), (512, 1024), (1024, NODES)], [(286, 798), (798, NODES), (0, 286)]]
OWN = [(0, 1024), (286, NODES)]
TB = [(0, 4), (4, 8), (8, TILES)]


def build(nc, a, out):
    ctx = ExitStack()
    with ctx:
        def sb(name, shape, dt=FP32):
            return ctx.enter_context(nc.sbuf_tensor(name, shape, dt))

        def sem(name):
            return ctx.enter_context(nc.semaphore(name))

        ds = bass.ds

        adj = sb("adj", [128, SLOTS, ADJ_W])
        regA = sb("regA", [128, TILES, D])
        regB = sb("regB", [128, TILES, D])
        xs = sb("xs", [128, TILES, D])
        wA = sb("wA", [128, FC, D])
        wB = sb("wB", [128, FC, D])
        wC = sb("wC", [128, FC, D])
        wD = sb("wD", [128, FC, D])
        wdT = sb("wdT", [128, FC, GRID])
        wu = sb("wu", [128, 2, D])
        work = sb("work", [128, 3, HEADS, KEYS])
        sim = work[:, 0, :, :]
        grid = work[:, 1, :, :]
        left = work[:, 2, :, :]
        row = sb("row", [128, D])
        colA = sb("colA", [128, FC, ROWS])
        colB = sb("colB", [128, FC, ROWS])
        xres = sb("xres", [128, D])
        ups = sb("ups", [128, D])
        hidT = sb("hidT", [128, 2 * ROWS])
        gt1 = sb("gt1", [128, 2 * ROWS])
        gelu = sb("gelu", [128, 2 * ROWS])
        coef = sb("coef", [128, 2 * ROWS])
        diag = sb("diag", [128, HEADS, ROWS])
        ident = sb("ident", [128, 128])
        ones_b = sb("ones_b", [128, 128], BF16)
        ones_r = sb("ones_r", [65, ROWS])
        biases = sb("biases", [65, D])
        st = sb("st", [128, 2, 6])
        mv = sb("mv", [128, 2, 2])
        rstd = sb("rstd", [128, 2])
        nhalf = sb("nhalf", [128, 2])
        v16 = sb("v16", [128, HEADS, TOPK])
        i16 = sb("i16", [128, HEADS, TOPK], U32)
        i16f = sb("i16f", [128, HEADS, TOPK])
        z16 = sb("z16", [128, HEADS, TOPK])
        e16 = sb("e16", [128, HEADS, TOPK])
        nz = sb("nz", [128, HEADS])
        zsum = sb("zsum", [128, HEADS])
        rz = sb("rz", [128, HEADS])
        b1c = sb("b1c", [128, FC])
        meanc = sb("meanc", [128, FC])
        rb1 = sb("rb1", [128, 1])
        rw2 = sb("rw2", [128, 3])
        hidr = sb("hidr", [128, 1])
        rt = sb("rt", [1, 32])
        rb2 = sb("rb2", [1, 3])
        seli = sb("seli", [1, 2], I32)
        basei = sb("basei", [1, GROUPS], I32)
        flagi = sb("flagi", [1, 2], I32)
        nmax = sb("nmax", [128, HEADS])
        psum_p = sb("psum_p", [128, 2, HEADS])
        psums = sb("psums", [128, HEADS])
        rinv = sb("rinv", [128, HEADS])
        ps = ctx.enter_context(nc.psum_tensor("ps", [128, 8, 512], FP32))

        xsf = xs[:, :, :].rearrange("p t n -> p (t n)")
        EG = EROWS * PER
        src_i = xsf[0:GROUPS, 0:EG].bitcast(I32)
        dst_i = xsf[0:GROUPS, 640:640 + EG].bitcast(I32)
        src_f = xsf[0:GROUPS, 1280:1280 + EG]
        rel_f = xsf[0:GROUPS, 1920:1920 + EG]
        bm = xsf[0:GROUPS, 2560:2562]
        src_c = xsf[0:EROWS, 2600:2600 + GROUPS * PER].rearrange("p (g j) -> p g j", j=PER)
        rel_c = xsf[0:EROWS, 2800:2800 + GROUPS * PER].rearrange("p (g j) -> p g j", j=PER)
        rem_c = xsf[0:EROWS, 3000:3000 + GROUPS * PER].rearrange("p (g j) -> p g j", j=PER)
        dst_f = xsf[0:GROUPS, 3200:3200 + EG]
        bmrow = xsf[0:1, 3900:3900 + 2 * GROUPS]
        cur = xsf[0:EROWS, 4000:4000 + PER]
        iota_w = xsf[0:EROWS, 4100:4100 + WIN]
        rem_t = xsf[0:EROWS, 4200:4200 + GROUPS * PER].rearrange("p (g j) -> p g j", j=PER)
        regBf = regB[:, :, :].rearrange("p t n -> p (t n)")
        half = 3136
        bf = regBf[0:EROWS, 0:half].bitcast(BF16)
        oh_src0 = bf[:, 0:PER * OH_W].rearrange("p (j n) -> p j n", j=PER)
        oh_dst = regBf[0:EROWS, half:half + 256].bitcast(BF16)[:, 0:2 * PER * WIN].rearrange(
            "p (b j w) -> p b j w", b=2, j=PER)
        iota_n = regBf[0:EROWS, 3500:3500 + 640].bitcast(FP16)[:, 0:OH_W]
        def words(t):
            return t.rearrange("p a b -> p (a b)")
        oh_src = [[oh_src0[:, j, :] for j in range(PER)],
                  [words((sim, sim, grid, grid, left)[j])[0:EROWS, 640 * (j % 2):640 * (j % 2) + 640].bitcast(BF16)[:, 0:OH_W]
                   for j in range(PER)]]
        rdeg = adj[:, TILES, 0:NODES]
        keyb = wB[:, :, :].rearrange("p a b -> p (a b)").rearrange("p (c n) -> p c n", c=2)
        adjf = adj[:, :, :].rearrange("p a b -> p (a b)")
        key_h = adjf[:, 0:5000].bitcast(FP16).rearrange("p (h n) -> p h n", n=NODES)
        key_l = adjf[:, 5000:10000].bitcast(FP16).rearrange("p (h n) -> p h n", n=NODES)
        probs = [adjf[0:ROWS, 10000 + 1250 * i:11250 + 1250 * i] for i in range(2)]
        cross = adjf[:, 10000:12500].bitcast(FP16).rearrange("p (c n) -> p c n", n=NODES)
        attn = adjf[0:ROWS, 12500:13012]
        outs = adjf[0:ROWS, 13012:13524]
        vals = work[:, :, :, :].rearrange("p a b c -> p (a b c)")[0:ROWS, 0:TILES * D].bitcast(FP16).rearrange(
            "p (t s n) -> p t s n", s=2, n=D)
        probT = [w[0:ROWS, :, :].rearrange("p a b -> p (a b)")[:, 0:1250].bitcast(FP16).rearrange(
            "p (s t n) -> p s t n", s=2, n=ROWS) for w in (wA, wB)]
        regAf = regA[:, :, :].rearrange("p t n -> p (t n)")
        query = regAf[:, 0:5000].bitcast(FP16).rearrange("p (h n) -> p h n", n=NODES)
        x4T = regBf[:, 0:FC * NODES].rearrange("p (c n) -> p c n", n=NODES)
        rw1 = wdT[:, :, 0:128]

        def cols(bank):
            return ps[:, bank, 0:FC * ROWS].rearrange("p (c n) -> p c n", n=ROWS)

        psAgg, psTr, psQ = cols(0), cols(1), cols(3)
        psOut = ps[0:ROWS, 2, :]
        psSim = ps[0:ROWS, 4:6, :]
        psHid = ps[:, 6, 0:2 * ROWS]
        psP = ps[:, 6, 256:256 + 2 * ROWS]
        psUp = ps[0:ROWS, 7, :]
        psAdj = [ps[:, i, 0:SLOTS * WIN].rearrange("p (s w) -> p s w", w=WIN) for i in range(2)]
        psE = ps[:, 2, :]
        psf = ps[0:ROWS, :, :].rearrange("p a b -> p (a b)")

        def psScore(i):
            return psf[:, NODES * i:NODES * (i + 1)]
        psTP = [ps[0:ROWS, 5 + i, :] for i in range(2)]
        psPV = ps[0:ROWS, 7, :]

        x_in = sem("x_in")
        edges_in = sem("edges_in")
        sage0_in = sem("sage0_in")
        bias_in = sem("bias_in")
        sage1_in = sem("sage1_in")
        adj_zero = sem("adj_zero")
        consts_set = sem("consts_set")
        iotas_set = sem("iotas_set")
        edge_dve = sem("edge_dve")
        edge_cols = sem("edge_cols")
        adj_onehot = sem("adj_onehot")
        adj_counted = sem("adj_counted")
        adj_added = sem("adj_added")
        degrees_set = sem("degrees_set")
        base_read = sem("base_read")
        rem_dve = sem("rem_dve")
        rem_counted = sem("rem_counted")
        ln1_dve = sem("ln1_dve")
        ln1_rstd = sem("ln1_rstd")
        ln1_done = sem("ln1_done")
        s0_rows = sem("s0_rows")
        s0_agg = sem("s0_agg")
        s0_aggT = sem("s0_aggT")
        s0_tr = sem("s0_tr")
        s0_trT = sem("s0_trT")
        s0_dense = sem("s0_dense")
        s0_out = sem("s0_out")
        peer_in = sem("peer_in")
        expert_in = sem("expert_in")
        keys_zero = sem("keys_zero")
        x_again = sem("x_again")
        s1_rows = sem("s1_rows")
        s1_agg = sem("s1_agg")
        s1_aggT = sem("s1_aggT")
        s1_tr = sem("s1_tr")
        s1_trT = sem("s1_trT")
        s1_dense = sem("s1_dense")
        x1_dve = sem("x1_dve")
        x1_rstd = sem("x1_rstd")
        x1_norm = sem("x1_norm")
        f_tr = sem("f_tr")
        f_trT = sem("f_trT")
        f_q = sem("f_q")
        f_qT = sem("f_qT")
        f_sim = sem("f_sim")
        f_simS = sem("f_simS")
        f_hid = sem("f_hid")
        f_hidT = sem("f_hidT")
        p_top = sem("p_top")
        p_grid = sem("p_grid")
        p_pick = sem("p_pick")
        p_nz = sem("p_nz")
        p_exp = sem("p_exp")
        p_rz = sem("p_rz")
        p_weight = sem("p_weight")
        p_diag = sem("p_diag")
        b_p = sem("b_p")
        b_pS = sem("b_pS")
        b_up = sem("b_up")
        b_upS = sem("b_upS")
        g_pool = sem("g_pool")
        g_tanh = sem("g_tanh")
        g_done = sem("g_done")
        b_coef = sem("b_coef")
        x2_done = sem("x2_done")
        gin_in = sem("gin_in")
        b1_in = sem("b1_in")
        ln3_dve = sem("ln3_dve")
        ln3_rstd = sem("ln3_rstd")
        ln3_done = sem("ln3_done")
        self_added = sem("self_added")
        n_agg = sem("n_agg")
        n_aggT = sem("n_aggT")
        n_u = sem("n_u")
        n_uT = sem("n_uT")
        n_dense = sem("n_dense")
        x3_done = sem("x3_done")
        x4_dve = sem("x4_dve")
        x4_rstd = sem("x4_rstd")
        x4_norm = sem("x4_norm")
        x4_tr = sem("x4_tr")
        x4_trT = sem("x4_trT")
        router_in = sem("router_in")
        r_mean = sem("r_mean")
        r_hid = sem("r_hid")
        r_hidS = sem("r_hidS")
        r_logit = sem("r_logit")
        r_dve = sem("r_dve")
        r_exp = sem("r_exp")
        r_sel = sem("r_sel")
        kv_arrived = sem("kv_arrived")
        kv_ready = sem("kv_ready")
        qo_arrived = sem("qo_arrived")
        qo_ready = sem("qo_ready")
        k_cols = sem("k_cols")
        k_k = sem("k_k")
        k_high = sem("k_high")
        k_low = sem("k_low")
        k_q = sem("k_q")
        q_high = sem("q_high")
        q_low = sem("q_low")
        k_v = sem("k_v")
        v_high = sem("v_high")
        v_low = sem("v_low")
        crossed = sem("crossed")
        a_score = sem("a_score")
        a_max = sem("a_max")
        a_exp = sem("a_exp")
        a_tr = sem("a_tr")
        tr_act = sem("tr_act")
        tr_dve = sem("tr_dve")
        a_pv = sem("a_pv")
        a_inv = sem("a_inv")
        a_norm = sem("a_norm")
        stored = sem("stored")
        out_free = sem("out_free")
        FREED = (
            adj_added, s0_aggT, s0_tr, s0_trT, s0_dense, s0_out, s1_aggT, s1_dense,
            x1_norm, f_tr, f_trT, f_q, f_qT, f_simS, f_hid, f_hidT, p_top, p_grid,
            p_exp, p_weight, p_diag, b_p, b_pS, b_up, b_upS, g_done, x2_done,
            n_aggT, x3_done, x4_tr, x4_trT, k_high, k_low, q_high, q_low, k_v, v_high, v_low,
            tr_dve, out_free)
        block = ctx.enter_context(nc.Block())

        def turns(t, h):
            out_ = ["probs"] * 3 if (h >= 2 or not first(t)) and (not last_(t) or h < 2) else []
            if not first(t) and h == 3:
                out_ = out_ + ["attnT"]
            if not first(t) and h == 4:
                out_ = out_ + ["out"]
            return out_

        def first(t):
            return isinstance(t, int) and t == 0

        def last_(t):
            return isinstance(t, int) and t == TILES

        def turn(t, h, n):
            kinds = [k for h_ in range(HEADS) for k in turns(1, h_)]
            if first(t):
                at, base = sum(len(turns(0, h_)) for h_ in range(h)) + n, 0
                kinds = ["probs"] * (3 * HEADS - 6)
                act = dve = max(at - 1, 0)
                return at, at, act, dve
            at = sum(len(turns(1, h_)) for h_ in range(h)) + n
            if last_(t):
                at = sum(len(turns(TILES, h_)) for h_ in range(h)) + n
                kinds = [k for h_ in range(HEADS) for k in turns(TILES, h_)]
            seq = ["probs", "probs"] + kinds
            act = sum(k != "out" for k in seq[:at + 1]) - 2
            dve = sum(k != "attnT" for k in seq[:at + 1]) - 2
            n0, a0 = 3 * HEADS - 6, 3 * HEADS - 6
            return at, n0 + (t - 1) * (3 * HEADS + 2) + at, a0 + (t - 1) * (3 * HEADS + 1) + act, \
                a0 + (t - 1) * (3 * HEADS + 1) + dve

        def OUT_DVE(t):
            seq = [k for h_ in range(5) for k in turns(TILES if last_(t + 1) else 1, h_)]
            return 3 * HEADS - 6 + t * (3 * HEADS + 1) + sum(k != "attnT" for k in seq)

        def w_view(ap):
            return ap.rearrange("(f p) n -> p f n", p=128)

        @block.sync
        def _(sp):
            sp.dma_start(src_i, a["src"].rearrange("(g e) -> g e", e=EG)).then_inc(edges_in, 16)
            sp.dma_start(dst_i, a["dst"].rearrange("(g e) -> g e", e=EG)).then_inc(edges_in, 16)
            sp.dma_start(regA[0:ROWS, :, :], a["x"].rearrange("(t p) n -> p t n", p=ROWS)).then_inc(x_in, 16)
            for freed in FREED:
                sp.sem_inc(freed, FREE)
            sp.dma_start(wA[:, :, :], w_view(a["Wl0T"])).then_inc(sage0_in, 16)
            sp.dma_start(wB[:, :, :], w_view(a["Wr0T"])).then_inc(sage0_in, 16)
            for i, n in enumerate(("bl0", "bl1", "b2")):
                sp.dma_start(biases[32 * i:32 * i + 1, :], a[n].rearrange("(o n) -> o n", o=1)).then_inc(bias_in, 16)
            sp.dma_start(wC[:, :, :], w_view(a["Wl1T"])).then_inc(sage1_in, 16)
            sp.dma_start(wD[:, :, :], w_view(a["Wr1T"])).then_inc(sage1_in, 16)
            sp.dma_start(wdT[:, :, :], w_view(a["wdT"][:, 0:GRID])).then_inc(expert_in, 16)
            sp.dma_start(wu[:, :, :], a["wu"][0:GRID, :].rearrange("(e p) n -> p e n", p=128)).then_inc(expert_in, 16)
            sp.dma_start(b1c[:, :], a["b1c"]).then_inc(b1_in, 16)
            sp.dma_start(rb1[:, :], a["rb1"].rearrange("(p o) -> p o", o=1)).then_inc(b1_in, 16)
            sp.dma_start(rw2[:, :], a["rw2"]).then_inc(b1_in, 16)
            sp.dma_start(rb2[:, :], a["rb2"].rearrange("(o n) -> o n", o=1)).then_inc(b1_in, 16)
            sp.wait_ge(s0_dense, TILES + FREE)
            sp.dma_start(wA[:, :, :], w_view(a["wq"])).then_inc(peer_in, 16)
            sp.wait_ge(keys_zero, 1)
            for h in range(HEADS):
                b = h % 4
                sp.dma_start(keyb[32 * b:32 * b + 32, h // 4, KEYS * b:KEYS * b + KEYS],
                             a["keysT"][0, h]).then_inc(peer_in, 16)
            with sp.Fori(0, TILES) as t:
                sp.wait_ge(x1_norm, t + FREE)
                sp.dma_start(xres[0:ROWS, :], a["x"].rearrange("(t p) n -> p t n", p=ROWS)[:, ds(t, 1), :]
                             ).then_inc(x_again, 16)
            sp.wait_ge(s1_dense, TILES + FREE)
            sp.dma_start(wC[:, :, :], w_view(a["W1"])).then_inc(gin_in, 16)
            sp.dma_start(wD[:, :, :], w_view(a["W2"])).then_inc(gin_in, 16)
            sp.wait_ge(f_hid, TILES + FREE)
            sp.dma_start(rw1, w_view(a["rw1"])).then_inc(router_in, 16)
            sp.wait_ge(r_sel, 1)
            sel = sp.value_load(seli[0:1, 0:1], min_val=0, max_val=2)
            for i, n_kv in enumerate(KV_OPTS):
                reps = HEADS // n_kv
                with sp.If(sel == i):
                    for w, n in ((wA, "wk"), (wB, "wv")):
                        for f in range(FC):
                            dst = w[:, f, :].rearrange("p (k r d) -> p k r d", r=reps, d=DHEAD)
                            rows_ = w_view(a[f"{n}{i}"])[:, f, :].rearrange("p (k d) -> p k d", d=DHEAD)
                            sp.dma_start(dst, rows_.unsqueeze(2).broadcast_to([128, n_kv, reps, DHEAD])
                                         ).then_inc(kv_arrived, 16)
                    sp.wait_ge(n_dense, TILES)
                    sp.dma_start(wC[:, :, :], w_view(a[f"wq{i}"])).then_inc(qo_arrived, 16)
                    sp.dma_start(wD[:, :, :], w_view(a[f"wo{i}"])).then_inc(qo_arrived, 16)
            sp.wait_ge(kv_arrived, 16 * 2 * FC)
            sp.sem_inc(kv_ready, 1)
            sp.wait_ge(qo_arrived, 32)
            sp.sem_inc(qo_ready, 1)
            for part in range(2):
                n = TILES // 2 * (part + 1)
                at = slice(NODES // 2 * part, NODES // 2 * (part + 1))
                sp.wait_ge(k_high, n + FREE)
                sp.wait_ge(k_low, n + FREE)
                for k in (key_h, key_l):
                    kk = k.rearrange("p (c e) n -> p e c n", e=2)
                    sp.dma_start(kk[64:128, 0, :, at], kk[0:64, 0, :, at]).then_inc(crossed, 16)
                    sp.dma_start(kk[0:64, 1, :, at], kk[64:128, 1, :, at]).then_inc(crossed, 16)
                sp.wait_ge(q_high, n + FREE)
                sp.wait_ge(q_low, n + FREE)
                qq = query.rearrange("p (c e) n -> p e c n", e=2)
                sp.dma_start(qq[64:128, 0, :, at], cross[0:64, :, at]).then_inc(crossed, 16)
                sp.dma_start(qq[0:64, 1, :, at], cross[64:128, :, at]).then_inc(crossed, 16)
            with sp.Fori(0, TILES - 1) as t:
                sp.wait_ge(tr_dve, OUT_DVE(t) + FREE)
                sp.dma_start(out.rearrange("(t p) n -> p t n", p=ROWS)[:, ds(t, 1), :], outs).then_inc(stored, 16)
                sp.wait_ge(stored, 16 * t + 16)
                sp.sem_inc(out_free, 1)
            sp.wait_ge(tr_dve, OUT_DVE(TILES - 1) + FREE)
            sp.dma_start(out[NODES - ROWS:NODES, :], outs).then_inc(stored, 16)
            sp.wait_ge(stored, 16 * TILES)

        @block.gpsimd
        def _(g):
            nc.gpsimd.memset(ident[:, :], 0.0).then_inc(consts_set, 1)
            nc.gpsimd.memset(nhalf[:, :], -0.5).then_inc(consts_set, 1)
            nc.gpsimd.memset(ones_b[:, :], 1.0).then_inc(consts_set, 1)
            nc.gpsimd.memset(ones_r[:, :], 1.0).then_inc(consts_set, 1)
            g.wait_ge(consts_set, 4)
            nc.gpsimd.affine_select(out=ident[:, :], in_=ident[:, :], compare_op=ALU.not_equal, fill=1.0, base=0,
                                    pattern=[[-1, 128]], channel_multiplier=1).then_inc(consts_set, 1)
            nc.gpsimd.iota(iota_n, pattern=[[1, OH_W]], base=0, channel_multiplier=0,
                           allow_small_or_imprecise_dtypes=True).then_inc(iotas_set, 1)
            nc.gpsimd.iota(iota_w, pattern=[[1, WIN]], base=0, channel_multiplier=0,
                           allow_small_or_imprecise_dtypes=True).then_inc(iotas_set, 1)
            nc.gpsimd.memset(adjf, 0.0).then_inc(adj_zero, 1)

            def inv_std(n, dve_sem, dve_at, sem_out, b):
                g.wait_ge(dve_sem, dve_at)
                g.nop(nofuse=True)
                nc.gpsimd.tensor_scalar(rstd[0:ROWS, b:b + 1], mv[0:ROWS, b, 1:2], LN_EPS, None, ALU.add
                                        ).then_inc(sem_out, 1)
                g.wait_ge(sem_out, n + 1)
                nc.gpsimd.tensor_tensor(rstd[0:ROWS, b:b + 1], rstd[0:ROWS, b:b + 1], nhalf[0:ROWS, 0:1], ALU.pow
                                        ).then_inc(sem_out, 1)

            with g.Fori(0, TILES // 2) as u:
                for b in range(2):
                    inv_std(4 * u + 2 * b, ln1_dve, 4 * u + 2 * (b + 1), ln1_rstd, b)

            g.wait_ge(ln1_done, TILES)
            with g.Fori(0, TILES) as t:
                g.wait_ge(s0_tr, t + FREE)
                g.nop(nofuse=True)
                nc.gpsimd.tensor_copy(row[0:ROWS, :], regA[0:ROWS, ds(t, 1), :]).then_inc(s0_rows, 1)
            g.wait_ge(s0_dense, TILES + FREE)
            nc.gpsimd.memset(wB[:, :, :], 0.0).then_inc(keys_zero, 1)

            def rows(t):
                g.wait_ge(s0_out, TILES + FREE)
                g.wait_ge(s0_tr, TILES + FREE)
                g.wait_ge(f_tr, t + FREE)
                g.nop(nofuse=True)
                nc.gpsimd.tensor_copy(row[0:ROWS, :], regB[0:ROWS, ds(t, 1), :]).then_inc(s1_rows, 1)

            def pair_scores(t, k):
                hs = slice(4 * k, 4 * k + 4)
                g.wait_ge(p_top, 10 * t + 5 * (k + 1) + FREE)
                if k == 0:
                    g.wait_ge(p_weight, 2 * t + FREE)
                g.nop(nofuse=True)
                nc.gpsimd.tensor_copy(i16f[0:ROWS, hs, :], i16[0:ROWS, hs, :]).then_inc(p_grid, 1)
                g.wait_ge(p_grid, 4 * t + 2 * k + 1 + FREE)
                o = grid[0:ROWS, hs, :].rearrange("p h (a b) -> p h a b", b=TOPK)
                nc.gpsimd.tensor_tensor(o, v16[0:ROWS, hs, :].unsqueeze(3).broadcast_to([ROWS, 4, TOPK, TOPK]),
                                        i16f[0:ROWS, hs, :].unsqueeze(2).broadcast_to([ROWS, 4, TOPK, TOPK]),
                                        ALU.add).then_inc(p_grid, 1)

            def neg_max(t, k):
                hs = slice(4 * k, 4 * k + 4)
                g.wait_ge(p_pick, 8 * t + 4 * k + 1)
                g.nop(nofuse=True)
                nc.gpsimd.tensor_scalar(nz[0:ROWS, hs], z16[0:ROWS, hs, 0], -1.0, None, ALU.mult).then_inc(p_nz, 1)

            def diagonals(t):
                g.wait_ge(p_rz, t + 1)
                g.wait_ge(b_p, t + FREE)
                g.nop(nofuse=True)
                for h in range(HEADS):
                    last = nc.gpsimd.tensor_scalar(diag[0:ROWS, h, :], ident[0:ROWS, 0:ROWS], rz[0:ROWS, h:h + 1],
                                                   None, ALU.mult)
                last.then_inc(p_diag, 1)

            def gelu_tile(t):
                g.wait_ge(f_hidT, t + 1 + FREE)
                nc.gpsimd.tensor_tensor(gt1[:, :], hidT[:, :], hidT[:, :], ALU.mult).then_inc(g_pool, 1)
                g.wait_ge(g_pool, 4 * t + 1)
                g.nop(nofuse=True)
                nc.gpsimd.tensor_scalar(gt1[:, :], gt1[:, :], GELU_A, 1.0, ALU.mult, ALU.add).then_inc(g_pool, 1)
                g.wait_ge(g_pool, 4 * t + 2)
                nc.gpsimd.tensor_tensor(gt1[:, :], gt1[:, :], hidT[:, :], ALU.mult).then_inc(g_pool, 1)
                g.wait_ge(g_tanh, t + 1)
                g.nop(nofuse=True)
                nc.gpsimd.tensor_scalar(gt1[:, :], gt1[:, :], 1.0, 0.5, ALU.add, ALU.mult).then_inc(g_pool, 1)
                g.wait_ge(g_pool, 4 * t + 4)
                nc.gpsimd.tensor_tensor(gelu[:, :], gt1[:, :], hidT[:, :], ALU.mult).then_inc(g_done, 1)

            def coefficients(t):
                g.wait_ge(b_pS, t + 1 + FREE)
                g.wait_ge(g_done, t + 1 + FREE)
                nc.gpsimd.tensor_tensor(coef[:, :], coef[:, :], gelu[:, :], ALU.mult).then_inc(b_coef, 1)

            def residual2(t):
                g.wait_ge(b_upS, t + 1 + FREE)
                nc.gpsimd.tensor_tensor(xs[0:ROWS, ds(t, 1), :], xs[0:ROWS, ds(t, 1), :], ups[0:ROWS, :].unsqueeze(1),
                                        ALU.add).then_inc(x2_done, 1)

            rows(0)
            inv_std(0, x1_dve, 3, x1_rstd, 0)
            gelu_tile(0)
            with g.Fori(1, TILES) as t:
                pair_scores(t - 1, 0)
                pair_scores(t - 1, 1)
                rows(t)
                neg_max(t - 1, 0)
                inv_std(2 * t, x1_dve, 3 * t + 3, x1_rstd, 0)
                neg_max(t - 1, 1)
                diagonals(t - 1)
                coefficients(t - 1)
                gelu_tile(t)
                residual2(t - 1)
            pair_scores(TILES - 1, 0)
            pair_scores(TILES - 1, 1)
            neg_max(TILES - 1, 0)
            neg_max(TILES - 1, 1)
            diagonals(TILES - 1)
            coefficients(TILES - 1)
            residual2(TILES - 1)

            g.wait_ge(s1_agg, TILES)
            for t in range(TILES):
                v = adj[0:ROWS, t, ROWS * t:ROWS * t + ROWS]
                last = nc.gpsimd.tensor_tensor(v, v, ident[0:ROWS, 0:ROWS], ALU.add)
            last.then_inc(self_added, 1)
            with g.Fori(0, TILES // 2) as u:
                for b in range(2):
                    inv_std(4 * u + 2 * b, ln3_dve, 4 * u + 2 * (b + 1), ln3_rstd, b)

            with g.Fori(0, TILES) as t:
                inv_std(2 * t, x4_dve, 2 * t + 2, x4_rstd, 0)

            g.wait_ge(x4_trT, TILES + FREE)
            with g.Fori(0, TILES) as t:
                g.wait_ge(k_v, t + FREE)
                g.nop(nofuse=True)
                nc.gpsimd.tensor_copy(colB[:, :, :], x4T[:, :, ds(t * ROWS, ROWS)]).then_inc(k_cols, 1)

        @block.scalar
        def _(act):
            with act.Fori(0, TILES) as t:
                act.wait_ge(s0_tr, t + 1 + FREE)
                act.wait_ge(s0_dense, t + FREE)
                nc.scalar.copy(colB[:, :, :], psTr).then_inc(s0_trT, 1)
                act.wait_ge(s0_dense, t + 1 + FREE)
                nc.scalar.activation(regB[0:ROWS, ds(t, 1), :], psOut.unsqueeze(1), ACT.Relu).then_inc(s0_out, 1)

            def rows_T(t):
                act.wait_ge(s1_tr, t + 1)
                act.wait_ge(f_q, t + FREE)
                nc.scalar.copy(colB[:, :, :], psTr).then_inc(s1_trT, 1)

            def front(t):
                act.wait_ge(f_tr, t + 1 + FREE)
                nc.scalar.copy(colB[:, :, :], psTr).then_inc(f_trT, 1)
                act.wait_ge(f_q, t + 1 + FREE)
                nc.scalar.mul(colA[:, :, :], psQ, BN_SCALE).then_inc(f_qT, 1)

            def sims(t):
                for c in range(2):
                    act.wait_ge(f_sim, 2 * t + c + 1)
                    if c == 0:
                        act.wait_ge(p_top, 10 * t + FREE)
                    nc.scalar.copy(sim[0:ROWS, 4 * c:4 * c + 4, :].rearrange("p h k -> p (h k)"),
                                   psSim.rearrange("p a b -> p (a b)")).then_inc(f_simS, 1)

            def hidden(t):
                act.wait_ge(f_hid, t + 1 + FREE)
                act.wait_ge(g_done, t + FREE)
                nc.scalar.copy(hidT[:, :], psHid).then_inc(f_hidT, 1)
                act.wait_ge(g_pool, 4 * t + 3)
                nc.scalar.activation(gt1[:, :], gt1[:, :], ACT.Tanh, scale=GELU_C).then_inc(g_tanh, 1)

            def exps(t, k):
                act.wait_ge(p_nz, 2 * t + k + 1)
                act.wait_ge(p_pick, 8 * t + 4 * k + 2)
                for h in range(4 * k, 4 * k + 4):
                    last = nc.scalar.activation(grid[0:ROWS, h, :], grid[0:ROWS, h, :], ACT.Exp,
                                                bias=nz[0:ROWS, h:h + 1])
                act.wait_ge(p_pick, 8 * t + 4 * k + 3)
                for h in range(4 * k, 4 * k + 4):
                    last = nc.scalar.activation(e16[0:ROWS, h, :], z16[0:ROWS, h, :], ACT.Exp,
                                                bias=nz[0:ROWS, h:h + 1], accum_out=zsum[0:ROWS, h:h + 1])
                last.then_inc(p_exp, 1)

            def weights_S(t):
                act.wait_ge(b_p, t + 1 + FREE)
                act.wait_ge(b_up, t + FREE)
                nc.scalar.copy(coef[:, :], psP).then_inc(b_pS, 1)

            def up_S(t):
                act.wait_ge(b_up, t + 1 + FREE)
                act.wait_ge(x2_done, t + FREE)
                nc.scalar.copy(ups[0:ROWS, :], psUp).then_inc(b_upS, 1)

            rows_T(0)
            front(0)
            sims(0)
            hidden(0)
            with act.Fori(1, TILES) as t:
                rows_T(t)
                exps(t - 1, 0)
                front(t)
                exps(t - 1, 1)
                sims(t)
                weights_S(t - 1)
                hidden(t)
                up_S(t - 1)
            exps(TILES - 1, 0)
            exps(TILES - 1, 1)
            weights_S(TILES - 1)
            up_S(TILES - 1)

            def x4_T(t):
                act.wait_ge(x4_tr, t + 1 + FREE)
                nc.scalar.copy(x4T[:, :, ds(t * ROWS, ROWS)], psTr).then_inc(x4_trT, 1)

            def gin(t):
                act.wait_ge(n_agg, t + 1)
                nc.scalar.copy(colA[:, :, :], psAgg).then_inc(n_aggT, 1)
                act.wait_ge(n_u, t + 1)
                for c in range(FC):
                    last = nc.scalar.activation(colB[:, c, :], psQ[:, c, :], ACT.Relu, bias=b1c[:, c:c + 1])
                last.then_inc(n_uT, 1)

            act.wait_ge(b1_in, 64)
            gin(0)
            with act.Fori(1, TILES) as t:
                gin(t)
                x4_T(t - 1)
            x4_T(TILES - 1)

            act.wait_ge(r_hid, 1)
            nc.scalar.activation(hidr[:, :], psE[:, 0:1], ACT.Relu, bias=rb1[:, 0:1]).then_inc(r_hidS, 1)
            act.wait_ge(r_dve, 2)
            nc.scalar.activation(rt[0:1, 8:11], rt[0:1, 0:3], ACT.Exp, bias=rt[0:1, 4:5],
                                 accum_out=rt[0:1, 12:13]).then_inc(r_exp, 1)

            kk = key_h.rearrange("p (c e) n -> p e c n", e=2)
            qq = query.rearrange("p (c e) n -> p e c n", e=2)
            with act.Fori(0, TILES) as t:
                at = ds(t * ROWS, ROWS)
                act.wait_ge(k_k, t + 1)
                nc.scalar.copy(kk[0:64, 0, :, at], psQ[0:64, :, :])
                nc.scalar.copy(kk[64:128, 1, :, at], psQ[64:128, :, :]).then_inc(k_high, 1)
                act.wait_ge(k_q, t + 1)
                nc.scalar.mul(qq[0:64, 0, :, at], psTr[0:64, :, :], DHEAD ** -0.5)
                nc.scalar.mul(cross[64:128, :, at], psTr[64:128, :, :], DHEAD ** -0.5).then_inc(q_high, 1)
                act.wait_ge(k_v, t + 1 + FREE)
                nc.scalar.copy(vals[:, ds(t, 1), 0, :], psOut.unsqueeze(1)).then_inc(v_high, 1)

            def exp_head(t, h):
                n = HEADS * t + h
                act.wait_ge(a_max, n + 1)
                if h == 0 and not first(t):
                    act.wait_ge(a_inv, 2 * t - 1)
                for i, (lo, hi) in enumerate((SC[h % 2][2], OWN[h % 2])):
                    nc.scalar.activation(probs[h % 2][:, lo:hi], psScore(h % 2)[:, lo:hi], ACT.Exp,
                                         bias=nmax[0:ROWS, h:h + 1], accum_out=psum_p[0:ROWS, i, h:h + 1]
                                         ).then_inc(a_exp, 1)

            def act_turn(t, h, n, kind):
                _, number, *_ = turn(t, h, n)
                if kind == "out":
                    return
                act.wait_ge(a_tr, number + 1)
                bank = turn(t, h, n)[0] % 2
                if kind == "attnT":
                    nc.scalar.copy(colB[:, :, :], cols(5 + bank)).then_inc(tr_act, 1)
                    return
                lo, hi = TB[n]
                if n == 0:
                    i = HEADS * t + h - 2
                    if not (first(t) and h < 4):
                        act.wait_ge(a_pv, i - 1)
                nc.scalar.copy(probT[h % 2][:, 0, lo:hi, :],
                               psTP[bank][:, 0:(hi - lo) * ROWS].rearrange("p (t n) -> p t n", n=ROWS)
                               ).then_inc(tr_act, 1)

            def act_step(t, h):
                kinds = turns(t, h)
                if kinds:
                    act_turn(t, h, 0, kinds[0])
                if not first(t) and h == 0:
                    exp_head(t - 1, HEADS - 1)
                elif h >= 1 and not last_(t):
                    exp_head(t, h - 1)
                for n in range(1, len(kinds)):
                    act_turn(t, h, n, kinds[n])

            for h in range(HEADS):
                act_step(0, h)
            with act.Fori(1, TILES) as t:
                for h in range(HEADS):
                    act_step(t, h)
            for h in range(HEADS):
                act_step(TILES, h)

        @block.vector
        def _(v):
            v.wait_ge(edges_in, 32)
            nc.vector.tensor_copy(src_f, src_i).then_inc(edge_dve, 1)
            nc.vector.tensor_copy(dst_f, dst_i).then_inc(edge_dve, 1)
            v.wait_ge(edge_dve, 2)
            nc.vector.tensor_reduce(bm[:, 0:1], dst_f, X, ALU.min).then_inc(edge_dve, 1)
            v.wait_ge(edge_dve, 3)
            nc.vector.tensor_scalar(rel_f, dst_f, bm[:, 0:1], None, ALU.subtract).then_inc(edge_dve, 1)
            v.wait_ge(edge_dve, 4)
            nc.vector.tensor_reduce(bm[:, 1:2], rel_f, X, ALU.max).then_inc(edge_dve, 1)
            v.wait_ge(edge_cols, 1)
            nc.vector.tensor_copy(src_c.rearrange("p g j -> p j g"),
                                  psE[0:EROWS, 0:PER * GROUPS].rearrange("p (j g) -> p j g", j=PER)).then_inc(edge_dve, 1)
            nc.vector.tensor_copy(rel_c.rearrange("p g j -> p j g"),
                                  psE[0:EROWS, PER * GROUPS:2 * PER * GROUPS].rearrange("p (j g) -> p j g", j=PER)
                                  ).then_inc(edge_dve, 1)
            nc.vector.tensor_copy(bmrow, psE[0:1, 2 * PER * GROUPS:2 * (PER + 1) * GROUPS]).then_inc(edge_dve, 1)
            v.wait_ge(edge_dve, 8)
            nc.vector.tensor_copy(basei[:, :], bmrow[:, 0:GROUPS]).then_inc(edge_dve, 1)
            nc.vector.tensor_scalar(bmrow[:, GROUPS:2 * GROUPS], bmrow[:, GROUPS:2 * GROUPS], float(WIN), None,
                                    ALU.is_ge).then_inc(edge_dve, 1)
            v.wait_ge(edge_dve, 10)
            nc.vector.tensor_reduce(flagi[:, 0:1], bmrow[:, GROUPS:2 * GROUPS], X, ALU.max).then_inc(edge_dve, 1)

            v.wait_ge(iotas_set, 2)
            v.wait_ge(adj_zero, 1)
            v.wait_ge(edge_dve, 11)

            def onehots(g_, b):
                for j in range(PER):
                    nc.vector.tensor_scalar(oh_src[b][j].unsqueeze(1), iota_n.unsqueeze(1), src_c[:, ds(g_, 1), j], None,
                                            ALU.is_equal)
                nc.vector.tensor_tensor(oh_dst[:, b, :, :], iota_w.unsqueeze(1).broadcast_to([EROWS, PER, WIN]),
                                        rel_c[:, ds(g_, 1), :].rearrange("p g j -> p (g j)").unsqueeze(2).broadcast_to([EROWS, PER, WIN]),
                                        ALU.is_equal).then_inc(adj_onehot, 1)

            def add_window(n, g_, b):
                v.wait_ge(adj_counted, n + 1)
                v.wait_ge(adj_added, n + FREE)
                first = v.value_load(basei[0:1, ds(g_, 1)], min_val=0, max_val=NODES - 1)
                w = adj[:, :, ds(first, WIN)]
                nc.vector.tensor_tensor(w, w, psAdj[b], ALU.add).then_inc(adj_added, 1)

            onehots(0, 0)
            onehots(1, 1)
            with v.Fori(0, GROUPS // 2 - 1) as u:
                for b in range(2):
                    add_window(2 * u + b, 2 * u + b, b)
                    onehots(2 * u + b + 2, b)
            add_window(GROUPS - 2, GROUPS - 2, 0)
            add_window(GROUPS - 1, GROUPS - 1, 1)

            v.wait_ge(adj_added, GROUPS + FREE)
            spread = v.value_load(flagi[0:1, 0:1], min_val=0, max_val=1)
            with v.If(spread == 1):
                v.wait_ge(rem_counted, 1)
                nc.vector.tensor_tensor(rem_c.rearrange("p g j -> p j g"), rel_c.rearrange("p g j -> p j g"),
                                        psE[0:EROWS, 0:GROUPS].unsqueeze(1).broadcast_to([EROWS, PER, GROUPS]),
                                        ALU.add).then_inc(rem_dve, 1)
                nc.vector.tensor_scalar(rem_t, rel_c, float(WIN), -float(4 * NODES), ALU.is_lt, ALU.mult
                                        ).then_inc(rem_dve, 1)
                v.wait_ge(rem_dve, 2)
                nc.vector.tensor_tensor(rem_c, rem_c, rem_t, ALU.add).then_inc(rem_dve, 1)
                v.wait_ge(rem_dve, 3)
                with v.Fori(0, GROUPS) as gi:
                    v.wait_ge(rem_dve, 3 + gi * (3 * WINDOWS + 1))
                    for j in range(PER):
                        nc.vector.tensor_scalar(oh_src[0][j].unsqueeze(1), iota_n.unsqueeze(1), src_c[:, ds(gi, 1), j],
                                                None, ALU.is_equal)
                    nc.vector.tensor_copy(cur, rem_c[:, ds(gi, 1), :].rearrange("p g j -> p (g j)")
                                          ).then_inc(rem_dve, 1)
                    with v.Fori(0, WINDOWS) as wi:
                        n = 3 + gi * (3 * WINDOWS + 1) + 1 + 3 * wi
                        v.wait_ge(rem_dve, n)
                        nc.vector.tensor_tensor(oh_dst[:, 0, :, :], iota_w.unsqueeze(1).broadcast_to([EROWS, PER, WIN]),
                                                cur.unsqueeze(2).broadcast_to([EROWS, PER, WIN]),
                                                ALU.is_equal).then_inc(rem_dve, 1)
                        v.wait_ge(rem_dve, n + 1)
                        nc.vector.tensor_scalar(cur, cur, float(WIN), None, ALU.subtract).then_inc(rem_dve, 1)
                        v.wait_ge(rem_counted, gi * WINDOWS + wi + 2)
                        w = adj[:, :, ds(wi * WIN, WIN)]
                        nc.vector.tensor_tensor(w, w, psAdj[0], ALU.add).then_inc(rem_dve, 1)
                v.wait_ge(rem_dve, 3 + GROUPS * (3 * WINDOWS + 1))
            nc.vector.tensor_scalar(rdeg, rdeg, 1.0, None, ALU.max).then_inc(degrees_set, 1)
            v.wait_ge(degrees_set, 1)
            nc.vector.reciprocal(rdeg, rdeg).then_inc(degrees_set, 1)

            def norm_two(u, buf_in, buf_out, dve, rs, done):
                for b in range(2):
                    nc.vector.bn_stats(st[0:ROWS, b, :], buf_in[0:ROWS, ds(2 * u + b, 1), :]).then_inc(dve, 1)
                    v.wait_ge(dve, 4 * u + 2 * b + 1)
                    v.nop(nofuse=True)
                    nc.vector.bn_aggr(mv[0:ROWS, b, :], st[0:ROWS, b, :]).then_inc(dve, 1)
                for b in range(2):
                    v.wait_ge(rs, 4 * u + 2 * b + 2)
                    nc.vector.tensor_scalar(buf_out[0:ROWS, ds(2 * u + b, 1), :], buf_in[0:ROWS, ds(2 * u + b, 1), :],
                                            mv[0:ROWS, b, 0:1], rstd[0:ROWS, b:b + 1], ALU.subtract, ALU.mult
                                            ).then_inc(done, 1)

            v.wait_ge(x_in, 16)
            v.wait_ge(consts_set, 5)
            with v.Fori(0, TILES // 2) as u:
                norm_two(u, regA, regA, ln1_dve, ln1_rstd, ln1_done)

            v.wait_ge(degrees_set, 2)

            def mean_T(t, agg, dense, outsem):
                v.wait_ge(agg, t + 1)
                v.wait_ge(dense, t + FREE)
                nc.vector.tensor_tensor(colA[:, :, :], psAgg,
                                        adj[:, TILES:TILES + 1, ds(t * ROWS, ROWS)].broadcast_to([128, FC, ROWS]),
                                        ALU.mult).then_inc(outsem, 1)

            with v.Fori(0, TILES) as t:
                mean_T(t, s0_agg, s0_dense, s0_aggT)

            def mean_T2(t):
                v.wait_ge(f_hid, t + FREE)
                mean_T(t, s1_agg, s1_dense, s1_aggT)

            def x1_tile(t):
                v.wait_ge(s1_dense, t + 1 + FREE)
                v.wait_ge(x_again, 16 * t + 16)
                nc.vector.scalar_tensor_tensor(xs[0:ROWS, ds(t, 1), :], psOut.unsqueeze(1), 0.0, xres[0:ROWS, :].unsqueeze(1),
                                               ALU.max, ALU.add).then_inc(x1_dve, 1)
                v.wait_ge(x1_dve, 3 * t + 1)
                v.nop(nofuse=True)
                nc.vector.bn_stats(st[0:ROWS, 0, :], xs[0:ROWS, ds(t, 1), :]).then_inc(x1_dve, 1)
                v.wait_ge(x1_dve, 3 * t + 2)
                v.nop(nofuse=True)
                nc.vector.bn_aggr(mv[0:ROWS, 0, :], st[0:ROWS, 0, :]).then_inc(x1_dve, 1)
                v.wait_ge(x1_rstd, 2 * t + 2)
                v.wait_ge(s1_tr, t + 1)
                nc.vector.tensor_scalar(row[0:ROWS, :].unsqueeze(1), xs[0:ROWS, ds(t, 1), :], mv[0:ROWS, 0, 0:1], rstd[0:ROWS, 0:1],
                                        ALU.subtract, ALU.mult).then_inc(x1_norm, 1)

            def top16(t, k):
                hs = range(4 * k, 4 * k + 4)
                v.wait_ge(f_simS, 2 * t + k + 1 + FREE)
                v.wait_ge(p_grid, 4 * t + FREE)
                n = 10 * t + 5 * k
                v.nop(nofuse=True)
                for h in hs:
                    last = nc.vector.max(v16[0:ROWS, h, 0:8], sim[0:ROWS, h, :])
                last.then_inc(p_top, 1)
                v.wait_ge(p_top, n + 1 + FREE)
                v.nop(nofuse=True)
                for h in hs:
                    last = nc.vector.max_index(i16[0:ROWS, h, 0:8], v16[0:ROWS, h, 0:8], sim[0:ROWS, h, :])
                last.then_inc(p_top, 1)
                v.wait_ge(p_top, n + 2 + FREE)
                v.nop(nofuse=True)
                for h in hs:
                    last = nc.vector.match_replace(sim[0:ROWS, h, :], v16[0:ROWS, h, 0:8], sim[0:ROWS, h, :], REPLACED)
                last.then_inc(p_top, 1)
                v.wait_ge(p_top, n + 3 + FREE)
                v.nop(nofuse=True)
                for h in hs:
                    last = nc.vector.max(v16[0:ROWS, h, 8:16], sim[0:ROWS, h, :])
                last.then_inc(p_top, 1)
                v.wait_ge(p_top, n + 4 + FREE)
                v.nop(nofuse=True)
                for h in hs:
                    last = nc.vector.max_index(i16[0:ROWS, h, 8:16], v16[0:ROWS, h, 8:16], sim[0:ROWS, h, :])
                last.then_inc(p_top, 1)

            def pick16(t, k):
                hs = range(4 * k, 4 * k + 4)
                n = 8 * t + 4 * k
                v.wait_ge(p_grid, 4 * t + 2 * k + 2 + FREE)
                v.wait_ge(p_exp, 2 * t + FREE)
                v.nop(nofuse=True)
                for h in hs:
                    last = nc.vector.max(z16[0:ROWS, h, 0:8], grid[0:ROWS, h, :])
                last.then_inc(p_pick, 1)
                v.wait_ge(p_pick, n + 1)
                v.wait_ge(b_p, t + FREE)
                v.nop(nofuse=True)
                for h in hs:
                    last = nc.vector.match_replace(left[0:ROWS, h, :], z16[0:ROWS, h, 0:8], grid[0:ROWS, h, :], REPLACED)
                last.then_inc(p_pick, 1)
                v.wait_ge(p_pick, n + 2)
                v.nop(nofuse=True)
                for h in hs:
                    last = nc.vector.max(z16[0:ROWS, h, 8:16], left[0:ROWS, h, :])
                last.then_inc(p_pick, 1)
                v.wait_ge(p_pick, n + 3)
                v.nop(nofuse=True)
                for h in hs:
                    last = nc.vector.match_replace(left[0:ROWS, h, :], z16[0:ROWS, h, 8:16], left[0:ROWS, h, :], REPLACED)
                last.then_inc(p_pick, 1)

            def chosen(t, k):
                hs = slice(4 * k, 4 * k + 4)
                v.wait_ge(p_pick, 8 * t + 4 * k + 4)
                v.wait_ge(p_exp, 2 * t + k + 1 + FREE)
                nc.vector.scalar_tensor_tensor(left[0:ROWS, hs, :], left[0:ROWS, hs, :], TAKEN, grid[0:ROWS, hs, :],
                                               ALU.is_le, ALU.mult).then_inc(p_weight, 1)

            def inv_sums(t):
                v.wait_ge(p_exp, 2 * t + 2 + FREE)
                v.wait_ge(p_diag, t + FREE)
                nc.vector.reciprocal(rz[0:ROWS, :], zsum[0:ROWS, :]).then_inc(p_rz, 1)

            mean_T2(0)
            x1_tile(0)
            top16(0, 0)
            top16(0, 1)
            with v.Fori(1, TILES) as t:
                mean_T2(t)
                pick16(t - 1, 0)
                x1_tile(t)
                pick16(t - 1, 1)
                chosen(t - 1, 0)
                inv_sums(t - 1)
                chosen(t - 1, 1)
                top16(t, 0)
                top16(t, 1)
            pick16(TILES - 1, 0)
            pick16(TILES - 1, 1)
            chosen(TILES - 1, 0)
            inv_sums(TILES - 1)
            chosen(TILES - 1, 1)

            v.wait_ge(x2_done, TILES + FREE)
            with v.Fori(0, TILES // 2) as u:
                norm_two(u, xs, regA, ln3_dve, ln3_rstd, ln3_done)

            with v.Fori(0, TILES) as t:
                v.wait_ge(n_dense, t + 1)
                nc.vector.tensor_tensor(xs[0:ROWS, ds(t, 1), :], xs[0:ROWS, ds(t, 1), :], psOut.unsqueeze(1), ALU.add
                                        ).then_inc(x3_done, 1)
                v.wait_ge(x3_done, t + 1 + FREE)
                v.nop(nofuse=True)
                nc.vector.bn_stats(st[0:ROWS, 0, :], xs[0:ROWS, ds(t, 1), :]).then_inc(x4_dve, 1)
                v.wait_ge(x4_dve, 2 * t + 1)
                v.nop(nofuse=True)
                nc.vector.bn_aggr(mv[0:ROWS, 0, :], st[0:ROWS, 0, :]).then_inc(x4_dve, 1)
                v.wait_ge(x4_rstd, 2 * t + 2)
                v.wait_ge(x4_tr, t + FREE)
                nc.vector.tensor_scalar(row[0:ROWS, :].unsqueeze(1), xs[0:ROWS, ds(t, 1), :], mv[0:ROWS, 0, 0:1], rstd[0:ROWS, 0:1],
                                        ALU.subtract, ALU.mult).then_inc(x4_norm, 1)

            v.wait_ge(x4_trT, TILES + FREE)
            nc.vector.tensor_reduce(meanc[:, :], x4T, X, ALU.add).then_inc(r_mean, 1)
            v.wait_ge(r_mean, 1)
            nc.vector.tensor_scalar(meanc[:, :], meanc[:, :], 1.0 / NODES, None, ALU.mult).then_inc(r_mean, 1)
            v.wait_ge(r_logit, 1)
            v.wait_ge(b1_in, 64)
            nc.vector.tensor_tensor(rt[0:1, 0:3], psE[0:1, 4:7], rb2[0:1, :], ALU.add).then_inc(r_dve, 1)
            v.wait_ge(r_dve, 1)
            nc.vector.tensor_reduce(rt[0:1, 4:5], rt[0:1, 0:3], X, ALU.max, negate=True).then_inc(r_dve, 1)
            v.wait_ge(r_exp, 1)
            nc.vector.reciprocal(rt[0:1, 13:14], rt[0:1, 12:13]).then_inc(r_dve, 1)
            v.wait_ge(r_dve, 3)
            nc.vector.tensor_scalar(rt[0:1, 16:19], rt[0:1, 8:11], rt[0:1, 13:14], None, ALU.mult).then_inc(r_dve, 1)
            v.wait_ge(r_dve, 4)
            nc.vector.tensor_reduce(rt[0:1, 20:21], rt[0:1, 16:19], X, ALU.max).then_inc(r_dve, 1)
            v.wait_ge(r_dve, 5)
            nc.vector.tensor_scalar(rt[0:1, 24:27], rt[0:1, 16:19], rt[0:1, 20:21], None, ALU.is_lt).then_inc(r_dve, 1)
            v.wait_ge(r_dve, 6)
            nc.vector.tensor_scalar(rt[0:1, 28:29], rt[0:1, 25:26], 1.0, None, ALU.add).then_inc(r_dve, 1)
            v.wait_ge(r_dve, 7)
            nc.vector.tensor_tensor(seli[0:1, 0:1], rt[0:1, 28:29], rt[0:1, 24:25], ALU.mult).then_inc(r_sel, 1)

            kl = key_l.rearrange("p (c e) n -> p e c n", e=2)
            kk = key_h.rearrange("p (c e) n -> p e c n", e=2)
            qq = query.rearrange("p (c e) n -> p e c n", e=2)
            with v.Fori(0, TILES) as t:
                at = ds(t * ROWS, ROWS)
                v.wait_ge(k_high, t + 1 + FREE)
                nc.vector.tensor_tensor(kl[0:64, 0, :, at], psQ[0:64, :, :], kk[0:64, 0, :, at], ALU.subtract)
                nc.vector.tensor_tensor(kl[64:128, 1, :, at], psQ[64:128, :, :], kk[64:128, 1, :, at], ALU.subtract
                                        ).then_inc(k_low, 1)
                v.wait_ge(q_high, t + 1 + FREE)
                nc.vector.scalar_tensor_tensor(cross[0:64, :, at], psTr[0:64, :, :], DHEAD ** -0.5,
                                               qq[0:64, 0, :, at], ALU.mult, ALU.subtract)
                nc.vector.scalar_tensor_tensor(qq[64:128, 1, :, at], psTr[64:128, :, :], DHEAD ** -0.5,
                                               cross[64:128, :, at], ALU.mult, ALU.subtract).then_inc(q_low, 1)
                v.wait_ge(v_high, t + 1 + FREE)
                nc.vector.tensor_tensor(vals[:, ds(t, 1), 1, :], psOut.unsqueeze(1), vals[:, ds(t, 1), 0, :],
                                        ALU.subtract).then_inc(v_low, 1)

            def max_head(t, h):
                n = HEADS * t + h
                v.wait_ge(a_score, n + 1)
                if not first(t):
                    v.wait_ge(a_exp, 2 * (HEADS * (t - 1) + h + 1))
                nc.vector.tensor_reduce(nmax[0:ROWS, h:h + 1], psScore(h % 2), X, ALU.max, negate=True
                                        ).then_inc(a_max, 1)

            def dve_turn(t, h, n, kind):
                place, number, act_n, _ = turn(t, h, n)
                bank = place % 2
                if kind == "attnT":
                    return
                if kind == "out":
                    v.wait_ge(a_tr, number + 1)
                    v.wait_ge(out_free, t - 1 + FREE)
                    nc.vector.tensor_tensor(outs.unsqueeze(1), psTP[bank].unsqueeze(1), xs[0:ROWS, ds(t - 1, 1), :],
                                            ALU.add).then_inc(tr_dve, 1)
                    return
                lo, hi = TB[n]
                v.wait_ge(tr_act, taken_act(t, h, n) + 1)
                nc.vector.tensor_tensor(probT[h % 2][:, 1, lo:hi, :],
                                        psTP[bank][:, 0:(hi - lo) * ROWS].rearrange("p (t n) -> p t n", n=ROWS),
                                        probT[h % 2][:, 0, lo:hi, :], ALU.subtract).then_inc(tr_dve, 1)

            def taken_act(t, h, n):
                if first(t):
                    return turn(t, h, n)[0]
                k = [x for h_ in range(h) for x in turns(t if last_(t) else 1, h_)] + turns(t if last_(t) else 1, h)[:n]
                return 3 * HEADS - 6 + (t - 1) * (3 * HEADS + 1) + sum(x != "out" for x in k)

            def dve_step(t, h):
                kinds = turns(t, h)
                if not first(t) and h == 0:
                    max_head(t - 1, HEADS - 1)
                elif h >= 1 and not last_(t):
                    max_head(t, h - 1)
                for n, kind in enumerate(kinds):
                    dve_turn(t, h, n, kind)
                if not first(t) and h == 0:
                    v.wait_ge(a_exp, 2 * HEADS * t)
                    nc.vector.tensor_tensor(psums[0:ROWS, :], psum_p[0:ROWS, 0, :], psum_p[0:ROWS, 1, :], ALU.add
                                            ).then_inc(a_inv, 1)
                if not first(t) and h == 1:
                    v.wait_ge(a_inv, 2 * t - 1)
                    nc.vector.reciprocal(rinv[0:ROWS, :], psums[0:ROWS, :]).then_inc(a_inv, 1)
                if not first(t) and h == 2:
                    v.wait_ge(a_inv, 2 * t)
                    v.wait_ge(a_pv, HEADS * t)
                    nc.vector.tensor_tensor(attn.rearrange("p (h d) -> p h d", d=DHEAD),
                                            psPV.rearrange("p (h d) -> p h d", d=DHEAD),
                                            rinv[0:ROWS, :].unsqueeze(2).broadcast_to([ROWS, HEADS, DHEAD]),
                                            ALU.mult).then_inc(a_norm, 1)

            for h in range(HEADS):
                dve_step(0, h)
            with v.Fori(1, TILES) as t:
                for h in range(HEADS):
                    dve_step(t, h)
            for h in range(HEADS):
                dve_step(TILES, h)

        @block.tensor
        def _(pe):
            mm, tr = nc.tensor.matmul, nc.tensor.transpose
            idr = ident[0:ROWS, 0:ROWS]
            pe.wait_ge(consts_set, 5)
            pe.wait_ge(edge_dve, 5)
            idg = ident[0:GROUPS, 0:GROUPS]
            for j in range(PER):
                tr(psE[0:EROWS, GROUPS * j:GROUPS * (j + 1)], src_f[:, EROWS * j:EROWS * (j + 1)], idg)
            for j in range(PER):
                tr(psE[0:EROWS, GROUPS * (PER + j):GROUPS * (PER + j + 1)], rel_f[:, EROWS * j:EROWS * (j + 1)], idg)
            tr(psE[0:1, 2 * PER * GROUPS:(2 * PER + 1) * GROUPS], bm[:, 0:1], idg)
            tr(psE[0:1, (2 * PER + 1) * GROUPS:(2 * PER + 2) * GROUPS], bm[:, 1:2], idg).then_inc(edge_cols, 1)

            def count(b, ohs):
                for t in range(TILES):
                    for j in range(PER):
                        mm(psAdj[b][:, t, :], ohs[j][:, ROWS * t:ROWS * t + 128], oh_dst[:, b, j, :],
                           start=j == 0, stop=j == PER - 1)
                for j in range(PER):
                    last = mm(psAdj[b][:, TILES, :], ones_b[0:EROWS, :], oh_dst[:, b, j, :],
                              start=j == 0, stop=j == PER - 1)
                return last

            with pe.Fori(0, GROUPS // 2) as u:
                for b in range(2):
                    pe.wait_ge(adj_onehot, 2 * u + b + 1)
                    count(b, oh_src[b]).then_inc(adj_counted, 1)
            pe.wait_ge(adj_added, GROUPS + FREE)
            spread = pe.value_load(flagi[0:1, 0:1], min_val=0, max_val=1)
            with pe.If(spread == 1):
                mm(psE[0:EROWS, 0:GROUPS], ones_r[0:1, 0:EROWS], bmrow[:, 0:GROUPS], start=True, stop=True
                   ).then_inc(rem_counted, 1)
                with pe.Fori(0, GROUPS) as gi:
                    with pe.Fori(0, WINDOWS) as wi:
                        pe.wait_ge(rem_dve, 3 + gi * (3 * WINDOWS + 1) + 1 + 3 * wi + 1)
                        count(0, oh_src[0]).then_inc(rem_counted, 1)

            def aggregate(t, x):
                for f in range(FC):
                    for k in range(TILES):
                        last = mm(psAgg[:, f, :], x[0:ROWS, k, 128 * f:128 * f + 128],
                                  adj[0:ROWS, k, ds(t * ROWS, ROWS)], start=k == 0, stop=k == TILES - 1)
                return last

            def transpose4(o, x):
                for f in range(FC):
                    last = tr(o[:, f, :], x[:, 128 * f:128 * f + 128], idr)
                return last

            def to_rows(o, lhs, w, start=True, stop=True):
                for f in range(FC):
                    last = mm(o, lhs[:, f, :], w[:, f, :], start=start and f == 0, stop=stop and f == FC - 1)
                return last

            def to_cols(o, w, rhs):
                for c in range(o.shape[1]):
                    for f in range(FC):
                        last = mm(o[:, c, :], w[:, f, 128 * c:128 * c + 128], rhs[:, f, :],
                                  start=f == 0, stop=f == FC - 1)
                return last

            def bias(o, i, stop):
                return mm(o, ones_r[32 * i:32 * i + 1, :], biases[32 * i:32 * i + 1, :], start=False, stop=stop)

            pe.wait_ge(degrees_set, 2)
            pe.wait_ge(ln1_done, TILES)
            pe.wait_ge(sage0_in, 32)
            pe.wait_ge(bias_in, 48)
            with pe.Fori(0, TILES) as t:
                pe.wait_ge(s0_aggT, t + FREE)
                aggregate(t, regA).then_inc(s0_agg, 1)
                pe.wait_ge(s0_rows, t + 1)
                pe.wait_ge(s0_trT, t + FREE)
                transpose4(psTr, row[0:ROWS, :]).then_inc(s0_tr, 1)
                pe.wait_ge(s0_out, t + FREE)
                pe.wait_ge(s0_aggT, t + 1 + FREE)
                to_rows(psOut, colA, wA, stop=False)
                pe.wait_ge(s0_trT, t + 1 + FREE)
                to_rows(psOut, colB, wB, start=False, stop=False)
                bias(psOut, 0, True).then_inc(s0_dense, 1)

            pe.wait_ge(s0_out, TILES + FREE)
            pe.wait_ge(sage1_in, 32)

            def sage(t):
                pe.wait_ge(s1_aggT, t + FREE)
                aggregate(t, regB).then_inc(s1_agg, 1)
                pe.wait_ge(s1_rows, t + 1)
                pe.wait_ge(f_trT, t + FREE)
                transpose4(psTr, row[0:ROWS, :]).then_inc(s1_tr, 1)
                pe.wait_ge(x1_norm, t + FREE)
                pe.wait_ge(s1_aggT, t + 1 + FREE)
                to_rows(psOut, colA, wC, stop=False)
                pe.wait_ge(s1_trT, t + 1)
                to_rows(psOut, colB, wD, start=False, stop=False)
                bias(psOut, 1, True).then_inc(s1_dense, 1)

            def front(t):
                pe.wait_ge(x1_norm, t + 1 + FREE)
                transpose4(psTr, row[0:ROWS, :]).then_inc(f_tr, 1)
                pe.wait_ge(f_trT, t + 1 + FREE)
                pe.wait_ge(f_qT, t + FREE)
                to_cols(psQ, wA, colB).then_inc(f_q, 1)
                pe.wait_ge(f_qT, t + 1 + FREE)
                for c in range(2):
                    pe.wait_ge(f_simS, 2 * t + c + FREE)
                    for n in range(2):
                        last = mm(psSim[:, n, :], colA[:, c, :], keyb[:, c, 512 * n:512 * n + 512],
                                  start=True, stop=True)
                    last.then_inc(f_sim, 1)
                pe.wait_ge(f_hidT, t + FREE)
                to_cols(psHid.rearrange("p (c n) -> p c n", n=ROWS), wdT, colA).then_inc(f_hid, 1)

            def back(t):
                pe.wait_ge(p_weight, 2 * t + 2 + FREE)
                pe.wait_ge(p_diag, t + 1 + FREE)
                pe.wait_ge(b_pS, t + FREE)
                pe.wait_ge(f_hidT, t + 1 + FREE)
                for e in range(2):
                    for h in range(HEADS):
                        last = mm(psP[:, ROWS * e:ROWS * (e + 1)], left[0:ROWS, h, 128 * e:128 * e + 128],
                                  diag[0:ROWS, h, :], start=h == 0, stop=h == HEADS - 1)
                last.then_inc(b_p, 1)
                pe.wait_ge(b_coef, t + 1)
                pe.wait_ge(b_upS, t + FREE)
                for e in range(2):
                    last = mm(psUp, coef[:, ROWS * e:ROWS * (e + 1)], wu[:, e, :], start=e == 0, stop=e == 1)
                last.then_inc(b_up, 1)

            sage(0)
            pe.wait_ge(peer_in, 16 * (1 + HEADS))
            pe.wait_ge(expert_in, 32)
            front(0)
            with pe.Fori(1, TILES) as t:
                sage(t)
                front(t)
                back(t - 1)
            back(TILES - 1)

            def gin(t):
                pe.wait_ge(n_aggT, t + FREE)
                aggregate(t, regA).then_inc(n_agg, 1)

            def gin_mlp(t):
                pe.wait_ge(n_aggT, t + 1 + FREE)
                to_cols(psQ, wC, colA).then_inc(n_u, 1)
                pe.wait_ge(n_uT, t + 1)
                pe.wait_ge(x3_done, t + FREE)
                to_rows(psOut, colB, wD, stop=False)
                bias(psOut, 2, True).then_inc(n_dense, 1)

            def x4_transposed(t):
                pe.wait_ge(x4_norm, t + 1)
                pe.wait_ge(x4_trT, t + FREE)
                transpose4(psTr, row[0:ROWS, :]).then_inc(x4_tr, 1)

            pe.wait_ge(ln3_done, TILES)
            pe.wait_ge(self_added, 1)
            pe.wait_ge(gin_in, 32)
            gin(0)
            gin_mlp(0)
            with pe.Fori(1, TILES) as t:
                gin(t)
                x4_transposed(t - 1)
                gin_mlp(t)
            x4_transposed(TILES - 1)

            pe.wait_ge(router_in, 16)
            pe.wait_ge(r_mean, 2)
            pe.wait_ge(b1_in, 64)
            for f in range(FC):
                last = mm(psE[:, 0:1], rw1[:, f, :], meanc[:, f:f + 1], start=f == 0, stop=f == FC - 1)
            last.then_inc(r_hid, 1)
            pe.wait_ge(r_hidS, 1)
            mm(psE[0:1, 4:7], hidr[:, :], rw2[:, :], start=True, stop=True).then_inc(r_logit, 1)

            pe.wait_ge(kv_ready, 1)
            pe.wait_ge(qo_ready, 1)
            with pe.Fori(0, TILES) as t:
                xt = x4T[:, :, ds(t * ROWS, ROWS)]
                pe.wait_ge(k_low, t + FREE)
                to_cols(psQ, wA, xt).then_inc(k_k, 1)
                pe.wait_ge(q_low, t + FREE)
                to_cols(psTr, wC, xt).then_inc(k_q, 1)
                pe.wait_ge(k_cols, t + 1)
                pe.wait_ge(v_low, t + FREE)
                to_rows(psOut, colB, wB).then_inc(k_v, 1)

            pe.wait_ge(crossed, 16 * 12)
            pe.wait_ge(v_low, TILES + FREE)

            def score(t, h, c):
                if c == 0 and not (first(t) and h < 2):
                    pe.wait_ge(a_exp, 2 * (HEADS * t + h - 1))
                if c == 2 and not (first(t) and h < 1):
                    pe.wait_ge(a_exp, 2 * (HEADS * t + h - 1) + 1)
                lo, hi = SC[h % 2][c]
                o = psScore(h % 2)[:, lo:hi]
                q = query[:, h, ds(t * ROWS, ROWS)]
                mm(o, q, key_h[:, h, lo:hi], start=True, stop=False)
                last = mm(o, q, key_l[:, h, lo:hi], start=False, stop=True)
                if c == 2:
                    last.then_inc(a_score, 1)

            def pe_turn(t, h, n, kind):
                place, number, act_n, dve_n = turn(t, h, n)
                bank = place % 2
                if not (first(t) and place < 2):
                    pe.wait_ge(tr_act, act_n)
                    pe.wait_ge(tr_dve, dve_n + FREE)
                if kind == "attnT":
                    pe.wait_ge(a_norm, t)
                    transpose4(cols(5 + bank), attn).then_inc(a_tr, 1)
                elif kind == "out":
                    pe.wait_ge(tr_act, attn_taken(t))
                    to_rows(psTP[bank], colB, wD).then_inc(a_tr, 1)
                else:
                    lo, hi = TB[n]
                    if n == 0:
                        pe.wait_ge(a_exp, 2 * (HEADS * t + h - 1))
                    for k in range(lo, hi):
                        last = tr(psTP[bank][:, ROWS * (k - lo):ROWS * (k - lo + 1)],
                                  probs[h % 2][:, ROWS * k:ROWS * (k + 1)], idr)
                    last.then_inc(a_tr, 1)

            def attn_taken(t):
                k = [x for h_ in range(4) for x in turns(t if last_(t) else 1, h_)]
                return 3 * HEADS - 6 + (t - 1) * (3 * HEADS + 1) + sum(x != "out" for x in k)

            def taken_by_dve(t, h):
                if first(t):
                    return sum(len(turns(0, h_)) for h_ in range(h + 1))
                k = [x for h_ in range(h + 1) for x in turns(t if last_(t) else 1, h_)]
                return 3 * HEADS - 6 + (t - 1) * (3 * HEADS + 1) + sum(x != "attnT" for x in k)

            def prob_v(t, h, step_t, step_h):
                pe.wait_ge(tr_dve, (taken_by_dve(step_t, step_h - 1) if step_h else taken_before(step_t)) + FREE)
                if h == 0 and not first(t):
                    pe.wait_ge(a_norm, t)
                for k in range(TILES):
                    for i in range(2):
                        for j in range(2):
                            last = mm(psPV[:, DHEAD * h:DHEAD * (h + 1)], probT[h % 2][:, i, k, :],
                                      vals[:, k, j, DHEAD * h:DHEAD * (h + 1)],
                                      start=k == i == j == 0, stop=k == TILES - 1 and i == j == 1)
                last.then_inc(a_pv, 1)

            def taken_before(t):
                return 3 * HEADS - 6 + (t - 1) * (3 * HEADS + 1)

            def pe_step(t, h):
                kinds = turns(t, h)
                for c in range(max(3, len(kinds))):
                    if c < 3 and not last_(t):
                        score(t, h, c)
                    if c < len(kinds):
                        pe_turn(t, h, c, kinds[c])
                if h < 3 and not first(t):
                    prob_v(t - 1, h + 5, t, h)
                elif h >= 3 and not last_(t):
                    prob_v(t, h - 3, t, h)

            for h in range(HEADS):
                pe_step(0, h)
            with pe.Fori(1, TILES) as t:
                for h in range(HEADS):
                    pe_step(t, h)
            for h in range(HEADS):
                pe_step(TILES, h)


def kernel(x, src, dst, L0_gnn_Wl0, L0_gnn_bl0, L0_gnn_Wr0, L0_gnn_Wl1, L0_gnn_bl1, L0_gnn_Wr1, L0_ffn_w_q,
           L0_ffn_keys, L0_ffn_weight_down_embed, L0_ffn_weight_up_embed, L1_gnn_W1, L1_gnn_b1, L1_gnn_W2,
           L1_gnn_b2, L1_ffn_r_w1, L1_ffn_r_b1, L1_ffn_r_w2, L1_ffn_r_b2, L1_ffn_wq0, L1_ffn_wk0, L1_ffn_wv0,
           L1_ffn_wo0, L1_ffn_wq1, L1_ffn_wk1, L1_ffn_wv1, L1_ffn_wo1, L1_ffn_wq2, L1_ffn_wk2, L1_ffn_wv2,
           L1_ffn_wo2):
    import numpy as np
    import concourse.bacc as bacc
    from concourse.bass_utils import run_bass_kernel_spmd

    given = dict(x=x, src=src, dst=dst, Wl0T=np.asarray(L0_gnn_Wl0).T, bl0=L0_gnn_bl0, Wr0T=np.asarray(L0_gnn_Wr0).T,
                 Wl1T=np.asarray(L0_gnn_Wl1).T, bl1=L0_gnn_bl1, Wr1T=np.asarray(L0_gnn_Wr1).T, wq=L0_ffn_w_q,
                 keysT=np.asarray(L0_ffn_keys).transpose(2, 0, 3, 1), wdT=np.asarray(L0_ffn_weight_down_embed).T,
                 wu=L0_ffn_weight_up_embed, W1=L1_gnn_W1, b1c=np.asarray(L1_gnn_b1).reshape(FC, 128).T, W2=L1_gnn_W2, b2=L1_gnn_b2,
                 rw1=L1_ffn_r_w1, rb1=L1_ffn_r_b1, rw2=L1_ffn_r_w2, rb2=L1_ffn_r_b2,
                 wq0=L1_ffn_wq0, wk0=L1_ffn_wk0, wv0=L1_ffn_wv0, wo0=L1_ffn_wo0,
                 wq1=L1_ffn_wq1, wk1=L1_ffn_wk1, wv1=L1_ffn_wv1, wo1=L1_ffn_wo1,
                 wq2=L1_ffn_wq2, wk2=L1_ffn_wk2, wv2=L1_ffn_wv2, wo2=L1_ffn_wo2)
    nc = bacc.Bacc("TRN2", target_bir_lowering=False, num_devices=1)
    arrays, aps = {}, {}
    for name, value in given.items():
        v = np.ascontiguousarray(value)
        arrays[f"in_{name}"] = v
        aps[name] = nc.dram_tensor(f"in_{name}", v.shape, mybir.dt.from_np(v.dtype), kind="ExternalInput").ap()
    out = nc.dram_tensor("out_x", (NODES, D), FP32, kind="ExternalOutput").ap()
    build(nc, aps, out)
    r = run_bass_kernel_spmd(nc, [arrays], core_ids=[0])
    return r.results[0]["out_x"]
```

```python
from contextlib import ExitStack

import concourse.bass as bass
from concourse import mybir

FP32 = mybir.dt.float32
BF16 = mybir.dt.bfloat16
FP16 = mybir.dt.float16
I32 = mybir.dt.int32
U32 = mybir.dt.uint32
ALU = mybir.AluOpType
ACT = mybir.ActivationFunctionType
X = mybir.AxisListType.X

NODES, D = 1250, 512
ROWS = 125
TILES = NODES // ROWS
FC = D // 128
EDGES = 21250
EROWS = 125
PER = 5
GROUPS = EDGES // (EROWS * PER)
WIN = 46
SLOTS = TILES + 1
WINDOWS = -(-NODES // WIN)
ADJ_W = NODES + WIN
OH_W = NODES + 3
HEADS, DKEY, KEYS, TOPK = 8, 32, 256, 16
GRID = TOPK * TOPK
DHEAD = 64
LN_EPS = 1e-5
BN_SCALE = float(1.0 / (1.0 + 1e-5) ** 0.5)
REPLACED = -3.0e38
TAKEN = -1.0e38
HALF_EXACT = 2048
FREE = 1
GELU_A, GELU_C = 0.044715, 0.7978845608028654
KV_OPTS = (8, 4, 1)
SC = [[(0, 512), (512, 1024), (1024, NODES)], [(286, 798), (798, NODES), (0, 286)]]
OWN = [(0, 1024), (286, NODES)]
TB = [(0, 4), (4, 8), (8, TILES)]


def build(nc, a, out):
    ctx = ExitStack()
    with ctx:
        def sb(name, shape, dt=FP32):
            return ctx.enter_context(nc.sbuf_tensor(name, shape, dt))

        def sem(name):
            return ctx.enter_context(nc.semaphore(name))

        ds = bass.ds

        adj = sb("adj", [128, SLOTS, ADJ_W])
        regA = sb("regA", [128, TILES, D])
        regB = sb("regB", [128, TILES, D])
        xs = sb("xs", [128, TILES, D])
        wA = sb("wA", [128, FC, D])
        wB = sb("wB", [128, FC, D])
        wC = sb("wC", [128, FC, D])
        wD = sb("wD", [128, FC, D])
        wdT = sb("wdT", [128, FC, GRID])
        wu = sb("wu", [128, 2, D])
        work = sb("work", [128, 3, HEADS, KEYS])
        sim = work[:, 0, :, :]
        grid = work[:, 1, :, :]
        left = work[:, 2, :, :]
        row = sb("row", [128, D])
        colA = sb("colA", [128, FC, ROWS])
        colB = sb("colB", [128, FC, ROWS])
        xres = sb("xres", [128, D])
        ups = sb("ups", [128, D])
        hidT = sb("hidT", [128, 2 * ROWS])
        gt1 = sb("gt1", [128, 2 * ROWS])
        gelu = sb("gelu", [128, 2 * ROWS])
        coef = sb("coef", [128, 2 * ROWS])
        diag = sb("diag", [128, HEADS, ROWS])
        ident = sb("ident", [128, 128])
        ident_h = sb("ident_h", [128, 128], FP16)
        norm_x = sb("norm_x", [128, D])
        ones_c = sb("ones_c", [128, 1])
        zero_c = sb("zero_c", [128, FC])
        ln_s = sb("ln_s", [128, 4])
        ones_b = sb("ones_b", [128, 128], BF16)
        ones_r = sb("ones_r", [65, ROWS])
        biases = sb("biases", [65, D])
        st = sb("st", [128, 2, 6])
        mv = sb("mv", [128, 2, 2])
        rstd = sb("rstd", [128, 2])
        nhalf = sb("nhalf", [128, 2])
        v16 = sb("v16", [128, HEADS, TOPK])
        i16 = sb("i16", [128, HEADS, TOPK], U32)
        i16f = sb("i16f", [128, HEADS, TOPK])
        z16 = sb("z16", [128, HEADS, TOPK])
        e16 = sb("e16", [128, HEADS, TOPK])
        nz = sb("nz", [128, HEADS])
        zsum = sb("zsum", [128, HEADS])
        rz = sb("rz", [128, HEADS])
        b1c = sb("b1c", [128, FC])
        meanc = sb("meanc", [128, FC])
        rb1 = sb("rb1", [128, 1])
        rw2 = sb("rw2", [128, 3])
        hidr = sb("hidr", [128, 1])
        rt = sb("rt", [1, 32])
        rb2 = sb("rb2", [1, 3])
        seli = sb("seli", [1, 2], I32)
        basei = sb("basei", [1, GROUPS], I32)
        flagi = sb("flagi", [1, 2], I32)
        maxdeg = sb("maxdeg", [1, 2])
        nmax = sb("nmax", [128, HEADS])
        psum_p = sb("psum_p", [128, 2, HEADS])
        psums = sb("psums", [128, HEADS])
        rinv = sb("rinv", [128, HEADS])
        ps = ctx.enter_context(nc.psum_tensor("ps", [128, 8, 512], FP32))

        xsf = xs[:, :, :].rearrange("p t n -> p (t n)")
        EG = EROWS * PER
        src_i = xsf[0:GROUPS, 0:EG].bitcast(I32)
        dst_i = xsf[0:GROUPS, 640:640 + EG].bitcast(I32)
        src_f = xsf[0:GROUPS, 1280:1280 + EG]
        rel_f = xsf[0:GROUPS, 1920:1920 + EG]
        bm = xsf[0:GROUPS, 2560:2562]
        src_c = xsf[0:EROWS, 2600:2600 + GROUPS * PER].rearrange("p (g j) -> p g j", j=PER)
        rel_c = xsf[0:EROWS, 2800:2800 + GROUPS * PER].rearrange("p (g j) -> p g j", j=PER)
        rem_c = xsf[0:EROWS, 3000:3000 + GROUPS * PER].rearrange("p (g j) -> p g j", j=PER)
        dst_f = xsf[0:GROUPS, 3200:3200 + EG]
        bmrow = xsf[0:1, 3900:3900 + 2 * GROUPS]
        cur = xsf[0:EROWS, 4000:4000 + PER]
        iota_w = xsf[0:EROWS, 4100:4100 + WIN]
        rem_t = xsf[0:EROWS, 4200:4200 + GROUPS * PER].rearrange("p (g j) -> p g j", j=PER)
        regBf = regB[:, :, :].rearrange("p t n -> p (t n)")
        half = 3136
        bf = regBf[0:EROWS, 0:half].bitcast(BF16)
        oh_src0 = bf[:, 0:PER * OH_W].rearrange("p (j n) -> p j n", j=PER)
        oh_dst = regBf[0:EROWS, half:half + 256].bitcast(BF16)[:, 0:2 * PER * WIN].rearrange(
            "p (b j w) -> p b j w", b=2, j=PER)
        iota_n = regBf[0:EROWS, 3500:3500 + 640].bitcast(FP16)[:, 0:OH_W]
        def words(t):
            return t.rearrange("p a b -> p (a b)")
        oh_src = [[oh_src0[:, j, :] for j in range(PER)],
                  [words((sim, sim, grid, grid, left)[j])[0:EROWS, 640 * (j % 2):640 * (j % 2) + 640].bitcast(BF16)[:, 0:OH_W]
                   for j in range(PER)]]
        rdeg = adj[:, TILES, 0:NODES]
        adj_hl = adj[:, 0:TILES, :].rearrange("p s n -> p (s n)").bitcast(FP16).rearrange(
            "p (m a i n) -> p m a i n", a=2, i=2, n=ADJ_W)

        def adj_h(k):
            return adj_hl[:, k // 2, 0, k % 2, :]

        def adj_l(k):
            return adj_hl[:, k // 2, 1, k % 2, :]
        xA = regA[:, :, :].rearrange("p t n -> p (t n)").bitcast(FP16).rearrange("p (t a n) -> p t a n", a=2, n=D)
        xB = regBf.bitcast(FP16).rearrange("p (t a n) -> p t a n", a=2, n=D)
        workf = work[:, :, :, :].rearrange("p a b c -> p (a b c)").bitcast(FP16)
        lows = [workf[:, NODES * k:NODES * (k + 1)] for k in range(9)] + [regBf[:, 0:NODES // 2].bitcast(FP16)]
        rounded = regBf[:, NODES // 2:NODES].bitcast(FP16)
        evens = regBf[:, NODES:NODES + 5 * NODES // 2].bitcast(FP16).rearrange("p (m n) -> p m n", n=NODES)
        keyb = wB[:, :, :].rearrange("p a b -> p (a b)").rearrange("p (c n) -> p c n", c=2)
        adjf = adj[:, :, :].rearrange("p a b -> p (a b)")
        key_h = adjf[:, 0:5000].bitcast(FP16).rearrange("p (h n) -> p h n", n=NODES)
        key_l = adjf[:, 5000:10000].bitcast(FP16).rearrange("p (h n) -> p h n", n=NODES)
        probs = [adjf[0:ROWS, 10000 + 1250 * i:11250 + 1250 * i] for i in range(2)]
        cross = adjf[:, 10000:12500].bitcast(FP16).rearrange("p (c n) -> p c n", n=NODES)
        attn = adjf[0:ROWS, 12500:13012]
        outs = adjf[0:ROWS, 13012:13524]
        vals = work[:, :, :, :].rearrange("p a b c -> p (a b c)")[0:ROWS, 0:TILES * D].rearrange(
            "p (t n) -> p t n", n=D)
        probT = [w[0:ROWS, :, :].rearrange("p a b -> p (a b)")[:, 0:NODES].rearrange("p (t n) -> p t n", n=ROWS)
                 for w in (wA, wB)]
        regAf = regA[:, :, :].rearrange("p t n -> p (t n)")
        query = regAf[:, 0:5000].bitcast(FP16).rearrange("p (h n) -> p h n", n=NODES)
        x4T = regBf[:, 0:FC * NODES].rearrange("p (c n) -> p c n", n=NODES)
        rw1 = wdT[:, :, 0:128]

        def cols(bank):
            return ps[:, bank, 0:FC * ROWS].rearrange("p (c n) -> p c n", n=ROWS)

        psAgg, psTr, psQ = cols(0), cols(1), cols(3)
        psOut = ps[0:ROWS, 2, :]
        psSim = ps[0:ROWS, 4:6, :]
        psHid = ps[:, 6, 0:2 * ROWS]
        psP = ps[:, 6, 256:256 + 2 * ROWS]
        psUp = ps[0:ROWS, 7, :]
        psAdj = [ps[:, i, 0:SLOTS * WIN].rearrange("p (s w) -> p s w", w=WIN) for i in range(2)]
        psE = ps[:, 2, :]
        psf = ps[0:ROWS, :, :].rearrange("p a b -> p (a b)")

        def psScore(i):
            return psf[:, NODES * i:NODES * (i + 1)]
        psTP = [ps[0:ROWS, 5 + i, :] for i in range(2)]
        psPV = ps[0:ROWS, 7, :]

        x_in = sem("x_in")
        edges_in = sem("edges_in")
        sage0_in = sem("sage0_in")
        bias_in = sem("bias_in")
        sage1_in = sem("sage1_in")
        adj_zero = sem("adj_zero")
        consts_set = sem("consts_set")
        columns_set = sem("columns_set")
        iotas_set = sem("iotas_set")
        edge_dve = sem("edge_dve")
        edge_cols = sem("edge_cols")
        adj_onehot = sem("adj_onehot")
        adj_counted = sem("adj_counted")
        adj_added = sem("adj_added")
        degrees_set = sem("degrees_set")
        inverse_set = sem("inverse_set")
        rem_dve = sem("rem_dve")
        rem_counted = sem("rem_counted")
        lows_kept = sem("lows_kept")
        evens_act = sem("evens_act")
        evens_dve = sem("evens_dve")
        adj_cast = sem("adj_cast")
        adj_ready = sem("adj_ready")
        ln1_act = sem("ln1_act")
        ln1_pool = sem("ln1_pool")
        ln1_done = sem("ln1_done")
        s0_low = sem("s0_low")
        s0_agg = sem("s0_agg")
        s0_aggT = sem("s0_aggT")
        s0_tr = sem("s0_tr")
        s0_trT = sem("s0_trT")
        s0_dense = sem("s0_dense")
        s0_out = sem("s0_out")
        peer_in = sem("peer_in")
        expert_in = sem("expert_in")
        keys_zero = sem("keys_zero")
        x_again = sem("x_again")
        s1_agg = sem("s1_agg")
        s1_aggT = sem("s1_aggT")
        s1_tr = sem("s1_tr")
        s1_trT = sem("s1_trT")
        s1_dense = sem("s1_dense")
        x1_dve = sem("x1_dve")
        x1_rstd = sem("x1_rstd")
        x1_norm = sem("x1_norm")
        f_tr = sem("f_tr")
        f_trT = sem("f_trT")
        f_q = sem("f_q")
        f_qT = sem("f_qT")
        f_sim = sem("f_sim")
        f_simS = sem("f_simS")
        f_hid = sem("f_hid")
        f_hidT = sem("f_hidT")
        p_top = sem("p_top")
        p_grid = sem("p_grid")
        p_pick = sem("p_pick")
        p_nz = sem("p_nz")
        p_exp = sem("p_exp")
        p_rz = sem("p_rz")
        p_weight = sem("p_weight")
        p_diag = sem("p_diag")
        b_p = sem("b_p")
        b_pS = sem("b_pS")
        b_up = sem("b_up")
        b_upS = sem("b_upS")
        g_pool = sem("g_pool")
        g_tanh = sem("g_tanh")
        g_done = sem("g_done")
        b_coef = sem("b_coef")
        x2_done = sem("x2_done")
        gin_in = sem("gin_in")
        b1_in = sem("b1_in")
        ln3_act = sem("ln3_act")
        ln3_pool = sem("ln3_pool")
        ln3_done = sem("ln3_done")
        n_agg = sem("n_agg")
        n_aggT = sem("n_aggT")
        n_u = sem("n_u")
        n_uT = sem("n_uT")
        n_dense = sem("n_dense")
        x3_done = sem("x3_done")
        x4_dve = sem("x4_dve")
        x4_rstd = sem("x4_rstd")
        x4_norm = sem("x4_norm")
        x4_tr = sem("x4_tr")
        x4_trT = sem("x4_trT")
        router_in = sem("router_in")
        r_mean = sem("r_mean")
        r_hid = sem("r_hid")
        r_hidS = sem("r_hidS")
        r_logit = sem("r_logit")
        r_dve = sem("r_dve")
        r_exp = sem("r_exp")
        r_sel = sem("r_sel")
        wk_in = sem("wk_in")
        wq_in = sem("wq_in")
        wv_in = sem("wv_in")
        wo_in = sem("wo_in")
        k_cols = sem("k_cols")
        k_k = sem("k_k")
        k_high = sem("k_high")
        k_low = sem("k_low")
        k_q = sem("k_q")
        q_high = sem("q_high")
        q_low = sem("q_low")
        k_v = sem("k_v")
        v_set = sem("v_set")
        crossed = sem("crossed")
        a_score = sem("a_score")
        a_max = sem("a_max")
        a_exp = sem("a_exp")
        a_tr = sem("a_tr")
        tr_act = sem("tr_act")
        tr_dve = sem("tr_dve")
        a_pv = sem("a_pv")
        a_inv = sem("a_inv")
        a_norm = sem("a_norm")
        stored = sem("stored")
        out_free = sem("out_free")
        FREED = (
            adj_added, s0_aggT, s0_tr, s0_trT, s0_dense, s0_out, s0_low, ln1_done, ln3_done, s1_aggT, s1_dense,
            x1_norm, f_tr, f_trT, f_q, f_qT, f_simS, f_hid, f_hidT, p_top, p_grid,
            p_exp, p_weight, p_diag, b_p, b_pS, b_up, b_upS, g_done, x2_done,
            n_aggT, x3_done, x4_tr, x4_trT, k_high, k_low, q_high, q_low, k_v, v_set, out_free)
        block = ctx.enter_context(nc.Block())

        def first(t):
            return isinstance(t, int) and t == 0

        def drain(t):
            return isinstance(t, int) and t == TILES

        def turns(t, h):
            kinds = [0, 1, 2] if (h >= 2 or not first(t)) and (h < 2 or not drain(t)) else []
            if h == 3 and not first(t):
                kinds.append("attnT")
            if h == 4 and not first(t):
                kinds.append("out")
            return kinds

        def taker(kind):
            return "act" if kind in (1, "attnT") else "dve"

        def tile_takers(t):
            return [taker(k) for h in range(HEADS) for k in turns(t, h)]

        def place(t, h, n):
            return sum(len(turns(t, h_)) for h_ in range(h)) + n

        def taken(t, who, until):
            before = 0 if first(t) else tile_takers(0).count(who) + (t - 1) * tile_takers(1).count(who)
            return before + tile_takers(t)[:max(until, 0)].count(who)

        def made(t, h, n):
            return taken(t, "act", place(t, h, n)) + taken(t, "dve", place(t, h, n)) + 1

        def there(t):
            return not isinstance(t, int) or 0 <= t < TILES

        def all_steps(engine, step):
            for t in range(3):
                step(t)
            with engine.Fori(3, TILES) as t:
                step(t)
            for t in range(TILES, TILES + 3):
                step(t)

        TOP_ORDER = [(0, 0), (0, 1), (1, 0), (1, 1), (2, 0), (2, 1), (3, 0), (4, 0), (3, 1), (4, 1)]
        PICK_ORDER = [(0, 0), (1, 0), (0, 1), (2, 0), (1, 1), (3, 0), (2, 1), (3, 1)]

        def topped(t, s, k):
            return 10 * t + TOP_ORDER.index((s, k)) + 1 + FREE

        def picked(t, s, k):
            return 8 * t + PICK_ORDER.index((s, k)) + 1

        def w_view(ap):
            return ap.rearrange("(f p) n -> p f n", p=128)

        @block.sync
        def _(sp):
            sp.dma_start(src_i, a["src"].rearrange("(g e) -> g e", e=EG)).then_inc(edges_in, 16)
            sp.dma_start(dst_i, a["dst"].rearrange("(g e) -> g e", e=EG)).then_inc(edges_in, 16)
            sp.dma_start(regA[0:ROWS, :, :], a["x"].rearrange("(t p) n -> p t n", p=ROWS)).then_inc(x_in, 16)
            for freed in FREED:
                sp.sem_inc(freed, FREE)
            sp.dma_start(wA[:, :, :], w_view(a["Wl0T"])).then_inc(sage0_in, 16)
            sp.dma_start(wB[:, :, :], w_view(a["Wr0T"])).then_inc(sage0_in, 16)
            for i, n in enumerate(("bl0", "bl1", "b2")):
                sp.dma_start(biases[32 * i:32 * i + 1, :], a[n].rearrange("(o n) -> o n", o=1)).then_inc(bias_in, 16)
            sp.dma_start(wC[:, :, :], w_view(a["Wl1T"])).then_inc(sage1_in, 16)
            sp.dma_start(wD[:, :, :], w_view(a["Wr1T"])).then_inc(sage1_in, 16)
            sp.dma_start(wdT[:, :, :], w_view(a["wdT"][:, 0:GRID])).then_inc(expert_in, 16)
            sp.dma_start(wu[:, :, :], a["wu"][0:GRID, :].rearrange("(e p) n -> p e n", p=128)).then_inc(expert_in, 16)
            sp.dma_start(b1c[:, :], a["b1c"]).then_inc(b1_in, 16)
            sp.dma_start(rb1[:, :], a["rb1"].rearrange("(p o) -> p o", o=1)).then_inc(b1_in, 16)
            sp.dma_start(rw2[:, :], a["rw2"]).then_inc(b1_in, 16)
            sp.dma_start(rb2[:, :], a["rb2"].rearrange("(o n) -> o n", o=1)).then_inc(b1_in, 16)
            sp.wait_ge(s0_dense, TILES + FREE)
            sp.dma_start(wA[:, :, :], w_view(a["wq"])).then_inc(peer_in, 16)
            sp.wait_ge(keys_zero, 1)
            for h in range(HEADS):
                b = h % 4
                sp.dma_start(keyb[32 * b:32 * b + 32, h // 4, KEYS * b:KEYS * b + KEYS],
                             a["keysT"][0, h]).then_inc(peer_in, 16)
            with sp.Fori(0, TILES) as t:
                sp.wait_ge(x1_norm, t + FREE)
                sp.dma_start(xres[0:ROWS, :], a["x"].rearrange("(t p) n -> p t n", p=ROWS)[:, ds(t, 1), :]
                             ).then_inc(x_again, 16)
            sp.wait_ge(s1_dense, TILES + FREE)
            sp.dma_start(wC[:, :, :], w_view(a["W1"])).then_inc(gin_in, 16)
            sp.dma_start(wD[:, :, :], w_view(a["W2"])).then_inc(gin_in, 16)
            sp.wait_ge(f_hid, TILES + FREE)
            sp.dma_start(rw1, w_view(a["rw1"])).then_inc(router_in, 16)
            sp.wait_ge(r_sel, 1)
            sel = sp.value_load(seli[0:1, 0:1], min_val=0, max_val=2)
            for i, n_kv in enumerate(KV_OPTS):
                reps = HEADS // n_kv
                with sp.If(sel == i):
                    def repeated(w, n, arrived):
                        for f in range(FC):
                            dst = w[:, f, :].rearrange("p (k r d) -> p k r d", r=reps, d=DHEAD)
                            rows_ = w_view(a[f"{n}{i}"])[:, f, :].rearrange("p (k d) -> p k d", d=DHEAD)
                            sp.dma_start(dst, rows_.unsqueeze(2).broadcast_to([128, n_kv, reps, DHEAD])
                                         ).then_inc(arrived, 16)
                    repeated(wA, "wk", wk_in)
                    sp.wait_ge(n_dense, TILES)
                    sp.dma_start(wC[:, :, :], w_view(a[f"wq{i}"])).then_inc(wq_in, 16)
                    repeated(wB, "wv", wv_in)
                    sp.dma_start(wD[:, :, :], w_view(a[f"wo{i}"])).then_inc(wo_in, 16)
            for part in range(2):
                n = TILES // 2 * (part + 1)
                at = slice(NODES // 2 * part, NODES // 2 * (part + 1))
                sp.wait_ge(k_high, n + FREE)
                sp.wait_ge(k_low, n + FREE)
                for k in (key_h, key_l):
                    kk = k.rearrange("p (c e) n -> p e c n", e=2)
                    sp.dma_start(kk[64:128, 0, :, at], kk[0:64, 0, :, at]).then_inc(crossed, 16)
                    sp.dma_start(kk[0:64, 1, :, at], kk[64:128, 1, :, at]).then_inc(crossed, 16)
                sp.wait_ge(q_high, n + FREE)
                sp.wait_ge(q_low, n + FREE)
                qq = query.rearrange("p (c e) n -> p e c n", e=2)
                sp.dma_start(qq[64:128, 0, :, at], cross[0:64, :, at]).then_inc(crossed, 16)
                sp.dma_start(qq[0:64, 1, :, at], cross[64:128, :, at]).then_inc(crossed, 16)
            with sp.Fori(0, TILES - 1) as t:
                sp.wait_ge(tr_dve, taken(t + 1, "dve", place(1, 4, 4)))
                sp.dma_start(out.rearrange("(t p) n -> p t n", p=ROWS)[:, ds(t, 1), :], outs).then_inc(stored, 16)
                sp.wait_ge(stored, 16 * t + 16)
                sp.sem_inc(out_free, 1)
            sp.wait_ge(tr_dve, taken(TILES, "dve", place(TILES, 4, 1)))
            sp.dma_start(out[NODES - ROWS:NODES, :], outs).then_inc(stored, 16)
            sp.wait_ge(stored, 16 * TILES)

        @block.gpsimd
        def _(g):
            nc.gpsimd.memset(ident[:, :], 0.0).then_inc(consts_set, 1)
            nc.gpsimd.memset(nhalf[:, :], -0.5).then_inc(consts_set, 1)
            nc.gpsimd.memset(ones_c[:, :], 1.0).then_inc(columns_set, 1)
            nc.gpsimd.memset(zero_c[:, :], 0.0).then_inc(columns_set, 1)
            nc.gpsimd.memset(ones_b[:, :], 1.0).then_inc(consts_set, 1)
            nc.gpsimd.memset(ones_r[:, :], 1.0).then_inc(consts_set, 1)
            g.wait_ge(consts_set, 4)
            nc.gpsimd.affine_select(out=ident[:, :], in_=ident[:, :], compare_op=ALU.not_equal, fill=1.0, base=0,
                                    pattern=[[-1, 128]], channel_multiplier=1).then_inc(consts_set, 1)
            g.wait_ge(consts_set, 5)
            nc.gpsimd.affine_select(out=ident_h[:, :], in_=ident[:, :], compare_op=ALU.not_equal, fill=1.0, base=0,
                                    pattern=[[-1, 128]], channel_multiplier=1).then_inc(consts_set, 1)
            nc.gpsimd.iota(iota_n, pattern=[[1, OH_W]], base=0, channel_multiplier=0,
                           allow_small_or_imprecise_dtypes=True).then_inc(iotas_set, 1)
            nc.gpsimd.iota(iota_w, pattern=[[1, WIN]], base=0, channel_multiplier=0,
                           allow_small_or_imprecise_dtypes=True).then_inc(iotas_set, 1)
            nc.gpsimd.memset(adj[:, 2:SLOTS, :], 0.0).then_inc(adj_zero, 1)

            def inv_std(n, dve_sem, dve_at, sem_out, b):
                g.wait_ge(dve_sem, dve_at)
                g.nop(nofuse=True)
                nc.gpsimd.tensor_scalar(rstd[0:ROWS, b:b + 1], mv[0:ROWS, b, 1:2], LN_EPS, None, ALU.add
                                        ).then_inc(sem_out, 1)
                g.wait_ge(sem_out, n + 1)
                nc.gpsimd.tensor_tensor(rstd[0:ROWS, b:b + 1], rstd[0:ROWS, b:b + 1], nhalf[0:ROWS, 0:1], ALU.pow
                                        ).then_inc(sem_out, 1)

            def inv_std_low(t, x, act_sem, pool_sem, done):
                g.wait_ge(act_sem, 6 * t + 3)
                g.nop(nofuse=True)
                nc.gpsimd.tensor_scalar(ln_s[0:ROWS, 3:4], ln_s[0:ROWS, 2:3], 1.0 / D, LN_EPS, ALU.mult, ALU.add
                                        ).then_inc(pool_sem, 1)
                g.wait_ge(pool_sem, 2 * t + 1)
                nc.gpsimd.tensor_tensor(ln_s[0:ROWS, 3:4], ln_s[0:ROWS, 3:4], nhalf[0:ROWS, 0:1], ALU.pow
                                        ).then_inc(pool_sem, 1)
                g.wait_ge(act_sem, 6 * t + 6)
                nc.gpsimd.tensor_tensor(x[0:ROWS, ds(t, 1), 1, :], norm_x[0:ROWS, :].unsqueeze(1),
                                        x[0:ROWS, ds(t, 1), 0, :], ALU.subtract).then_inc(done, 1)

            with g.Fori(0, TILES) as t:
                inv_std_low(t, xA, ln1_act, ln1_pool, ln1_done)

            g.wait_ge(s0_dense, TILES + FREE)
            nc.gpsimd.memset(wB[:, :, :], 0.0).then_inc(keys_zero, 1)

            def pair_scores(t, k):
                hs = slice(4 * k, 4 * k + 4)
                g.wait_ge(p_top, topped(t, 4, k))
                if k == 0:
                    g.wait_ge(p_weight, 2 * t + FREE)
                g.nop(nofuse=True)
                nc.gpsimd.tensor_copy(i16f[0:ROWS, hs, :], i16[0:ROWS, hs, :]).then_inc(p_grid, 1)
                g.wait_ge(p_grid, 4 * t + 2 * k + 1 + FREE)
                o = grid[0:ROWS, hs, :].rearrange("p h (a b) -> p h a b", b=TOPK)
                nc.gpsimd.tensor_tensor(o, v16[0:ROWS, hs, :].unsqueeze(3).broadcast_to([ROWS, 4, TOPK, TOPK]),
                                        i16f[0:ROWS, hs, :].unsqueeze(2).broadcast_to([ROWS, 4, TOPK, TOPK]),
                                        ALU.add).then_inc(p_grid, 1)

            def neg_max(t, k):
                hs = slice(4 * k, 4 * k + 4)
                g.wait_ge(p_pick, picked(t, 0, k))
                g.nop(nofuse=True)
                nc.gpsimd.tensor_scalar(nz[0:ROWS, hs], z16[0:ROWS, hs, 0], -1.0, None, ALU.mult).then_inc(p_nz, 1)

            def gelu_tile(t):
                g.wait_ge(f_hidT, t + 1 + FREE)
                nc.gpsimd.tensor_tensor(gt1[:, :], hidT[:, :], hidT[:, :], ALU.mult).then_inc(g_pool, 1)
                g.wait_ge(g_pool, 4 * t + 1)
                g.nop(nofuse=True)
                nc.gpsimd.tensor_scalar(gt1[:, :], gt1[:, :], GELU_A, 1.0, ALU.mult, ALU.add).then_inc(g_pool, 1)
                g.wait_ge(g_pool, 4 * t + 2)
                nc.gpsimd.tensor_tensor(gt1[:, :], gt1[:, :], hidT[:, :], ALU.mult).then_inc(g_pool, 1)
                g.wait_ge(g_tanh, t + 1)
                g.nop(nofuse=True)
                nc.gpsimd.tensor_scalar(gt1[:, :], gt1[:, :], 1.0, 0.5, ALU.add, ALU.mult).then_inc(g_pool, 1)

            def gelu_end(t):
                if not first(t):
                    g.wait_ge(b_coef, t)
                g.wait_ge(g_pool, 4 * t + 4)
                nc.gpsimd.tensor_tensor(gelu[:, :], gt1[:, :], hidT[:, :], ALU.mult).then_inc(g_done, 1)

            def coefficients(t):
                g.wait_ge(b_pS, t + 1 + FREE)
                g.wait_ge(g_done, t + 1 + FREE)
                nc.gpsimd.tensor_tensor(coef[:, :], coef[:, :], gelu[:, :], ALU.mult).then_inc(b_coef, 1)

            def residual2(t):
                g.wait_ge(b_upS, t + 1 + FREE)
                nc.gpsimd.tensor_tensor(xs[0:ROWS, ds(t, 1), :], xs[0:ROWS, ds(t, 1), :], ups[0:ROWS, :].unsqueeze(1),
                                        ALU.add).then_inc(x2_done, 1)

            def peer_step(t):
                if there(t - 2):
                    pair_scores(t - 2, 0)
                if there(t - 3):
                    coefficients(t - 3)
                if there(t - 2):
                    pair_scores(t - 2, 1)
                    gelu_end(t - 2)
                    neg_max(t - 2, 0)
                    neg_max(t - 2, 1)
                if there(t - 3):
                    residual2(t - 3)
                if there(t - 1):
                    gelu_tile(t - 1)
                if there(t - 3):
                    inv_std_low(t - 3, xA, ln3_act, ln3_pool, ln3_done)
                if there(t):
                    inv_std(2 * t, x1_dve, 3 * t + 3, x1_rstd, 0)

            all_steps(g, peer_step)

            with g.Fori(0, TILES) as t:
                inv_std(2 * t, x4_dve, 2 * t + 2, x4_rstd, 0)

            g.wait_ge(x4_trT, TILES + FREE)
            with g.Fori(0, TILES) as t:
                g.wait_ge(k_v, t + FREE)
                g.nop(nofuse=True)
                nc.gpsimd.tensor_copy(colB[:, :, :], x4T[:, :, ds(t * ROWS, ROWS)]).then_inc(k_cols, 1)

        @block.scalar
        def _(act):
            def norm_high(t, x, high, sem_, pool_sem, done):
                n = 6 * t
                rows_ = x[0:ROWS, ds(t, 1), :]
                o = norm_x[0:ROWS, :].unsqueeze(1)
                if x is xs:
                    act.wait_ge(x2_done, t + 1 + FREE)
                act.wait_ge(done, t + FREE)
                act.nop(nofuse=True)
                nc.scalar.activation(o, rows_, ACT.Copy, accum_out=ln_s[0:ROWS, 0:1]).then_inc(sem_, 1)
                act.wait_ge(sem_, n + 1)
                nc.scalar.mul(ln_s[0:ROWS, 1:2], ln_s[0:ROWS, 0:1], -1.0 / D).then_inc(sem_, 1)
                act.wait_ge(sem_, n + 2)
                act.nop(nofuse=True)
                nc.scalar.activation(o, rows_, ACT.Square, bias=ln_s[0:ROWS, 1:2], accum_out=ln_s[0:ROWS, 2:3]
                                     ).then_inc(sem_, 1)
                act.wait_ge(pool_sem, 2 * t + 2)
                act.nop(nofuse=True)
                nc.scalar.activation(o, rows_, ACT.Identity, bias=ln_s[0:ROWS, 1:2]).then_inc(sem_, 1)
                act.wait_ge(sem_, n + 4)
                act.nop(nofuse=True)
                nc.scalar.mul(o, o, ln_s[0:ROWS, 3:4]).then_inc(sem_, 1)
                act.wait_ge(sem_, n + 5)
                nc.scalar.copy(high[0:ROWS, ds(t, 1), 0, :], o).then_inc(sem_, 1)

            act.wait_ge(x_in, 16)
            with act.Fori(0, TILES) as t:
                norm_high(t, regA, xA, ln1_act, ln1_pool, ln1_done)
            act.wait_ge(lows_kept, 1)
            for m in range(2):
                last = nc.scalar.copy(evens[:, m, :], adj[:, 2 * m, 0:NODES])
            last.then_inc(evens_act, 1)
            act.wait_ge(evens_act, 1)
            for m in range(2):
                nc.scalar.copy(adj_h(2 * m + 1)[:, 0:NODES], adj[:, 2 * m + 1, 0:NODES])
                last = nc.scalar.copy(adj_h(2 * m)[:, 0:NODES], evens[:, m, :])
            last.then_inc(adj_cast, 1)

            with act.Fori(0, TILES) as t:
                act.wait_ge(s0_tr, t + 1 + FREE)
                act.wait_ge(s0_dense, t + FREE)
                nc.scalar.copy(colB[:, :, :], psTr).then_inc(s0_trT, 1)
                act.wait_ge(s0_dense, t + 1 + FREE)
                nc.scalar.activation(xB[0:ROWS, ds(t, 1), 0, :], psOut.unsqueeze(1), ACT.Relu).then_inc(s0_out, 1)

            def rows_T(t):
                act.wait_ge(s1_tr, t + 1)
                act.wait_ge(f_q, t + FREE)
                nc.scalar.copy(colB[:, :, :], psTr).then_inc(s1_trT, 1)

            def front(t):
                act.wait_ge(f_tr, t + 1 + FREE)
                nc.scalar.copy(colB[:, :, :], psTr).then_inc(f_trT, 1)

            def queries_S(t):
                act.wait_ge(f_q, t + 1 + FREE)
                nc.scalar.mul(colA[:, :, :], psQ, BN_SCALE).then_inc(f_qT, 1)

            def sims(t):
                for c in range(2):
                    act.wait_ge(f_sim, 2 * t + c + 1)
                    if c == 0:
                        act.wait_ge(p_top, 10 * t + FREE)
                    nc.scalar.copy(sim[0:ROWS, 4 * c:4 * c + 4, :].rearrange("p h k -> p (h k)"),
                                   psSim.rearrange("p a b -> p (a b)")).then_inc(f_simS, 1)

            def hidden(t):
                act.wait_ge(f_hid, t + 1 + FREE)
                act.wait_ge(g_done, t + FREE)
                nc.scalar.copy(hidT[:, :], psHid).then_inc(f_hidT, 1)

            def tanh(t):
                act.wait_ge(g_pool, 4 * t + 3)
                nc.scalar.activation(gt1[:, :], gt1[:, :], ACT.Tanh, scale=GELU_C).then_inc(g_tanh, 1)

            def exps(t, k):
                act.wait_ge(p_nz, 2 * t + k + 1)
                act.wait_ge(p_pick, picked(t, 1, k))
                for h in range(4 * k, 4 * k + 4):
                    last = nc.scalar.activation(grid[0:ROWS, h, :], grid[0:ROWS, h, :], ACT.Exp,
                                                bias=nz[0:ROWS, h:h + 1])
                act.wait_ge(p_pick, picked(t, 2, k))
                for h in range(4 * k, 4 * k + 4):
                    last = nc.scalar.activation(e16[0:ROWS, h, :], z16[0:ROWS, h, :], ACT.Exp,
                                                bias=nz[0:ROWS, h:h + 1], accum_out=zsum[0:ROWS, h:h + 1])
                last.then_inc(p_exp, 1)

            def diagonals(t):
                act.wait_ge(p_rz, t + 1)
                act.wait_ge(b_p, t + FREE)
                act.nop(nofuse=True)
                for h in range(HEADS):
                    last = nc.scalar.mul(diag[0:ROWS, h, :], ident[0:ROWS, 0:ROWS], rz[0:ROWS, h:h + 1])
                last.then_inc(p_diag, 1)

            def weights_S(t):
                act.wait_ge(b_p, t + 1 + FREE)
                act.wait_ge(b_up, t + FREE)
                nc.scalar.copy(coef[:, :], psP).then_inc(b_pS, 1)

            def up_S(t):
                act.wait_ge(b_up, t + 1 + FREE)
                act.wait_ge(x2_done, t + FREE)
                nc.scalar.copy(ups[0:ROWS, :], psUp).then_inc(b_upS, 1)

            def peer_step(t):
                if there(t - 1):
                    front(t - 1)
                    queries_S(t - 1)
                if there(t - 3):
                    up_S(t - 3)
                if there(t - 1):
                    sims(t - 1)
                    hidden(t - 1)
                if there(t):
                    rows_T(t)
                if there(t - 2):
                    exps(t - 2, 0)
                    exps(t - 2, 1)
                if there(t - 1):
                    tanh(t - 1)
                if there(t - 2):
                    diagonals(t - 2)
                if there(t - 3):
                    norm_high(t - 3, xs, xA, ln3_act, ln3_pool, ln3_done)
                if there(t - 2):
                    weights_S(t - 2)

            all_steps(act, peer_step)

            def x4_T(t):
                act.wait_ge(x4_tr, t + 1 + FREE)
                nc.scalar.copy(x4T[:, :, ds(t * ROWS, ROWS)], psTr).then_inc(x4_trT, 1)

            def gin(t):
                act.wait_ge(n_agg, t + 1)
                nc.scalar.copy(colA[:, :, :], psAgg).then_inc(n_aggT, 1)
                act.wait_ge(n_u, t + 1)
                for c in range(FC):
                    last = nc.scalar.activation(colB[:, c, :], psQ[:, c, :], ACT.Relu, bias=b1c[:, c:c + 1])
                last.then_inc(n_uT, 1)

            act.wait_ge(b1_in, 64)
            gin(0)
            with act.Fori(1, TILES) as t:
                gin(t)
                x4_T(t - 1)
            x4_T(TILES - 1)

            act.wait_ge(r_hid, 1)
            nc.scalar.activation(hidr[:, :], psE[:, 0:1], ACT.Relu, bias=rb1[:, 0:1]).then_inc(r_hidS, 1)
            act.wait_ge(r_dve, 2)
            nc.scalar.activation(rt[0:1, 8:11], rt[0:1, 0:3], ACT.Exp, bias=rt[0:1, 4:5],
                                 accum_out=rt[0:1, 12:13]).then_inc(r_exp, 1)

            kk = key_h.rearrange("p (c e) n -> p e c n", e=2)
            qq = query.rearrange("p (c e) n -> p e c n", e=2)
            with act.Fori(0, TILES) as t:
                at = ds(t * ROWS, ROWS)
                act.wait_ge(k_k, t + 1)
                nc.scalar.copy(kk[0:64, 0, :, at], psQ[0:64, :, :])
                nc.scalar.copy(kk[64:128, 1, :, at], psQ[64:128, :, :]).then_inc(k_high, 1)
                act.wait_ge(k_q, t + 1)
                nc.scalar.mul(qq[0:64, 0, :, at], psTr[0:64, :, :], DHEAD ** -0.5)
                nc.scalar.mul(cross[64:128, :, at], psTr[64:128, :, :], DHEAD ** -0.5).then_inc(q_high, 1)
                act.wait_ge(k_v, t + 1 + FREE)
                nc.scalar.copy(vals[:, ds(t, 1), :], psOut.unsqueeze(1)).then_inc(v_set, 1)

            def exp_head(t, h, step_t, step_h):
                n = HEADS * t + h
                if not (first(step_t) and step_h < 3):
                    act.wait_ge(a_tr, sum(taken(step_t, who, place(step_t, step_h, 0)) for who in ("act", "dve")))
                act.wait_ge(a_max, n + 1)
                if h == 0 and not first(t):
                    act.wait_ge(a_inv, 2 * t - 1)
                for i, (lo, hi) in enumerate((SC[h % 2][2], OWN[h % 2])):
                    nc.scalar.activation(probs[h % 2][:, lo:hi], psScore(h % 2)[:, lo:hi], ACT.Exp,
                                         bias=nmax[0:ROWS, h:h + 1], accum_out=psum_p[0:ROWS, i, h:h + 1]
                                         ).then_inc(a_exp, 1)

            def act_turn(t, h, n, kind):
                if taker(kind) != "act":
                    return
                act.wait_ge(a_tr, made(t, h, n))
                bank = place(t, h, n) % 2
                if kind == "attnT":
                    nc.scalar.copy(colB[:, :, :], cols(5 + bank)).then_inc(tr_act, 1)
                    return
                if not (first(t) and h < 4):
                    act.wait_ge(a_pv, HEADS * t + h - 3)
                lo, hi = TB[kind]
                nc.scalar.copy(probT[h % 2][:, lo:hi, :],
                               psTP[bank][:, 0:(hi - lo) * ROWS].rearrange("p (t n) -> p t n", n=ROWS)
                               ).then_inc(tr_act, 1)

            def act_step(t, h):
                kinds = turns(t, h)
                if not first(t) and h == 0:
                    exp_head(t - 1, HEADS - 1, t, h)
                elif h >= 1 and not drain(t):
                    exp_head(t, h - 1, t, h)
                for n, kind in enumerate(kinds):
                    act_turn(t, h, n, kind)

            for h in range(HEADS):
                act_step(0, h)
            with act.Fori(1, TILES) as t:
                for h in range(HEADS):
                    act_step(t, h)
            for h in range(HEADS):
                act_step(TILES, h)

        @block.vector
        def _(v):
            v.wait_ge(edges_in, 32)
            nc.vector.tensor_copy(src_f, src_i).then_inc(edge_dve, 1)
            nc.vector.tensor_copy(dst_f, dst_i).then_inc(edge_dve, 1)
            v.wait_ge(edge_dve, 2)
            nc.vector.tensor_reduce(bm[:, 0:1], dst_f, X, ALU.min).then_inc(edge_dve, 1)
            v.wait_ge(edge_dve, 3)
            nc.vector.tensor_scalar(rel_f, dst_f, bm[:, 0:1], None, ALU.subtract).then_inc(edge_dve, 1)
            v.wait_ge(edge_dve, 4)
            nc.vector.tensor_reduce(bm[:, 1:2], rel_f, X, ALU.max).then_inc(edge_dve, 1)
            nc.vector.memset(adj[:, 0:2, :], 0.0).then_inc(adj_zero, 1)
            v.wait_ge(edge_cols, 1)
            nc.vector.tensor_copy(src_c.rearrange("p g j -> p j g"),
                                  psE[0:EROWS, 0:PER * GROUPS].rearrange("p (j g) -> p j g", j=PER)).then_inc(edge_dve, 1)
            nc.vector.tensor_copy(rel_c.rearrange("p g j -> p j g"),
                                  psE[0:EROWS, PER * GROUPS:2 * PER * GROUPS].rearrange("p (j g) -> p j g", j=PER)
                                  ).then_inc(edge_dve, 1)
            nc.vector.tensor_copy(bmrow, psE[0:1, 2 * PER * GROUPS:2 * (PER + 1) * GROUPS]).then_inc(edge_dve, 1)
            v.wait_ge(edge_dve, 8)
            nc.vector.tensor_copy(basei[:, :], bmrow[:, 0:GROUPS]).then_inc(edge_dve, 1)
            nc.vector.tensor_scalar(bmrow[:, GROUPS:2 * GROUPS], bmrow[:, GROUPS:2 * GROUPS], float(WIN), None,
                                    ALU.is_ge).then_inc(edge_dve, 1)
            v.wait_ge(edge_dve, 10)
            nc.vector.tensor_reduce(flagi[:, 0:1], bmrow[:, GROUPS:2 * GROUPS], X, ALU.max).then_inc(edge_dve, 1)

            v.wait_ge(iotas_set, 2)
            v.wait_ge(edge_dve, 11)

            def onehots(g_, b):
                for j in range(PER):
                    nc.vector.tensor_scalar(oh_src[b][j].unsqueeze(1), iota_n.unsqueeze(1), src_c[:, ds(g_, 1), j], None,
                                            ALU.is_equal)
                nc.vector.tensor_tensor(oh_dst[:, b, :, :], iota_w.unsqueeze(1).broadcast_to([EROWS, PER, WIN]),
                                        rel_c[:, ds(g_, 1), :].rearrange("p g j -> p (g j)").unsqueeze(2).broadcast_to([EROWS, PER, WIN]),
                                        ALU.is_equal).then_inc(adj_onehot, 1)

            def add_window(n, g_, b):
                v.wait_ge(adj_counted, n + 1)
                v.wait_ge(adj_added, n + FREE)
                first = v.value_load(basei[0:1, ds(g_, 1)], min_val=0, max_val=NODES - 1)
                w = adj[:, :, ds(first, WIN)]
                nc.vector.tensor_tensor(w, w, psAdj[b], ALU.add).then_inc(adj_added, 1)

            onehots(0, 0)
            onehots(1, 1)
            v.wait_ge(adj_zero, 2)
            with v.Fori(0, GROUPS // 2 - 1) as u:
                for b in range(2):
                    add_window(2 * u + b, 2 * u + b, b)
                    onehots(2 * u + b + 2, b)
            add_window(GROUPS - 2, GROUPS - 2, 0)
            add_window(GROUPS - 1, GROUPS - 1, 1)

            v.wait_ge(adj_added, GROUPS + FREE)
            spread = v.value_load(flagi[0:1, 0:1], min_val=0, max_val=1)
            with v.If(spread == 1):
                v.wait_ge(rem_counted, 1)
                nc.vector.tensor_tensor(rem_c.rearrange("p g j -> p j g"), rel_c.rearrange("p g j -> p j g"),
                                        psE[0:EROWS, 0:GROUPS].unsqueeze(1).broadcast_to([EROWS, PER, GROUPS]),
                                        ALU.add).then_inc(rem_dve, 1)
                nc.vector.tensor_scalar(rem_t, rel_c, float(WIN), -float(4 * NODES), ALU.is_lt, ALU.mult
                                        ).then_inc(rem_dve, 1)
                v.wait_ge(rem_dve, 2)
                nc.vector.tensor_tensor(rem_c, rem_c, rem_t, ALU.add).then_inc(rem_dve, 1)
                v.wait_ge(rem_dve, 3)
                with v.Fori(0, GROUPS) as gi:
                    v.wait_ge(rem_dve, 3 + gi * (3 * WINDOWS + 1))
                    for j in range(PER):
                        nc.vector.tensor_scalar(oh_src[0][j].unsqueeze(1), iota_n.unsqueeze(1), src_c[:, ds(gi, 1), j],
                                                None, ALU.is_equal)
                    nc.vector.tensor_copy(cur, rem_c[:, ds(gi, 1), :].rearrange("p g j -> p (g j)")
                                          ).then_inc(rem_dve, 1)
                    with v.Fori(0, WINDOWS) as wi:
                        n = 3 + gi * (3 * WINDOWS + 1) + 1 + 3 * wi
                        v.wait_ge(rem_dve, n)
                        nc.vector.tensor_tensor(oh_dst[:, 0, :, :], iota_w.unsqueeze(1).broadcast_to([EROWS, PER, WIN]),
                                                cur.unsqueeze(2).broadcast_to([EROWS, PER, WIN]),
                                                ALU.is_equal).then_inc(rem_dve, 1)
                        v.wait_ge(rem_dve, n + 1)
                        nc.vector.tensor_scalar(cur, cur, float(WIN), None, ALU.subtract).then_inc(rem_dve, 1)
                        v.wait_ge(rem_counted, gi * WINDOWS + wi + 2)
                        w = adj[:, :, ds(wi * WIN, WIN)]
                        nc.vector.tensor_tensor(w, w, psAdj[0], ALU.add).then_inc(rem_dve, 1)
                v.wait_ge(rem_dve, 3 + GROUPS * (3 * WINDOWS + 1))
            nc.vector.tensor_scalar(rdeg, rdeg, 1.0, None, ALU.max).then_inc(degrees_set, 1)
            v.wait_ge(degrees_set, 1)
            nc.vector.tensor_reduce(maxdeg[0:1, 0:1], adj[0:1, TILES, 0:NODES], X, ALU.max).then_inc(degrees_set, 1)
            v.wait_ge(degrees_set, 2)
            nc.vector.tensor_scalar(flagi[0:1, 1:2], maxdeg[0:1, 0:1], float(HALF_EXACT), None, ALU.is_gt
                                    ).then_inc(degrees_set, 1)
            v.wait_ge(degrees_set, 3)
            large = v.value_load(flagi[0:1, 1:2], min_val=0, max_val=1)
            with v.If(large == 1):
                for k in range(TILES):
                    v.wait_ge(degrees_set, 3 + 2 * k)
                    nc.vector.tensor_copy(rounded, adj[:, k, 0:NODES]).then_inc(degrees_set, 1)
                    v.wait_ge(degrees_set, 4 + 2 * k)
                    nc.vector.tensor_tensor(lows[k], adj[:, k, 0:NODES], rounded, ALU.subtract).then_inc(degrees_set, 1)
                v.wait_ge(degrees_set, 3 + 2 * TILES)
            v.sem_inc(lows_kept, 1)
            for m in range(2, TILES // 2):
                last = nc.vector.tensor_copy(evens[:, m, :], adj[:, 2 * m, 0:NODES])
            last.then_inc(evens_dve, 1)
            v.wait_ge(evens_dve, 1)
            for m in range(2, TILES // 2):
                nc.vector.tensor_copy(adj_h(2 * m + 1)[:, 0:NODES], adj[:, 2 * m + 1, 0:NODES])
                last = nc.vector.tensor_copy(adj_h(2 * m)[:, 0:NODES], evens[:, m, :])
            last.then_inc(adj_cast, 1)
            with v.If(large == 1):
                v.wait_ge(adj_cast, 2)
                for k in range(TILES):
                    last = nc.vector.tensor_copy(adj_l(k)[:, 0:NODES], lows[k])
                last.then_inc(adj_cast, 1)
                v.wait_ge(adj_cast, 3)
            v.wait_ge(adj_cast, 2)
            v.sem_inc(adj_ready, 1)
            nc.vector.reciprocal(rdeg, rdeg).then_inc(inverse_set, 1)

            v.wait_ge(inverse_set, 1)

            def mean_T(t, agg, dense, outsem):
                v.wait_ge(agg, t + 1)
                v.wait_ge(dense, t + FREE)
                nc.vector.tensor_tensor(colA[:, :, :], psAgg,
                                        adj[:, TILES:TILES + 1, ds(t * ROWS, ROWS)].broadcast_to([128, FC, ROWS]),
                                        ALU.mult).then_inc(outsem, 1)

            with v.Fori(0, TILES) as t:
                mean_T(t, s0_agg, s0_dense, s0_aggT)
                v.wait_ge(s0_out, t + 1 + FREE)
                nc.vector.scalar_tensor_tensor(xB[0:ROWS, ds(t, 1), 1, :], psOut.unsqueeze(1), 0.0,
                                               xB[0:ROWS, ds(t, 1), 0, :], ALU.max, ALU.subtract).then_inc(s0_low, 1)

            def mean_T2(t):
                v.wait_ge(f_hid, t + FREE)
                mean_T(t, s1_agg, s1_dense, s1_aggT)

            def x1_piece(t, piece):
                if piece == 0:
                    v.wait_ge(s1_dense, t + 1 + FREE)
                    v.wait_ge(x_again, 16 * t + 16)
                    nc.vector.scalar_tensor_tensor(xs[0:ROWS, ds(t, 1), :], psOut.unsqueeze(1), 0.0,
                                                   xres[0:ROWS, :].unsqueeze(1), ALU.max, ALU.add).then_inc(x1_dve, 1)
                elif piece == 1:
                    v.wait_ge(x1_dve, 3 * t + 1)
                    v.nop(nofuse=True)
                    nc.vector.bn_stats(st[0:ROWS, 0, :], xs[0:ROWS, ds(t, 1), :]).then_inc(x1_dve, 1)
                elif piece == 2:
                    v.wait_ge(x1_dve, 3 * t + 2)
                    v.nop(nofuse=True)
                    nc.vector.bn_aggr(mv[0:ROWS, 0, :], st[0:ROWS, 0, :]).then_inc(x1_dve, 1)
                else:
                    v.wait_ge(x1_rstd, 2 * t + 2)
                    v.wait_ge(f_tr, t + FREE)
                    nc.vector.tensor_scalar(row[0:ROWS, :].unsqueeze(1), xs[0:ROWS, ds(t, 1), :], mv[0:ROWS, 0, 0:1],
                                            rstd[0:ROWS, 0:1], ALU.subtract, ALU.mult).then_inc(x1_norm, 1)

            def top_stage(t, s, k):
                hs = range(4 * k, 4 * k + 4)
                if s == 0:
                    v.wait_ge(f_simS, 2 * t + k + 1 + FREE)
                    v.wait_ge(p_grid, 4 * t + FREE)
                else:
                    v.wait_ge(p_top, topped(t, s - 1, k))
                v.nop(nofuse=True)
                eight = slice(0, 8) if s < 3 else slice(8, 16)
                for h in hs:
                    best, keys = v16[0:ROWS, h, eight], sim[0:ROWS, h, :]
                    if s in (0, 3):
                        last = nc.vector.max(best, keys)
                    elif s in (1, 4):
                        last = nc.vector.max_index(i16[0:ROWS, h, eight], best, keys)
                    else:
                        last = nc.vector.match_replace(keys, best, keys, REPLACED)
                last.then_inc(p_top, 1)

            def pick_stage(t, s, k):
                hs = range(4 * k, 4 * k + 4)
                if s == 0:
                    v.wait_ge(p_grid, 4 * t + 2 * k + 2 + FREE)
                    v.wait_ge(p_exp, 2 * t + FREE)
                else:
                    v.wait_ge(p_pick, picked(t, s - 1, k))
                if s == 1:
                    v.wait_ge(b_p, t + FREE)
                v.nop(nofuse=True)
                eight = slice(0, 8) if s < 2 else slice(8, 16)
                for h in hs:
                    best, pairs = z16[0:ROWS, h, eight], (grid if s < 2 else left)[0:ROWS, h, :]
                    if s in (0, 2):
                        last = nc.vector.max(best, pairs)
                    else:
                        last = nc.vector.match_replace(left[0:ROWS, h, :], best, pairs, REPLACED)
                last.then_inc(p_pick, 1)

            def chosen(t, k):
                hs = slice(4 * k, 4 * k + 4)
                v.wait_ge(p_pick, picked(t, 3, k))
                v.wait_ge(p_exp, 2 * t + k + 1 + FREE)
                nc.vector.scalar_tensor_tensor(left[0:ROWS, hs, :], left[0:ROWS, hs, :], TAKEN, grid[0:ROWS, hs, :],
                                               ALU.is_le, ALU.mult).then_inc(p_weight, 1)

            def inv_sums(t):
                v.wait_ge(p_exp, 2 * t + 2 + FREE)
                v.wait_ge(p_diag, t + FREE)
                nc.vector.reciprocal(rz[0:ROWS, :], zsum[0:ROWS, :]).then_inc(p_rz, 1)

            def peer_step(t):
                if there(t - 2):
                    for s_, k in PICK_ORDER:
                        pick_stage(t - 2, s_, k)
                for n, (s_, k) in enumerate(TOP_ORDER):
                    if there(t - 1):
                        top_stage(t - 1, s_, k)
                    if there(t) and n == 3:
                        mean_T2(t)
                    if there(t - 2) and n == 3:
                        chosen(t - 2, 0)
                        inv_sums(t - 2)
                    if there(t - 2) and n == 4:
                        chosen(t - 2, 1)
                    if there(t) and n == 6:
                        x1_piece(t, 0)
                    if there(t) and n == 7:
                        x1_piece(t, 1)
                        x1_piece(t, 2)
                    if there(t) and n == 8:
                        x1_piece(t, 3)

            all_steps(v, peer_step)
            v.wait_ge(x2_done, TILES + FREE)

            with v.Fori(0, TILES) as t:
                v.wait_ge(n_dense, t + 1)
                nc.vector.tensor_tensor(xs[0:ROWS, ds(t, 1), :], xs[0:ROWS, ds(t, 1), :], psOut.unsqueeze(1), ALU.add
                                        ).then_inc(x3_done, 1)
                v.wait_ge(x3_done, t + 1 + FREE)
                v.nop(nofuse=True)
                nc.vector.bn_stats(st[0:ROWS, 0, :], xs[0:ROWS, ds(t, 1), :]).then_inc(x4_dve, 1)
                v.wait_ge(x4_dve, 2 * t + 1)
                v.nop(nofuse=True)
                nc.vector.bn_aggr(mv[0:ROWS, 0, :], st[0:ROWS, 0, :]).then_inc(x4_dve, 1)
                v.wait_ge(x4_rstd, 2 * t + 2)
                v.wait_ge(x4_tr, t + FREE)
                nc.vector.tensor_scalar(row[0:ROWS, :].unsqueeze(1), xs[0:ROWS, ds(t, 1), :], mv[0:ROWS, 0, 0:1], rstd[0:ROWS, 0:1],
                                        ALU.subtract, ALU.mult).then_inc(x4_norm, 1)

            v.wait_ge(x4_tr, TILES + FREE)
            nc.vector.tensor_scalar(meanc[:, :], ps[:, 4, 0:FC], 1.0 / NODES, None, ALU.mult).then_inc(r_mean, 1)
            v.wait_ge(r_logit, 1)
            v.wait_ge(b1_in, 64)
            nc.vector.tensor_tensor(rt[0:1, 0:3], psE[0:1, 4:7], rb2[0:1, :], ALU.add).then_inc(r_dve, 1)
            v.wait_ge(r_dve, 1)
            nc.vector.tensor_reduce(rt[0:1, 4:5], rt[0:1, 0:3], X, ALU.max, negate=True).then_inc(r_dve, 1)
            v.wait_ge(r_exp, 1)
            nc.vector.reciprocal(rt[0:1, 13:14], rt[0:1, 12:13]).then_inc(r_dve, 1)
            v.wait_ge(r_dve, 3)
            nc.vector.tensor_scalar(rt[0:1, 16:19], rt[0:1, 8:11], rt[0:1, 13:14], None, ALU.mult).then_inc(r_dve, 1)
            v.wait_ge(r_dve, 4)
            nc.vector.tensor_reduce(rt[0:1, 20:21], rt[0:1, 16:19], X, ALU.max).then_inc(r_dve, 1)
            v.wait_ge(r_dve, 5)
            nc.vector.tensor_scalar(rt[0:1, 24:27], rt[0:1, 16:19], rt[0:1, 20:21], None, ALU.is_lt).then_inc(r_dve, 1)
            v.wait_ge(r_dve, 6)
            nc.vector.tensor_scalar(rt[0:1, 28:29], rt[0:1, 25:26], 1.0, None, ALU.add).then_inc(r_dve, 1)
            v.wait_ge(r_dve, 7)
            nc.vector.tensor_tensor(seli[0:1, 0:1], rt[0:1, 28:29], rt[0:1, 24:25], ALU.mult).then_inc(r_sel, 1)

            kl = key_l.rearrange("p (c e) n -> p e c n", e=2)
            kk = key_h.rearrange("p (c e) n -> p e c n", e=2)
            qq = query.rearrange("p (c e) n -> p e c n", e=2)
            with v.Fori(0, TILES) as t:
                at = ds(t * ROWS, ROWS)
                v.wait_ge(k_high, t + 1 + FREE)
                nc.vector.tensor_tensor(kl[0:64, 0, :, at], psQ[0:64, :, :], kk[0:64, 0, :, at], ALU.subtract)
                nc.vector.tensor_tensor(kl[64:128, 1, :, at], psQ[64:128, :, :], kk[64:128, 1, :, at], ALU.subtract
                                        ).then_inc(k_low, 1)
                v.wait_ge(q_high, t + 1 + FREE)
                nc.vector.scalar_tensor_tensor(cross[0:64, :, at], psTr[0:64, :, :], DHEAD ** -0.5,
                                               qq[0:64, 0, :, at], ALU.mult, ALU.subtract)
                nc.vector.scalar_tensor_tensor(qq[64:128, 1, :, at], psTr[64:128, :, :], DHEAD ** -0.5,
                                               cross[64:128, :, at], ALU.mult, ALU.subtract).then_inc(q_low, 1)

            def max_head(t, h):
                n = HEADS * t + h
                v.wait_ge(a_score, n + 1)
                if not first(t):
                    v.wait_ge(a_exp, 2 * (HEADS * (t - 1) + h + 1))
                nc.vector.tensor_reduce(nmax[0:ROWS, h:h + 1], psScore(h % 2), X, ALU.max, negate=True
                                        ).then_inc(a_max, 1)

            def dve_turn(t, h, n, kind):
                if taker(kind) != "dve":
                    return
                v.wait_ge(a_tr, made(t, h, n))
                bank = place(t, h, n) % 2
                if kind == "out":
                    v.wait_ge(out_free, t - 1 + FREE)
                    nc.vector.tensor_tensor(outs.unsqueeze(1), psTP[bank].unsqueeze(1), xs[0:ROWS, ds(t - 1, 1), :],
                                            ALU.add).then_inc(tr_dve, 1)
                    return
                if not (first(t) and h < 4):
                    v.wait_ge(a_pv, HEADS * t + h - 3)
                lo, hi = TB[kind]
                nc.vector.tensor_copy(probT[h % 2][:, lo:hi, :],
                                      psTP[bank][:, 0:(hi - lo) * ROWS].rearrange("p (t n) -> p t n", n=ROWS)
                                      ).then_inc(tr_dve, 1)

            def dve_step(t, h):
                kinds = turns(t, h)
                if not first(t) and h == 0:
                    max_head(t - 1, HEADS - 1)
                elif h >= 1 and not drain(t):
                    max_head(t, h - 1)
                for n, kind in enumerate(kinds):
                    dve_turn(t, h, n, kind)
                if not first(t) and h == 0:
                    v.wait_ge(a_exp, 2 * HEADS * t)
                    nc.vector.tensor_tensor(psums[0:ROWS, :], psum_p[0:ROWS, 0, :], psum_p[0:ROWS, 1, :], ALU.add
                                            ).then_inc(a_inv, 1)
                if not first(t) and h == 1:
                    v.wait_ge(a_inv, 2 * t - 1)
                    nc.vector.reciprocal(rinv[0:ROWS, :], psums[0:ROWS, :]).then_inc(a_inv, 1)
                if not first(t) and h == 2:
                    v.wait_ge(a_inv, 2 * t)
                    v.wait_ge(a_pv, HEADS * t)
                    nc.vector.tensor_tensor(attn.rearrange("p (h d) -> p h d", d=DHEAD),
                                            psPV.rearrange("p (h d) -> p h d", d=DHEAD),
                                            rinv[0:ROWS, :].unsqueeze(2).broadcast_to([ROWS, HEADS, DHEAD]),
                                            ALU.mult).then_inc(a_norm, 1)

            for h in range(HEADS):
                dve_step(0, h)
            with v.Fori(1, TILES) as t:
                for h in range(HEADS):
                    dve_step(t, h)
            for h in range(HEADS):
                dve_step(TILES, h)

        @block.tensor
        def _(pe):
            mm, tr = nc.tensor.matmul, nc.tensor.transpose
            idr = ident[0:ROWS, 0:ROWS]
            pe.wait_ge(consts_set, 5)
            pe.wait_ge(edge_dve, 5)
            idg = ident[0:GROUPS, 0:GROUPS]
            for j in range(PER):
                tr(psE[0:EROWS, GROUPS * j:GROUPS * (j + 1)], src_f[:, EROWS * j:EROWS * (j + 1)], idg)
            for j in range(PER):
                tr(psE[0:EROWS, GROUPS * (PER + j):GROUPS * (PER + j + 1)], rel_f[:, EROWS * j:EROWS * (j + 1)], idg)
            tr(psE[0:1, 2 * PER * GROUPS:(2 * PER + 1) * GROUPS], bm[:, 0:1], idg)
            tr(psE[0:1, (2 * PER + 1) * GROUPS:(2 * PER + 2) * GROUPS], bm[:, 1:2], idg).then_inc(edge_cols, 1)

            def count(b, ohs):
                for t in range(TILES):
                    for j in range(PER):
                        mm(psAdj[b][:, t, :], ohs[j][:, ROWS * t:ROWS * t + 128], oh_dst[:, b, j, :],
                           start=j == 0, stop=j == PER - 1)
                for j in range(PER):
                    last = mm(psAdj[b][:, TILES, :], ones_b[0:EROWS, :], oh_dst[:, b, j, :],
                              start=j == 0, stop=j == PER - 1)
                return last

            with pe.Fori(0, GROUPS // 2) as u:
                for b in range(2):
                    pe.wait_ge(adj_onehot, 2 * u + b + 1)
                    count(b, oh_src[b]).then_inc(adj_counted, 1)
            pe.wait_ge(adj_added, GROUPS + FREE)
            spread = pe.value_load(flagi[0:1, 0:1], min_val=0, max_val=1)
            with pe.If(spread == 1):
                mm(psE[0:EROWS, 0:GROUPS], ones_r[0:1, 0:EROWS], bmrow[:, 0:GROUPS], start=True, stop=True
                   ).then_inc(rem_counted, 1)
                with pe.Fori(0, GROUPS) as gi:
                    with pe.Fori(0, WINDOWS) as wi:
                        pe.wait_ge(rem_dve, 3 + gi * (3 * WINDOWS + 1) + 1 + 3 * wi + 1)
                        count(0, oh_src[0]).then_inc(rem_counted, 1)

            def rows_T(t, x, o, start, stop):
                for f in range(FC):
                    for i in range(2):
                        last = mm(o[:, f, :], x[0:ROWS, ds(t, 1), i, 128 * f:128 * f + 128].rearrange("p t n -> p (t n)"),
                                  ident_h[0:ROWS, 0:ROWS], start=start and i == 0, stop=stop and i == 1)
                return last

            def aggregate(t, x, nodes_too=False):
                def product(f, k, i, counts, start=False, stop=False):
                    return mm(psAgg[:, f, :], x[0:ROWS, k, i, 128 * f:128 * f + 128], counts(k)[0:ROWS, at],
                              start=start, stop=stop)

                terms = [(k, i) for k in range(TILES) for i in range(2)]
                at = ds(t * ROWS, ROWS)
                for f in range(FC):
                    if nodes_too:
                        for i in range(2):
                            mm(psAgg[:, f, :], x[0:ROWS, ds(t, 1), i, 128 * f:128 * f + 128].rearrange("p t n -> p (t n)"),
                               ident_h[0:ROWS, 0:ROWS], start=f == i == 0, stop=False)
                    for k, i in terms[:-1]:
                        product(f, k, i, adj_h, start=f == k == i == 0 and not nodes_too)
                with pe.If(large == 1):
                    for f in range(FC):
                        for k, i in terms:
                            product(f, k, i, adj_l)
                for f in range(FC):
                    last = product(f, *terms[-1], adj_h, stop=f == FC - 1)
                return last

            def transpose4(o, x):
                for f in range(FC):
                    last = tr(o[:, f, :], x[:, 128 * f:128 * f + 128], idr)
                return last

            def to_rows(o, lhs, w, start=True, stop=True):
                for f in range(FC):
                    last = mm(o, lhs[:, f, :], w[:, f, :], start=start and f == 0, stop=stop and f == FC - 1)
                return last

            def to_cols(o, w, rhs):
                for c in range(o.shape[1]):
                    for f in range(FC):
                        last = mm(o[:, c, :], w[:, f, 128 * c:128 * c + 128], rhs[:, f, :],
                                  start=f == 0, stop=f == FC - 1)
                return last

            def bias(o, i, stop):
                return mm(o, ones_r[32 * i:32 * i + 1, :], biases[32 * i:32 * i + 1, :], start=False, stop=stop)

            pe.wait_ge(adj_ready, 1)
            large = pe.value_load(flagi[0:1, 1:2], min_val=0, max_val=1)
            pe.wait_ge(ln1_done, TILES + FREE)
            pe.wait_ge(sage0_in, 32)
            pe.wait_ge(bias_in, 48)
            with pe.Fori(0, TILES) as t:
                pe.wait_ge(s0_trT, t + FREE)
                rows_T(t, xA, psTr, True, True).then_inc(s0_tr, 1)
                pe.wait_ge(s0_aggT, t + FREE)
                aggregate(t, xA).then_inc(s0_agg, 1)
                pe.wait_ge(s0_low, t + FREE)
                pe.wait_ge(s0_trT, t + 1 + FREE)
                to_rows(psOut, colB, wB, stop=False)
                pe.wait_ge(s0_aggT, t + 1 + FREE)
                to_rows(psOut, colA, wA, start=False, stop=False)
                bias(psOut, 0, True).then_inc(s0_dense, 1)

            pe.wait_ge(s0_low, TILES + FREE)
            pe.wait_ge(sage1_in, 32)

            def sage(t):
                pe.wait_ge(f_trT, t + FREE)
                rows_T(t, xB, psTr, True, True).then_inc(s1_tr, 1)
                pe.wait_ge(s1_aggT, t + FREE)
                aggregate(t, xB).then_inc(s1_agg, 1)
                pe.wait_ge(x1_norm, t + FREE)
                pe.wait_ge(s1_trT, t + 1)
                to_rows(psOut, colB, wD, stop=False)
                pe.wait_ge(s1_aggT, t + 1 + FREE)
                to_rows(psOut, colA, wC, start=False, stop=False)
                bias(psOut, 1, True).then_inc(s1_dense, 1)

            def front(t):
                pe.wait_ge(x1_norm, t + 1 + FREE)
                transpose4(psTr, row[0:ROWS, :]).then_inc(f_tr, 1)
                pe.wait_ge(f_trT, t + 1 + FREE)
                pe.wait_ge(f_qT, t + FREE)
                to_cols(psQ, wA, colB).then_inc(f_q, 1)

            def front_keys(t):
                pe.wait_ge(f_qT, t + 1 + FREE)
                for c in range(2):
                    pe.wait_ge(f_simS, 2 * t + c + FREE)
                    for n in range(2):
                        last = mm(psSim[:, n, :], colA[:, c, :], keyb[:, c, 512 * n:512 * n + 512],
                                  start=True, stop=True)
                    last.then_inc(f_sim, 1)
                pe.wait_ge(f_hidT, t + FREE)
                to_cols(psHid.rearrange("p (c n) -> p c n", n=ROWS), wdT, colA).then_inc(f_hid, 1)

            def back(t):
                pe.wait_ge(p_weight, 2 * t + 2 + FREE)
                pe.wait_ge(p_diag, t + 1 + FREE)
                pe.wait_ge(b_pS, t + FREE)
                pe.wait_ge(f_hidT, t + 1 + FREE)
                for e in range(2):
                    for h in range(HEADS):
                        last = mm(psP[:, ROWS * e:ROWS * (e + 1)], left[0:ROWS, h, 128 * e:128 * e + 128],
                                  diag[0:ROWS, h, :], start=h == 0, stop=h == HEADS - 1)
                last.then_inc(b_p, 1)

            def up(t):
                pe.wait_ge(b_coef, t + 1)
                pe.wait_ge(b_upS, t + FREE)
                for e in range(2):
                    last = mm(psUp, coef[:, ROWS * e:ROWS * (e + 1)], wu[:, e, :], start=e == 0, stop=e == 1)
                last.then_inc(b_up, 1)

            def peer_step(t):
                if isinstance(t, int) and t == 1:
                    pe.wait_ge(peer_in, 16 * (1 + HEADS))
                    pe.wait_ge(expert_in, 32)
                if there(t - 1):
                    front(t - 1)
                if there(t - 3):
                    up(t - 3)
                if there(t - 1):
                    front_keys(t - 1)
                if there(t):
                    sage(t)
                if there(t - 2):
                    back(t - 2)

            all_steps(pe, peer_step)

            psMean = ps[:, 4, 0:FC]
            pe.wait_ge(columns_set, 2)
            mm(psMean, ident[:, :], zero_c[:, 0:FC], start=True, stop=False)

            def gin(t):
                pe.wait_ge(n_aggT, t + FREE)
                aggregate(t, xA, nodes_too=True).then_inc(n_agg, 1)

            def gin_mlp(t):
                pe.wait_ge(n_aggT, t + 1 + FREE)
                to_cols(psQ, wC, colA).then_inc(n_u, 1)
                pe.wait_ge(n_uT, t + 1)
                pe.wait_ge(x3_done, t + FREE)
                to_rows(psOut, colB, wD, stop=False)
                bias(psOut, 2, True).then_inc(n_dense, 1)

            def x4_transposed(t):
                pe.wait_ge(x4_norm, t + 1)
                pe.wait_ge(x4_trT, t + FREE)
                last_tile = isinstance(t, int) and t == TILES - 1
                for f in range(FC):
                    mm(psMean[:, f:f + 1], row[0:ROWS, 128 * f:128 * f + 128], ones_c[0:ROWS, 0:1],
                       start=False, stop=f == FC - 1 and last_tile)
                transpose4(psTr, row[0:ROWS, :]).then_inc(x4_tr, 1)

            pe.wait_ge(ln3_done, TILES + FREE)
            pe.wait_ge(gin_in, 32)
            gin(0)
            gin_mlp(0)
            with pe.Fori(1, TILES) as t:
                gin(t)
                x4_transposed(t - 1)
                gin_mlp(t)
            x4_transposed(TILES - 1)

            pe.wait_ge(router_in, 16)
            pe.wait_ge(r_mean, 1)
            pe.wait_ge(b1_in, 64)
            for f in range(FC):
                last = mm(psE[:, 0:1], rw1[:, f, :], meanc[:, f:f + 1], start=f == 0, stop=f == FC - 1)
            last.then_inc(r_hid, 1)
            pe.wait_ge(r_hidS, 1)
            mm(psE[0:1, 4:7], hidr[:, :], rw2[:, :], start=True, stop=True).then_inc(r_logit, 1)

            def project(t):
                xt = x4T[:, :, ds(t * ROWS, ROWS)]
                if first(t):
                    pe.wait_ge(wk_in, 16 * FC)
                pe.wait_ge(k_low, t + FREE)
                to_cols(psQ, wA, xt).then_inc(k_k, 1)
                if first(t):
                    pe.wait_ge(wq_in, 16)
                pe.wait_ge(q_low, t + FREE)
                to_cols(psTr, wC, xt).then_inc(k_q, 1)
                if first(t):
                    pe.wait_ge(wv_in, 16 * FC)
                pe.wait_ge(k_cols, t + 1)
                pe.wait_ge(v_set, t + FREE)
                to_rows(psOut, colB, wB).then_inc(k_v, 1)

            project(0)
            with pe.Fori(1, TILES) as t:
                project(t)

            pe.wait_ge(crossed, 16 * 12)
            pe.wait_ge(wo_in, 16)
            pe.wait_ge(v_set, TILES + FREE)

            def score(t, h, c):
                if c == 0 and not (first(t) and h < 2):
                    pe.wait_ge(a_exp, 2 * (HEADS * t + h - 1))
                if c == 2 and not (first(t) and h < 1):
                    pe.wait_ge(a_exp, 2 * (HEADS * t + h - 1) + 1)
                lo, hi = SC[h % 2][c]
                o = psScore(h % 2)[:, lo:hi]
                q = query[:, h, ds(t * ROWS, ROWS)]
                mm(o, q, key_h[:, h, lo:hi], start=True, stop=False)
                last = mm(o, q, key_l[:, h, lo:hi], start=False, stop=True)
                if c == 2:
                    last.then_inc(a_score, 1)

            def pe_turn(t, h, n, kind):
                at = place(t, h, n)
                if not (first(t) and at < 2):
                    who = (["act", "dve"] + tile_takers(t))[at]
                    pe.wait_ge(tr_act if who == "act" else tr_dve, taken(t, who, at - 1))
                bank = at % 2
                if kind == "attnT":
                    pe.wait_ge(a_norm, t)
                    transpose4(cols(5 + bank), attn).then_inc(a_tr, 1)
                elif kind == "out":
                    pe.wait_ge(tr_act, taken(t, "act", place(t, 4, 0)))
                    to_rows(psTP[bank], colB, wD).then_inc(a_tr, 1)
                else:
                    if kind == 0:
                        pe.wait_ge(a_exp, 2 * (HEADS * t + h - 1))
                    lo, hi = TB[kind]
                    for k in range(lo, hi):
                        last = tr(psTP[bank][:, ROWS * (k - lo):ROWS * (k - lo + 1)],
                                  probs[h % 2][:, ROWS * k:ROWS * (k + 1)], idr)
                    last.then_inc(a_tr, 1)

            def prob_v(t, h, step_t, step_h):
                for who, freed in (("act", tr_act), ("dve", tr_dve)):
                    pe.wait_ge(freed, taken(step_t, who, place(step_t, step_h, 0)))
                if h == 0 and not first(t):
                    pe.wait_ge(a_norm, t)
                for k in range(TILES):
                    last = mm(psPV[:, DHEAD * h:DHEAD * (h + 1)], probT[h % 2][:, k, :],
                              vals[:, k, DHEAD * h:DHEAD * (h + 1)], start=k == 0, stop=k == TILES - 1)
                last.then_inc(a_pv, 1)

            def pe_step(t, h):
                kinds = turns(t, h)
                for c in range(max(3, len(kinds))):
                    if c < 3 and not drain(t):
                        score(t, h, c)
                    if c < len(kinds):
                        pe_turn(t, h, c, kinds[c])
                if h < 3 and not first(t):
                    prob_v(t - 1, h + 5, t, h)
                elif h >= 3 and not drain(t):
                    prob_v(t, h - 3, t, h)

            for h in range(HEADS):
                pe_step(0, h)
            with pe.Fori(1, TILES) as t:
                for h in range(HEADS):
                    pe_step(t, h)
            for h in range(HEADS):
                pe_step(TILES, h)


def kernel(x, src, dst, L0_gnn_Wl0, L0_gnn_bl0, L0_gnn_Wr0, L0_gnn_Wl1, L0_gnn_bl1, L0_gnn_Wr1, L0_ffn_w_q,
           L0_ffn_keys, L0_ffn_weight_down_embed, L0_ffn_weight_up_embed, L1_gnn_W1, L1_gnn_b1, L1_gnn_W2,
           L1_gnn_b2, L1_ffn_r_w1, L1_ffn_r_b1, L1_ffn_r_w2, L1_ffn_r_b2, L1_ffn_wq0, L1_ffn_wk0, L1_ffn_wv0,
           L1_ffn_wo0, L1_ffn_wq1, L1_ffn_wk1, L1_ffn_wv1, L1_ffn_wo1, L1_ffn_wq2, L1_ffn_wk2, L1_ffn_wv2,
           L1_ffn_wo2):
    import numpy as np
    import concourse.bacc as bacc
    from concourse.bass_utils import run_bass_kernel_spmd

    given = dict(x=x, src=src, dst=dst, Wl0T=np.asarray(L0_gnn_Wl0).T, bl0=L0_gnn_bl0, Wr0T=np.asarray(L0_gnn_Wr0).T,
                 Wl1T=np.asarray(L0_gnn_Wl1).T, bl1=L0_gnn_bl1, Wr1T=np.asarray(L0_gnn_Wr1).T, wq=L0_ffn_w_q,
                 keysT=np.asarray(L0_ffn_keys).transpose(2, 0, 3, 1), wdT=np.asarray(L0_ffn_weight_down_embed).T,
                 wu=L0_ffn_weight_up_embed, W1=L1_gnn_W1, b1c=np.asarray(L1_gnn_b1).reshape(FC, 128).T, W2=L1_gnn_W2, b2=L1_gnn_b2,
                 rw1=L1_ffn_r_w1, rb1=L1_ffn_r_b1, rw2=L1_ffn_r_w2, rb2=L1_ffn_r_b2,
                 wq0=L1_ffn_wq0, wk0=L1_ffn_wk0, wv0=L1_ffn_wv0, wo0=L1_ffn_wo0,
                 wq1=L1_ffn_wq1, wk1=L1_ffn_wk1, wv1=L1_ffn_wv1, wo1=L1_ffn_wo1,
                 wq2=L1_ffn_wq2, wk2=L1_ffn_wk2, wv2=L1_ffn_wv2, wo2=L1_ffn_wo2)
    nc = bacc.Bacc("TRN2", target_bir_lowering=False, num_devices=1)
    arrays, aps = {}, {}
    for name, value in given.items():
        v = np.ascontiguousarray(value)
        arrays[f"in_{name}"] = v
        aps[name] = nc.dram_tensor(f"in_{name}", v.shape, mybir.dt.from_np(v.dtype), kind="ExternalInput").ap()
    out = nc.dram_tensor("out_x", (NODES, D), FP32, kind="ExternalOutput").ap()
    build(nc, aps, out)
    r = run_bass_kernel_spmd(nc, [arrays], core_ids=[0])
    return r.results[0]["out_x"]
```
